# Optimizing a Trainium2 kernel written in Bass

```python
import numpy as np
import jax
import jax.numpy as jnp

def _softmax(x, axis=-1):
    return jax.nn.softmax(x, axis=axis)

def _gelu(x):
    return jax.nn.gelu(x, approximate=True)

def _silu(x):
    return jax.nn.silu(x)

def _sigmoid(x):
    return jax.nn.sigmoid(x)

def _layernorm(x, axis=-1, eps=1e-05):
    m = jnp.mean(x, axis=axis, keepdims=True)
    v = jnp.var(x, axis=axis, keepdims=True)
    return (x - m) / jnp.sqrt(v + eps)

def _scatter_add(tgt, idx, src, axis=0):
    return tgt.at[idx].add(src)

def _segment_sum(src, seg, n):
    return jax.ops.segment_sum(src, seg, n)
kernel_name = 'mk_decoder_preln_d2_seqx_r4_56949b'

def setup_inputs(seed: int=0):
    np.random.seed(seed)
    _w = jnp.asarray

    def _rec_inputs():
        import jax
        import jax.numpy as jnp
        _rk = jax.random.key(seed)
        x = -0.0002928 + 1 * jax.random.normal(jax.random.fold_in(_rk, 1), (64, 128, 256), jnp.float32)
        _lenS = 128 - jax.random.randint(jax.random.fold_in(_rk, 7), (64,), 0, max(1, 128 // 4) + 1, jnp.int32)
        _lenS2 = 128 - jax.random.randint(jax.random.fold_in(_rk, 8), (64,), 0, max(1, 128 // 4) + 1, jnp.int32)
        _ctx_1024P = jax.random.normal(jax.random.fold_in(_rk, 11), (64, 16, 256), jnp.float32)
        _ctx_1024c = jax.random.dirichlet(jax.random.fold_in(_rk, 511), 0.3 * jnp.ones((16,), jnp.float32), (64, 128))
        _ctx_1024t = jnp.einsum('bsk,bkd->bsd', _ctx_1024c, _ctx_1024P)
        _ctx_1024t = _ctx_1024t * jax.lax.rsqrt(jnp.mean(jnp.square(_ctx_1024t)) + 1e-12) * 0.953939
        ctx_1024 = -1.39393e-06 + 0.999914 * (_ctx_1024t + 0.3 * jax.random.normal(jax.random.fold_in(_rk, 611), (64, 128, 256), jnp.float32))
        _validS = jnp.arange(128)[None, :] < _lenS[:, None]
        _validS2 = jnp.arange(128)[None, :] < _lenS2[:, None]
        _causal = jnp.tril(jnp.ones((128, 128), dtype=bool))
        mask_BxS2_ik0 = jnp.where(jnp.broadcast_to(_validS2[:, :], (64, 128)), 0, 1).astype(jnp.int32)
        mask_BxS2_bk0 = jnp.logical_not(jnp.broadcast_to(_validS2[:, :], (64, 128)))
        return (x, ctx_1024, mask_BxS2_ik0, mask_BxS2_bk0)
    x, ctx_1024, mask_BxS2_ik0, mask_BxS2_bk0 = _rec_inputs()

    def _L0_attn_setup():
        import jax, jax.numpy as jnp
        import numpy as np
        D_MODEL = 256
        EXPAND = 2
        D_INNER = EXPAND * D_MODEL
        D_STATE = 128
        D_CONV = 4
        NHEADS = 32
        NGROUPS = 1
        HEADDIM = D_INNER // NHEADS
        D_PROJ = 2 * D_INNER + 2 * NGROUPS * D_STATE + NHEADS
        EPS = 1e-05

        def _rmsnorm(y, w):
            return y * jax.lax.rsqrt(jnp.mean(y * y, axis=-1, keepdims=True) + EPS) * w

        def _forward(x, in_proj_w, conv_w, conv_b, A_log, Dp, dt_bias, norm_w, out_proj_w):
            B, T, _ = x.shape
            hpg = NHEADS // NGROUPS
            proj = jnp.einsum('btd,pd->btp', x, in_proj_w)
            s1 = D_INNER
            s2 = 2 * D_INNER
            s3 = s2 + NGROUPS * D_STATE
            s4 = s3 + NGROUPS * D_STATE
            x_ssm, z, B_in, C_in, dt_in = jnp.split(proj, [s1, s2, s3, s4], axis=-1)
            xc = jax.lax.conv_general_dilated(x_ssm.transpose(0, 2, 1), conv_w, window_strides=(1,), padding=[(D_CONV - 1, 0)], dimension_numbers=('NCH', 'OIH', 'NCH'), feature_group_count=D_INNER)
            xc = xc + conv_b[None, :, None]
            x_ssm = jax.nn.silu(xc.transpose(0, 2, 1))
            x_heads = x_ssm.reshape(B, T, NHEADS, HEADDIM)
            B_g = B_in.reshape(B, T, NGROUPS, D_STATE)
            C_g = C_in.reshape(B, T, NGROUPS, D_STATE)
            B_h = jnp.repeat(B_g, hpg, axis=2)
            C_h = jnp.repeat(C_g, hpg, axis=2)
            dt = jax.nn.softplus(dt_in + dt_bias)
            A = -jnp.exp(A_log)
            A_bar = jnp.exp(A * dt)

            def step(h, inp):
                ab, dtt, bt, ct, xt = inp
                h = ab[..., None, None] * h + (dtt[..., None] * bt)[:, :, None, :] * xt[..., None]
                y = jnp.einsum('bhn,bhpn->bhp', ct, h)
                return (h, y)
            h0 = jnp.zeros((B, NHEADS, HEADDIM, D_STATE), dtype=x.dtype)
            xs = (A_bar.transpose(1, 0, 2), dt.transpose(1, 0, 2), B_h.transpose(1, 0, 2, 3), C_h.transpose(1, 0, 2, 3), x_heads.transpose(1, 0, 2, 3))
            _, y_t = jax.lax.scan(step, h0, xs)
            y = y_t.transpose(1, 0, 2, 3)
            y = y + Dp[None, None, :, None] * x_heads
            y = y.reshape(B, T, D_INNER)
            y = _rmsnorm(y, norm_w) * jax.nn.silu(z)
            return jnp.einsum('bti,di->btd', y, out_proj_w)
        key = jax.random.key(seed)
        ks = jax.random.split(key, 8)
        B, T = (2, 512)
        x = jax.random.normal(ks[0], (B, T, D_MODEL), dtype=jnp.float32)
        in_proj_w = jax.random.normal(ks[1], (D_PROJ, D_MODEL), dtype=jnp.float32) * D_MODEL ** (-0.5)
        conv_w = jax.random.normal(ks[2], (D_INNER, 1, D_CONV), dtype=jnp.float32) * 0.3
        conv_b = jax.random.normal(ks[3], (D_INNER,), dtype=jnp.float32) * 0.02
        A_log = jax.random.normal(ks[4], (NHEADS,), dtype=jnp.float32) * 0.1
        Dp = jnp.ones((NHEADS,), dtype=jnp.float32)
        dt_bias = jax.random.normal(ks[5], (NHEADS,), dtype=jnp.float32) * 0.1
        norm_w = jnp.ones((D_INNER,), dtype=jnp.float32)
        out_proj_w = jax.random.normal(ks[6], (D_MODEL, D_INNER), dtype=jnp.float32) * D_INNER ** (-0.5)
        return {'x': x, 'in_proj_w': in_proj_w, 'conv_w': conv_w, 'conv_b': conv_b, 'A_log': A_log, 'Dp': Dp, 'dt_bias': dt_bias, 'norm_w': norm_w, 'out_proj_w': out_proj_w}
    _L0_attn_all = _L0_attn_setup()
    _L0_attn_in = {k: v for k, v in _L0_attn_all.items() if k in ('in_proj_w', 'conv_w', 'conv_b', 'A_log', 'Dp', 'dt_bias', 'norm_w', 'out_proj_w')}
    del _L0_attn_all

    def _L0_xattn_setup():
        import jax, jax.numpy as jnp
        import numpy as np
        B, SQ, SKV, D, H = (2, 512, 512, 256, 16)
        W = D // H

        def _heads(x):
            b, s, _ = x.shape
            return x.reshape(b, s, H, W).transpose(0, 2, 1, 3)
        key = jax.random.key(seed)
        ks = jax.random.split(key, 10)
        s = 1.0 / np.sqrt(D)
        return {'x_q': jax.random.normal(ks[0], (B, SQ, D), jnp.float32), 'x_k': jax.random.normal(ks[1], (B, SKV, D), jnp.float32), 'x_v': jax.random.normal(ks[2], (B, SKV, D), jnp.float32), 'mask': jax.random.randint(ks[3], (B, SKV), 0, 2, jnp.int32), 'Wq': jax.random.normal(ks[4], (D, D), jnp.float32) * s, 'bq': jnp.zeros((D,), jnp.float32), 'Wk': jax.random.normal(ks[5], (D, D), jnp.float32) * s, 'bk': jnp.zeros((D,), jnp.float32), 'Wv': jax.random.normal(ks[6], (D, D), jnp.float32) * s, 'bv': jnp.zeros((D,), jnp.float32)}
    _L0_xattn_all = _L0_xattn_setup()
    _L0_xattn_in = {k: v for k, v in _L0_xattn_all.items() if k in ('Wq', 'bq', 'Wk', 'bk', 'Wv', 'bv')}
    del _L0_xattn_all

    def _L0_ffn_setup():
        import jax, jax.numpy as jnp
        import numpy as np
        B, S, D = (2, 512, 256)
        E, K, F = (16, 2, 128)
        FS = 256
        key = jax.random.key(seed)
        ks = jax.random.split(key, 8)

        def w(k, shape, fan_in):
            return jax.random.normal(k, shape, jnp.float32) / np.sqrt(fan_in).astype(np.float32)
        return {'x': jax.random.normal(ks[0], (B, S, D), jnp.float32), 'Wr': w(ks[1], (D, E), D), 'Wg': w(ks[2], (E, D, F), D), 'Wu': w(ks[3], (E, D, F), D), 'Wd': w(ks[4], (E, F, D), F), 'Sg': w(ks[5], (D, FS), D), 'Su': w(ks[6], (D, FS), D), 'Sd': w(ks[7], (FS, D), FS)}
    _L0_ffn_all = _L0_ffn_setup()
    _L0_ffn_in = {k: v for k, v in _L0_ffn_all.items() if k in ('Wr', 'Wg', 'Wu', 'Wd', 'Sg', 'Su', 'Sd')}
    del _L0_ffn_all

    def _L1_attn_setup():
        import jax, jax.numpy as jnp
        import numpy as np
        B, S, D = (4, 512, 256)
        H = 16
        HD = D // H
        key = jax.random.key(seed)
        k1, k2, k3 = jax.random.split(key, 3)
        x = jax.random.normal(k1, (B, S, D), dtype=jnp.float32)
        w_qkv = jax.random.normal(k2, (D, 3 * D), dtype=jnp.float32) * 0.02
        w_proj = jax.random.normal(k3, (D, D), dtype=jnp.float32) * 0.02
        return {'x': x, 'w_qkv': w_qkv, 'w_proj': w_proj}
    _L1_attn_all = _L1_attn_setup()
    _L1_attn_in = {k: v for k, v in _L1_attn_all.items() if k in ('w_qkv', 'w_proj')}
    del _L1_attn_all

    def _L1_xattn_setup():
        import jax, jax.numpy as jnp
        import numpy as np
        DIM, DIM_HEAD, HEADS, SCALE = (256, 64, 8, 8.0)
        INNER = DIM_HEAD * HEADS
        LN_EPS = 1e-05
        L2_EPS = 1e-12

        def layer_norm(x, w, b):
            mu = jnp.mean(x, axis=-1, keepdims=True)
            var = jnp.mean(jnp.square(x - mu), axis=-1, keepdims=True)
            return (x - mu) * jax.lax.rsqrt(var + LN_EPS) * w + b

        def l2norm(t):
            n = jnp.sqrt(jnp.sum(jnp.square(t), axis=-1, keepdims=True))
            return t / jnp.maximum(n, L2_EPS)
        key = jax.random.key(seed)
        ks = jax.random.split(key, 8)
        b, n, m = (8, 2048, 64)
        x = jax.random.normal(ks[0], (b, n, DIM), dtype=jnp.float32)
        latents = jax.random.normal(ks[1], (b, m, DIM), dtype=jnp.float32)
        mask = jax.random.randint(ks[2], (b, n), 0, 2) > 0
        Wq = jax.random.normal(ks[3], (DIM, INNER), dtype=jnp.float32) * DIM ** (-0.5)
        Wkv = jax.random.normal(ks[4], (DIM, 2 * INNER), dtype=jnp.float32) * DIM ** (-0.5)
        Wo = jax.random.normal(ks[5], (INNER, DIM), dtype=jnp.float32) * INNER ** (-0.5)
        return {'x': x, 'latents': latents, 'mask': mask, 'ln_x_w': jnp.ones((DIM,)), 'ln_x_b': jnp.zeros((DIM,)), 'ln_l_w': jnp.ones((DIM,)), 'ln_l_b': jnp.zeros((DIM,)), 'Wq': Wq, 'Wkv': Wkv, 'q_scale': jnp.ones((DIM_HEAD,)), 'k_scale': jnp.ones((DIM_HEAD,)), 'Wo': Wo, 'ln_o_w': jnp.ones((DIM,)), 'ln_o_b': jnp.zeros((DIM,))}
    _L1_xattn_all = _L1_xattn_setup()
    _L1_xattn_in = {k: v for k, v in _L1_xattn_all.items() if k in ('ln_x_w', 'ln_x_b', 'ln_l_w', 'ln_l_b', 'Wq', 'Wkv', 'q_scale', 'k_scale', 'Wo', 'ln_o_w', 'ln_o_b')}
    del _L1_xattn_all

    def _L1_ffn_setup():
        import jax, jax.numpy as jnp
        import numpy as np
        EPS = 1e-08
        key = jax.random.key(seed)
        kx, kw = jax.random.split(key)
        x = jax.random.normal(kx, (8, 1024, 256), dtype=jnp.float32)
        weight = jax.random.normal(kw, (256, 256), dtype=jnp.float32) * (1.0 / np.sqrt(256))
        return {'x': x, 'weight': weight}
    _L1_ffn_all = _L1_ffn_setup()
    _L1_ffn_in = {k: v for k, v in _L1_ffn_all.items() if k in ('weight',)}
    del _L1_ffn_all
    return {'x': x, 'ctx_1024': ctx_1024, 'mask_BxS2_ik0': mask_BxS2_ik0, 'mask_BxS2_bk0': mask_BxS2_bk0, 'L0_attn_in_proj_w': _L0_attn_in['in_proj_w'], 'L0_attn_conv_w': _L0_attn_in['conv_w'], 'L0_attn_conv_b': _L0_attn_in['conv_b'], 'L0_attn_A_log': _L0_attn_in['A_log'], 'L0_attn_Dp': _L0_attn_in['Dp'], 'L0_attn_dt_bias': _L0_attn_in['dt_bias'], 'L0_attn_norm_w': _L0_attn_in['norm_w'], 'L0_attn_out_proj_w': _L0_attn_in['out_proj_w'], 'L0_xattn_Wq': _L0_xattn_in['Wq'], 'L0_xattn_bq': _L0_xattn_in['bq'], 'L0_xattn_Wk': _L0_xattn_in['Wk'], 'L0_xattn_bk': _L0_xattn_in['bk'], 'L0_xattn_Wv': _L0_xattn_in['Wv'], 'L0_xattn_bv': _L0_xattn_in['bv'], 'L0_ffn_Wr': _L0_ffn_in['Wr'], 'L0_ffn_Wg': _L0_ffn_in['Wg'], 'L0_ffn_Wu': _L0_ffn_in['Wu'], 'L0_ffn_Wd': _L0_ffn_in['Wd'], 'L0_ffn_Sg': _L0_ffn_in['Sg'], 'L0_ffn_Su': _L0_ffn_in['Su'], 'L0_ffn_Sd': _L0_ffn_in['Sd'], 'L1_attn_w_qkv': _L1_attn_in['w_qkv'], 'L1_attn_w_proj': _L1_attn_in['w_proj'], 'L1_xattn_ln_x_w': _L1_xattn_in['ln_x_w'], 'L1_xattn_ln_x_b': _L1_xattn_in['ln_x_b'], 'L1_xattn_ln_l_w': _L1_xattn_in['ln_l_w'], 'L1_xattn_ln_l_b': _L1_xattn_in['ln_l_b'], 'L1_xattn_Wq': _L1_xattn_in['Wq'], 'L1_xattn_Wkv': _L1_xattn_in['Wkv'], 'L1_xattn_q_scale': _L1_xattn_in['q_scale'], 'L1_xattn_k_scale': _L1_xattn_in['k_scale'], 'L1_xattn_Wo': _L1_xattn_in['Wo'], 'L1_xattn_ln_o_w': _L1_xattn_in['ln_o_w'], 'L1_xattn_ln_o_b': _L1_xattn_in['ln_o_b'], 'L1_ffn_weight': _L1_ffn_in['weight']}

def reference(x, ctx_1024, mask_BxS2_ik0, mask_BxS2_bk0, L0_attn_in_proj_w, L0_attn_conv_w, L0_attn_conv_b, L0_attn_A_log, L0_attn_Dp, L0_attn_dt_bias, L0_attn_norm_w, L0_attn_out_proj_w, L0_xattn_Wq, L0_xattn_bq, L0_xattn_Wk, L0_xattn_bk, L0_xattn_Wv, L0_xattn_bv, L0_ffn_Wr, L0_ffn_Wg, L0_ffn_Wu, L0_ffn_Wd, L0_ffn_Sg, L0_ffn_Su, L0_ffn_Sd, L1_attn_w_qkv, L1_attn_w_proj, L1_xattn_ln_x_w, L1_xattn_ln_x_b, L1_xattn_ln_l_w, L1_xattn_ln_l_b, L1_xattn_Wq, L1_xattn_Wkv, L1_xattn_q_scale, L1_xattn_k_scale, L1_xattn_Wo, L1_xattn_ln_o_w, L1_xattn_ln_o_b, L1_ffn_weight):
    import jax
    import jax.numpy as jnp

    def _L0_attn_ref(x, in_proj_w, conv_w, conv_b, A_log, Dp, dt_bias, norm_w, out_proj_w):
        import jax, jax.numpy as jnp
        import numpy as np
        D_MODEL = 256
        EXPAND = 2
        D_INNER = EXPAND * D_MODEL
        D_STATE = 128
        D_CONV = 4
        NHEADS = 32
        NGROUPS = 1
        HEADDIM = D_INNER // NHEADS
        D_PROJ = 2 * D_INNER + 2 * NGROUPS * D_STATE + NHEADS
        EPS = 1e-05

        def _rmsnorm(y, w):
            return y * jax.lax.rsqrt(jnp.mean(y * y, axis=-1, keepdims=True) + EPS) * w

        def _forward(x, in_proj_w, conv_w, conv_b, A_log, Dp, dt_bias, norm_w, out_proj_w):
            B, T, _ = x.shape
            hpg = NHEADS // NGROUPS
            proj = jnp.einsum('btd,pd->btp', x, in_proj_w)
            s1 = D_INNER
            s2 = 2 * D_INNER
            s3 = s2 + NGROUPS * D_STATE
            s4 = s3 + NGROUPS * D_STATE
            x_ssm, z, B_in, C_in, dt_in = jnp.split(proj, [s1, s2, s3, s4], axis=-1)
            xc = jax.lax.conv_general_dilated(x_ssm.transpose(0, 2, 1), conv_w, window_strides=(1,), padding=[(D_CONV - 1, 0)], dimension_numbers=('NCH', 'OIH', 'NCH'), feature_group_count=D_INNER)
            xc = xc + conv_b[None, :, None]
            x_ssm = jax.nn.silu(xc.transpose(0, 2, 1))
            x_heads = x_ssm.reshape(B, T, NHEADS, HEADDIM)
            B_g = B_in.reshape(B, T, NGROUPS, D_STATE)
            C_g = C_in.reshape(B, T, NGROUPS, D_STATE)
            B_h = jnp.repeat(B_g, hpg, axis=2)
            C_h = jnp.repeat(C_g, hpg, axis=2)
            dt = jax.nn.softplus(dt_in + dt_bias)
            A = -jnp.exp(A_log)
            A_bar = jnp.exp(A * dt)

            def step(h, inp):
                ab, dtt, bt, ct, xt = inp
                h = ab[..., None, None] * h + (dtt[..., None] * bt)[:, :, None, :] * xt[..., None]
                y = jnp.einsum('bhn,bhpn->bhp', ct, h)
                return (h, y)
            h0 = jnp.zeros((B, NHEADS, HEADDIM, D_STATE), dtype=x.dtype)
            xs = (A_bar.transpose(1, 0, 2), dt.transpose(1, 0, 2), B_h.transpose(1, 0, 2, 3), C_h.transpose(1, 0, 2, 3), x_heads.transpose(1, 0, 2, 3))
            _, y_t = jax.lax.scan(step, h0, xs)
            y = y_t.transpose(1, 0, 2, 3)
            y = y + Dp[None, None, :, None] * x_heads
            y = y.reshape(B, T, D_INNER)
            y = _rmsnorm(y, norm_w) * jax.nn.silu(z)
            return jnp.einsum('bti,di->btd', y, out_proj_w)
        return _forward(x, in_proj_w, conv_w, conv_b, A_log, Dp, dt_bias, norm_w, out_proj_w)

    def _L0_xattn_ref(x_q, x_k, x_v, mask, Wq, bq, Wk, bk, Wv, bv):
        import jax, jax.numpy as jnp
        import numpy as np
        B, SQ, SKV, D, H = (2, 512, 512, 256, 16)
        W = D // H

        def _heads(x):
            b, s, _ = x.shape
            return x.reshape(b, s, H, W).transpose(0, 2, 1, 3)
        q = _heads(x_q @ Wq.T + bq)
        k = _heads(x_k @ Wk.T + bk)
        v = _heads(x_v @ Wv.T + bv)
        scores = jnp.einsum('bhqw,bhkw->bhqk', q, k) / np.sqrt(W).astype(np.float32)
        m = mask[:, None, None, :].astype(scores.dtype)
        scores = scores - 10000.0 * (1.0 - m)
        p = jax.nn.softmax(scores, axis=-1)
        h = jnp.einsum('bhqk,bhkw->bhqw', p, v)
        return h.transpose(0, 2, 1, 3).reshape(x_q.shape[0], x_q.shape[1], D)

    def _L0_ffn_ref(x, Wr, Wg, Wu, Wd, Sg, Su, Sd):
        import jax, jax.numpy as jnp
        import numpy as np
        B, S, D = (2, 512, 256)
        E, K, F = (16, 2, 128)
        FS = 256
        b, s, d = x.shape
        T = b * s
        xf = x.reshape(T, d)
        shared = jax.nn.silu(xf @ Sg) * (xf @ Su) @ Sd
        probs = jax.nn.softmax(xf @ Wr, axis=-1)
        topk_p, topk_i = jax.lax.top_k(probs, K)
        n_exp = Wr.shape[1]
        cw = jnp.zeros((T, n_exp), x.dtype).at[jnp.arange(T)[:, None], topk_i].add(topk_p)

        def step(acc, ew):
            wg, wu, wd, c = ew
            y = jax.nn.silu(xf @ wg) * (xf @ wu) @ wd
            return (acc + y * c[:, None], None)
        routed, _ = jax.lax.scan(step, jnp.zeros_like(xf), (Wg, Wu, Wd, cw.T))
        return (routed + shared).reshape(b, s, d)

    def _L1_attn_ref(x, w_qkv, w_proj):
        import jax, jax.numpy as jnp
        import numpy as np
        B, S, D = (4, 512, 256)
        H = 16
        HD = D // H
        b, s, d = x.shape
        qkv = x @ w_qkv
        q, k, v = jnp.split(qkv, 3, axis=2)
        q = q.reshape(b, s, H, HD).transpose(0, 2, 1, 3)
        k = k.reshape(b, s, H, HD).transpose(0, 2, 1, 3)
        v = v.reshape(b, s, H, HD).transpose(0, 2, 1, 3)
        att = jnp.einsum('bhqd,bhkd->bhqk', q, k) / jnp.sqrt(jnp.float32(HD))
        causal = jnp.tril(jnp.ones((s, s), dtype=bool))
        att = jnp.where(causal[None, None], att, jnp.float32(-jnp.inf))
        att = jax.nn.softmax(att, axis=-1)
        y = jnp.einsum('bhqk,bhkd->bhqd', att, v)
        y = y.transpose(0, 2, 1, 3).reshape(b, s, d)
        return y @ w_proj

    def _L1_xattn_ref(x, latents, mask, ln_x_w, ln_x_b, ln_l_w, ln_l_b, Wq, Wkv, q_scale, k_scale, Wo, ln_o_w, ln_o_b):
        import jax, jax.numpy as jnp
        import numpy as np
        DIM, DIM_HEAD, HEADS, SCALE = (256, 64, 8, 8.0)
        INNER = DIM_HEAD * HEADS
        LN_EPS = 1e-05
        L2_EPS = 1e-12

        def layer_norm(x, w, b):
            mu = jnp.mean(x, axis=-1, keepdims=True)
            var = jnp.mean(jnp.square(x - mu), axis=-1, keepdims=True)
            return (x - mu) * jax.lax.rsqrt(var + LN_EPS) * w + b

        def l2norm(t):
            n = jnp.sqrt(jnp.sum(jnp.square(t), axis=-1, keepdims=True))
            return t / jnp.maximum(n, L2_EPS)
        b, n, _ = x.shape
        m = latents.shape[1]
        x = layer_norm(x, ln_x_w, ln_x_b)
        latents = layer_norm(latents, ln_l_w, ln_l_b)
        q = latents @ Wq
        kv_input = jnp.concatenate([x, latents], axis=1)
        kv = kv_input @ Wkv
        k, v = jnp.split(kv, 2, axis=-1)

        def to_heads(t):
            return t.reshape(t.shape[0], t.shape[1], HEADS, DIM_HEAD).transpose(0, 2, 1, 3)
        q, k, v = map(to_heads, (q, k, v))
        q = l2norm(q) * q_scale
        k = l2norm(k) * k_scale
        sim = jnp.einsum('bhid,bhjd->bhij', q, k) * SCALE
        full_mask = jnp.concatenate([mask, jnp.ones((b, m), dtype=bool)], axis=1)[:, None, None, :]
        max_neg = -jnp.finfo(sim.dtype).max
        sim = jnp.where(full_mask, sim, max_neg)
        attn = jax.nn.softmax(sim.astype(jnp.float32), axis=-1).astype(sim.dtype)
        out = jnp.einsum('bhij,bhjd->bhid', attn, v)
        out = out.transpose(0, 2, 1, 3).reshape(b, m, INNER)
        return layer_norm(out @ Wo, ln_o_w, ln_o_b)

    def _L1_ffn_ref(x, weight):
        import jax, jax.numpy as jnp
        import numpy as np
        EPS = 1e-08
        w_scale = jnp.mean(jnp.abs(weight)) + EPS
        u = weight / w_scale
        w_quant = u + jax.lax.stop_gradient(jnp.clip(jnp.round(u), -1.0, 1.0) - u)
        a_scale = jnp.max(jnp.abs(x), axis=-1, keepdims=True) + EPS
        z = jnp.clip(x / a_scale * 127.0, -128.0, 127.0)
        a_quant = z + jax.lax.stop_gradient(jnp.round(z) - z)
        y = jnp.einsum('bsi,oi->bso', a_quant, w_quant)
        y = y * (w_scale * a_scale / 127.0)
        return y
    x = x + _L0_attn_ref(_layernorm(x, axis=-1), L0_attn_in_proj_w, L0_attn_conv_w, L0_attn_conv_b, L0_attn_A_log, L0_attn_Dp, L0_attn_dt_bias, L0_attn_norm_w, L0_attn_out_proj_w)
    x = x + _L0_xattn_ref(_layernorm(x, axis=-1), ctx_1024, ctx_1024, mask_BxS2_ik0, L0_xattn_Wq, L0_xattn_bq, L0_xattn_Wk, L0_xattn_bk, L0_xattn_Wv, L0_xattn_bv)
    x = x + _L0_ffn_ref(_layernorm(x, axis=-1), L0_ffn_Wr, L0_ffn_Wg, L0_ffn_Wu, L0_ffn_Wd, L0_ffn_Sg, L0_ffn_Su, L0_ffn_Sd)
    x = x + _L1_attn_ref(_layernorm(x, axis=-1), L1_attn_w_qkv, L1_attn_w_proj)
    x = x + _L1_xattn_ref(ctx_1024, _layernorm(x, axis=-1), mask_BxS2_bk0, L1_xattn_ln_x_w, L1_xattn_ln_x_b, L1_xattn_ln_l_w, L1_xattn_ln_l_b, L1_xattn_Wq, L1_xattn_Wkv, L1_xattn_q_scale, L1_xattn_k_scale, L1_xattn_Wo, L1_xattn_ln_o_w, L1_xattn_ln_o_b)
    x = x + _L1_ffn_ref(_layernorm(x, axis=-1), L1_ffn_weight)
    return x

_drawn_inputs = setup_inputs


def setup_inputs(seed=0):
    import zlib

    import numpy as np

    out = dict(_drawn_inputs(seed))
    spreads = {'L0_attn_Dp': (1.0, 0.6),
     'L0_attn_norm_w': (1.0, 0.2),
     'L0_xattn_bq': (0.0, 0.1),
     'L0_xattn_bk': (0.0, 0.8),
     'L0_xattn_bv': (0.0, 0.1),
     'L1_xattn_ln_x_w': (1.0, 0.2),
     'L1_xattn_ln_x_b': (0.0, 0.304),
     'L1_xattn_ln_l_w': (1.0, 0.2),
     'L1_xattn_ln_l_b': (0.0, 0.1),
     'L1_xattn_q_scale': (1.0, 0.2),
     'L1_xattn_k_scale': (1.0, 0.2),
     'L1_xattn_ln_o_w': (1.0, 0.2),
     'L1_xattn_ln_o_b': (0.0, 0.1)}
    factors = {'L0_attn_conv_b': 3.286}
    for name, (base, spread) in spreads.items():
        noise = np.random.default_rng([zlib.crc32(name.encode()), seed]).standard_normal(out[name].shape)
        drawn = base * np.exp(spread * noise) if base else spread * noise
        out[name] = jnp.asarray(drawn.astype(out[name].dtype))
    for name, factor in factors.items():
        out[name] = (out[name] * factor).astype(out[name].dtype)
    return out
```

```python
from contextlib import ExitStack

import numpy as np

import concourse.bass as bass
from concourse import mybir

F32 = mybir.dt.float32
BF16 = mybir.dt.bfloat16
I32 = mybir.dt.int32
U32 = mybir.dt.uint32
U8 = mybir.dt.uint8
ACT = mybir.ActivationFunctionType
ALU = mybir.AluOpType
AX = mybir.AxisListType

NB, T, D = 64, 128, 256
P = 128
DC = D // P
DI, NH, HP, NS, NCONV = 512, 32, 16, 128, 4
IC = DI // P
AH, AW = 16, 16
NG = AH // 4
NE, FF, FS = 16, 128, 256
NBLK = NE + FS // FF
XH, XW = 8, 64
LN_EPS, RMS_EPS, L2_CAP, Q_EPS = 1e-5, 1e-5, 1e12, 1e-8
MASK0 = 10000.0
NEG = -1e30
ROUND = 1.5 * 2.0 ** 23
CHAIN0, CHAIN1 = 41, 18
PCHAIN0, PCHAIN1 = 4, 11


def two_layers(nc, x_d, ctx_d, m0_d, m1_d, w_in, conv_w, conv_b, a_log, d_p, dt_bias, norm_w, w_out,
               wq0, bq0, wk0, bk0, wv0, bv0, w_r, w_g, w_u, w_d, s_g, s_u, s_d, w_qkv, w_proj,
               lnx_w, lnx_b, lnl_w, lnl_b, wq1, wkv1, q_sc, k_sc, wo1, lno_w, lno_b, w_tern, out_d):
    with ExitStack() as ctx:
        def sb(name, shape, dt=F32):
            return ctx.enter_context(nc.sbuf_tensor(name, shape, dt))

        PER = {}
        SEM = {}
        BASE = {"out_done": 16}

        def sig(name, per=1):
            SEM[name] = ctx.enter_context(nc.semaphore(name))
            PER[name] = per

        def at(name, b, k=1):
            return b * PER[name] + k + BASE.get(name, 0)

        Win = sb("Win", [P, DC, 2 * DI + 2 * NS + NH])
        Wout = sb("Wout", [P, IC, D])
        Wq0 = sb("Wq0", [P, DC, NG, P])
        Wk0 = sb("Wk0", [P, DC, NG, P])
        Wv0 = sb("Wv0", [P, DC, D])
        QB0 = sb("QB0", [2, NG, P])
        KB0 = sb("KB0", [2, NG, P])
        VB0 = sb("VB0", [2, D])
        Wr = sb("Wr", [P, DC, NE])
        Wg = sb("Wg", [P, DC, NBLK * FF])
        Wu = sb("Wu", [P, DC, NBLK * FF])
        Wd = sb("Wd", [P, NBLK, D])
        Wq1 = sb("Wq1", [P, DC, NG, P])
        Wk1 = sb("Wk1", [P, DC, NG, P])
        Wv1 = sb("Wv1", [P, DC, D])
        Wp1 = sb("Wp1", [P, DC, D])
        Wql = sb("Wql", [P, DC, XH * XW])
        Wkvl = sb("Wkvl", [P, DC, 2 * XH * XW])
        Wol = sb("Wol", [P, IC, D])
        Wtq = sb("Wtq", [P, DC, D], BF16)
        wscale = sb("wscale", [P, 4])
        convw = sb("convw", [P, IC, NCONV])
        convb = sb("convb", [P, IC])
        normw = sb("normw", [P, IC])
        Aneg = sb("Aneg", [P, NH])
        Dpb = sb("Dpb", [P, NH])
        dtb = sb("dtb", [P, NH])
        qks = sb("qks", [P, 2])
        lnx = sb("lnx", [P, 2, DC])
        lnl = sb("lnl", [P, 2, DC])
        lno = sb("lno", [P, 2, D])
        ident = sb("ident", [P, P])
        identb = sb("identb", [P, P], BF16)
        triu = sb("triu", [P, P])
        strict = sb("strict", [P, P])
        causal = sb("causal", [P, 4, P], BF16)
        ones = sb("ones", [P, P])
        onesb = sb("onesb", [1, P], BF16)
        iota = sb("iota", [P, NE])
        half_pow = sb("half_pow", [P, XH])
        x = sb("x", [P, D])
        ctx0 = sb("ctx0", [P, D])
        mask0i = sb("mask0i", [1, T], I32)
        mrow = sb("mrow", [2, T])
        big0 = sb("big0", [P, 6144])
        xn0 = sb("xn0", [P, D])
        xT0 = sb("xT0", [P, DC, T])
        st0 = sb("st0", [P, 6])
        mv0 = sb("mv0", [P, 4])
        xpad = sb("xpad", [P, IC, T + NCONV - 1])
        xc = sb("xc", [P, IC, T])
        th0 = sb("th0", [P, DI])
        xs2 = sb("xs2", [P, IC, T])
        bcT = sb("bcT", [P, 2, T])
        cbm = sb("cbm", [P, T])
        dts = sb("dts", [P, 8, NH])
        xdt = sb("xdt", [P, DI])
        ss0 = sb("ss0", [P, 4])
        tz = sb("tz", [P, DI])
        gz = sb("gz", [P, DI])
        x1 = sb("x1", [P, D])
        V0 = sb("V0", [P, AH, AW + 1])
        mx0 = sb("mx0", [P, AH])
        rc0 = sb("rc0", [P, AH])
        rt = sb("rt", [P, 10, NE])
        rti = sb("rti", [P, 2, 8], U32)
        cw = sb("cw", [P, NBLK])
        handoff = sb("handoff", [P, D])
        ctx1 = sb("ctx1", [P, D])
        mask1i = sb("mask1i", [1, T // 4], I32)
        mrow1 = sb("mrow1", [1, 2, 2 * T], BF16)
        big1 = sb("big1", [P, 4096])
        xn1 = sb("xn1", [P, D])
        xT1 = sb("xT1", [P, DC, T])
        st1 = sb("st1", [P, 6])
        mv1 = sb("mv1", [P, 4])
        V1 = sb("V1", [P, AH, AW + 1])
        mx1 = sb("mx1", [P, AH])
        rc1 = sb("rc1", [P, AH])
        x4 = sb("x4", [P, D])
        cT = sb("cT", [P, DC, T])
        l5 = sb("l5", [P, D])
        l2 = sb("l2", [P, 3, XH])
        qlT = sb("qlT", [P, 4, T])
        klT = sb("klT", [P, 4, 2 * T])
        Vl = sb("Vl", [P, 2, DI])
        mxl = sb("mxl", [P, XH])
        den = sb("den", [P, XH])
        x5 = sb("x5", [P, D])
        am = sb("am", [P, 4])
        aq = sb("aq", [P, D], BF16)
        aqT = sb("aqT", [P, DC, T], BF16)
        x6 = sb("x6", [P, D])

        A = [ctx.enter_context(nc.psum_tensor(f"A{i}", [P, 512], F32)) for i in range(4)]
        B = [ctx.enter_context(nc.psum_tensor(f"B{i}", [P, 512], F32)) for i in range(4)]

        def cut(t, at, c):
            return t[:, at:at + c * P].rearrange("p (c t) -> p c t", c=c)

        Wt = cut(big0, 0, 2 * DC).rearrange("p (c h) t -> p c (h t)", c=DC)
        y2 = xc[:, :, :].rearrange("p c t -> p (c t)")
        sq0 = xs2[:, :, :].rearrange("p c t -> p (c t)")
        xD, yT, ctxT, o0, x2 = th0, cut(xdt, 0, IC), cut(gz, 0, DC), xn0, x1
        QT0, KT0 = cut(big0, 4096, NG), cut(big0, 4608, NG)
        thf, hg, hh, hT = (big0[:, 512 * k:512 * k + 512] for k in range(4))
        QT1, KT1 = qlT, klT[:, :, :].rearrange("p c t -> p (c t)")[:, 0:512].rearrange("p (g t) -> p g t", g=NG)
        sq1, qn, ol = big1[:, 0:512], big1[:, 512:1024], big1[:, 0:512]
        kn = big1[:, 1024:2048].rearrange("p (c n) -> p c n", c=2)
        olT, o1, oT1, lT, fo, xf = cut(big1, 512, IC), xn1, xT1, xT1, l5, l5

        R = big0[:, 0:4096].rearrange("p (h t) -> p h t", t=T)
        Ed = [big0[:, 4096 + 512 * i:4608 + 512 * i].rearrange("p (h t) -> p h t", t=T) for i in range(2)]
        Mh = [big0[:, 5120 + 512 * i:5632 + 512 * i].rearrange("p (h t) -> p h t", t=T) for i in range(2)]
        S0 = big0[:, 0:2048].rearrange("p (j g k) -> p j g k", j=4, g=NG)
        PT0 = big0[:, 2048:4096].rearrange("p (j g q) -> p j g q", j=4, g=NG)
        S1 = big1[:, 0:2048].rearrange("p (j g k) -> p j g k", j=4, g=NG)
        PT1 = big1[:, 2048:4096].rearrange("p (j g q) -> p j g q", j=4, g=NG)

        for n, per in (("x_in", 16), ("ctx0_in", 16), ("mask0_in", 16), ("ctx1_in", 16), ("mask1_in", 16), ("out_done", 16)):
            sig(n, per)
        LNS = ("ln1", "ln2", "ln3", "ln4", "lnc", "ln5", "ln6", "lno", "ln7")
        for n in LNS:
            for what in ("var", "rstd", "xn") + ("Tps", "T") * (n not in ("ln5", "lno", "ln7")):
                sig(f"{n}_{what}")
        for n, per in (("dtBC", 1), ("xs", 1), ("z", 1), ("bcT", 1), ("xpad", 1), ("tz", 1), ("dt_abs", 1), ("dt_pre", 1),
                       ("dt_exp", 1), ("a", 1), ("R", 4), ("conv", 1), ("conv_th", 1), ("xs2", 1), ("CB", 1),
                       ("cbm", 1), ("xsT", 1), ("xdt", 1), ("arg", 8), ("E", 8), ("M", 8), ("Yk", 8), ("y2", 1), ("ss", 1),
                       ("rms", 1), ("yg", 1), ("yTps", 1), ("yT", 1), ("mamba", 1), ("x1", 1),
                       ("ctxTps", 1), ("ctxT", 1), ("mrow", 1), ("qk0", 3), ("qk0c", 3), ("S0", 4), ("S0sub", 4), ("P0", 4),
                       ("PT0ps", 4), ("PT0", 4), ("PV0", 1), ("x2", 1),
                       ("rout", 1), ("rmax", 1), ("rexp", 1), ("cw", 1), ("gate", 5), ("up", 5), ("gth", 5), ("hh", 5),
                       ("hTps", 5), ("hT", 5), ("down", 1), ("x3", 1)):
            sig(n, per)
        for n, per in (("qk1", 3), ("qk1c", 3), ("S1", 4), ("S1sub", 4), ("P1", 4), ("PT1ps", 4), ("PT1", 4), ("PV1", 1),
                       ("o1", 1), ("oT1ps", 1), ("oT1", 1), ("proj1", 1), ("x4", 1), ("mrow1", 1),
                       ("lat", 5), ("latsq", 3), ("latss", 3), ("latr", 3), ("latn", 3), ("Vl", 2), ("qlTps", 3), ("qlT", 3),
                       ("Sl", 4), ("mxl", 1), ("Pl", 4), ("PTlps", 4), ("PTl", 4), ("PVl", 1), ("ol", 1), ("olTps", 1),
                       ("olT", 1), ("wo", 1), ("x5", 1), ("aq", 1), ("aqTps", 1), ("aqT", 1), ("tern", 1), ("x6", 1)):
            sig(n, per)
        sig("dve0", CHAIN0)
        sig("dve1", CHAIN1)
        sig("pool0", PCHAIN0)
        sig("pool1", PCHAIN1)
        for n in ("passed_SP", "passed_DVE", "passed_Pool"):
            sig(n)
        for n in ("w_in", "pads", "consts", "dve_setup", "act_setup", "pe_setup", "pool_setup"):
            sig(n, 0)
        steps = {"dve0": 0, "dve1": 0, "pool0": 0, "pool1": 0}

        def link(eng, name, b, ins, bare=False):
            steps[name] += 1
            ins.then_inc(SEM[name], 1)
            eng.wait_ge(SEM[name], at(name, b, steps[name]))
            if bare:
                eng.sem_inc(SEM[f"passed_{eng.engine.name}"], 1)

        def program(eng, stages0, stages1):
            def chain(stages, b):
                for s in stages:
                    if s:
                        s(b)

            def both(i):
                for s0, s1 in zip(stages0, stages1):
                    if s0:
                        s0(i + 1)
                    if s1:
                        s1(i)

            def reset():
                for n in ("dve0", "dve1", "pool0", "pool1"):
                    assert steps[n] in (0, PER[n]), (n, steps[n])
                    steps[n] = 0

            reset()
            chain(stages0, 0)
            reset()
            with eng.Fori(0, NB - 1) as i:
                both(i)
            reset()
            chain(stages1, NB - 1)
            reset()

        SLOTS = (("ln1", "ln4"), ("dt", None), ("conv", "attn"), ("ssd", "lnc"), ("y", "ln5"), ("ln2", "ln6"), ("attn", "l2"),
                 ("ln3", "lmax"), ("route", "lno"), ("experts", "ln7"))

        def slots(s0, s1):
            return [s0.get(a) for a, _ in SLOTS], [s1.get(c) for _, c in SLOTS]

        Pl = big1[:, 0:2048].rearrange("p (k n) -> p k n", k=4)
        PTl = big1[:, 2048:4096].rearrange("p (k n) -> p k n", k=4)
        BANKS_DONE = (0, 2, 1, 3)

        def head_at(k, i):
            return 2 * (2 * (k % 2) + i) + k // 2

        loads = []
        block = ctx.enter_context(nc.Block())

        @block.sync
        def _(sp):
            n_w = 0

            def load(dst, src, slow=False):
                nonlocal n_w
                sp.dma_start(dst, src, allow_slow_non_contiguous=slow).then_inc(SEM["w_in"], 16)
                n_w += 16

            def chunks(dst, src):
                load(dst[:, :, :], src.rearrange("(c p) n -> p c n", p=P))

            chunks(Win, w_in)
            chunks(Wout, w_out)
            chunks(Wv0, wv0)
            chunks(Wr, w_r)
            for c in range(DC):
                rows = slice(c * P, (c + 1) * P)
                load(Wg[:, c, 0:NE * FF].rearrange("p (e f) -> p e f", f=FF), w_g[:, rows, :].rearrange("e p f -> p e f"))
                load(Wu[:, c, 0:NE * FF].rearrange("p (e f) -> p e f", f=FF), w_u[:, rows, :].rearrange("e p f -> p e f"))
                load(Wg[:, c, NE * FF:NBLK * FF], s_g[rows, :])
                load(Wu[:, c, NE * FF:NBLK * FF], s_u[rows, :])
            load(Wd[:, 0:NE, :], w_d.rearrange("e p d -> p e d"))
            load(Wd[:, NE:NBLK, :], s_d.rearrange("(c p) d -> p c d", p=P))
            load(Wv1[:, :, :], w_qkv[:, 2 * D:3 * D].rearrange("(c p) n -> p c n", p=P))
            chunks(Wp1, w_proj)
            chunks(Wql, wq1)
            chunks(Wkvl, wkv1)
            chunks(Wol, wo1)
            chunks(Wt, w_tern)
            load(convw[:, :, :], conv_w.rearrange("(c p) o k -> p c (o k)", p=P))
            for dst, src, c in ((convb, conv_b, IC), (normw, norm_w, IC)):
                load(dst[:, :], src.rearrange("(c p) -> p c", p=P), slow=True)
            for dst, src in ((Aneg, a_log), (Dpb, d_p), (dtb, dt_bias)):
                load(dst[:, :], src.partition_broadcast(P))
            for r in range(2):
                load(qks[64 * r:64 * r + 64, 0:1], q_sc.rearrange("(p a) -> p a", a=1))
                load(qks[64 * r:64 * r + 64, 1:2], k_sc.rearrange("(p a) -> p a", a=1))
            for dst, w, b_ in ((lnx, lnx_w, lnx_b), (lnl, lnl_w, lnl_b)):
                load(dst[:, 0, :], w.rearrange("(c p) -> p c", p=P), slow=True)
                load(dst[:, 1, :], b_.rearrange("(c p) -> p c", p=P), slow=True)
            load(lno[:, 0, :], lno_w.partition_broadcast(P))
            load(lno[:, 1, :], lno_b.partition_broadcast(P))
            sp.wait_ge(SEM["pads"], 1)
            for c in range(DC):
                rows = slice(c * P, (c + 1) * P)
                for dst, src in ((Wq0, wq0[rows, :]), (Wk0, wk0[rows, :]), (Wq1, w_qkv[rows, 0:D]), (Wk1, w_qkv[rows, D:2 * D])):
                    load(dst[:, c, :, :].rearrange("p g (j w) -> p (g j) w", w=32)[:, :, 1:1 + AW],
                         src.rearrange("p (h w) -> p h w", w=AW))
            for dst, src in ((QB0, bq0), (KB0, bk0)):
                load(dst[1:2, :, :].rearrange("p g (j w) -> p (g j) w", w=32)[:, :, 1:1 + AW],
                     src.rearrange("(a h w) -> a h w", a=1, w=AW))
            load(VB0[1:2, :], bv0.rearrange("(a n) -> a n", a=1))
            sp.wait_ge(SEM["w_in"], n_w)
            loads.append(n_w)

            def in0(b, first=False):
                if not first:
                    sp.wait_ge(SEM["x1"], at("x1", b, 0))
                sp.dma_start(x[:, :], x_d[bass.ds(b, 1)].rearrange("a p d -> (a p) d")).then_inc(SEM["x_in"], 16)
                if not first:
                    sp.wait_ge(SEM["ctxTps"], at("ctxTps", b, 0))
                sp.dma_start(ctx0[:, :], ctx_d[bass.ds(b, 1)].rearrange("a p d -> (a p) d")).then_inc(SEM["ctx0_in"], 16)
                if not first:
                    sp.wait_ge(SEM["mrow"], at("mrow", b, 0))
                sp.dma_start(mask0i[:, :], m0_d[bass.ds(b, 1), :]).then_inc(SEM["mask0_in"], 16)

            def in1(b, first=False):
                if not first:
                    sp.wait_ge(SEM["lnc_xn"], at("lnc_xn", b, 0))
                sp.dma_start(ctx1[:, :], ctx_d[bass.ds(b, 1)].rearrange("a p d -> (a p) d")).then_inc(SEM["ctx1_in"], 16)
                if not first:
                    sp.wait_ge(SEM["mrow1"], at("mrow1", b, 0))
                    sp.sem_inc(SEM["passed_SP"], 1)
                sp.dma_start(mask1i[:, :], m1_d[bass.ds(b, 1), :]).then_inc(SEM["mask1_in"], 16)

            def out1(b):
                sp.wait_ge(SEM["x6"], at("x6", b))
                sp.dma_start(out_d[bass.ds(b, 1)].rearrange("a p d -> (a p) d"), x6[:, :]).then_inc(SEM["out_done"], 16)

            in0(0, first=True)
            in1(0, first=True)
            in0(1)
            with sp.Fori(0, NB - 2) as i:
                in0(i + 2)
                in1(i + 1)
                out1(i)
            in1(NB - 1)
            out1(NB - 2)
            out1(NB - 1)
            sp.wait_ge(SEM["out_done"], at("out_done", NB, 0))

        @block.gpsimd
        def _(pool):
            g = nc.gpsimd
            for t in (Wq0, Wk0, Wq1, Wk1, QB0, KB0, VB0):
                g.memset(t[:], 0.0)
            g.memset(V0[:], 1.0)
            g.memset(V1[:], 1.0)
            g.memset(mrow[:], 1.0)
            g.memset(mrow1[:], 0.0)
            g.memset(xpad[:], 0.0)
            g.memset(half_pow[:], -0.5)
            g.memset(cw[:], 0.5)
            g.memset(onesb[:], 1.0)
            g.memset(causal[:], 0.0)
            g.memset(ident[:], 0.0)
            g.memset(identb[:], 0.0)
            g.memset(triu[:], 1.0)
            g.memset(strict[:], 1.0)
            g.memset(ones[:], 1.0).then_inc(SEM["pads"], 1)
            pool.wait_ge(SEM["pads"], 1)
            g.affine_select(out=ident[:, :], in_=ident[:, :], compare_op=ALU.not_equal, fill=1.0, base=0,
                            pattern=[[-1, P]], channel_multiplier=1)
            g.affine_select(out=identb[:, :], in_=identb[:, :], compare_op=ALU.not_equal, fill=1.0, base=0,
                            pattern=[[-1, P]], channel_multiplier=1)
            g.affine_select(out=triu[:, :], in_=triu[:, :], compare_op=ALU.is_ge, fill=0.0, base=0,
                            pattern=[[1, P]], channel_multiplier=-1)
            g.affine_select(out=strict[:, :], in_=strict[:, :], compare_op=ALU.is_gt, fill=0.0, base=0,
                            pattern=[[-1, P]], channel_multiplier=1)
            g.affine_select(out=causal[:, :, :], in_=causal[:, :, :], compare_op=ALU.is_ge, fill=NEG, base=0,
                            pattern=[[0, 4], [-1, P]], channel_multiplier=1)
            for t, row in ((QB0, 1), (KB0, 0)):
                v = t[:, :, :].rearrange("p g (j w) -> p (g j) w", w=32)[:, :, 0:1]
                g.memset(v, 1.0)
            g.iota(iota[:, :], pattern=[[1, NE]], base=0, channel_multiplier=0,
                   allow_small_or_imprecise_dtypes=True).then_inc(SEM["consts"], 1)
            pool.wait_ge(SEM["consts"], 1)
            pool.wait_ge(SEM["w_in"], loads[0])
            for t, row in ((QB0, 1), (KB0, 0)):
                v = t[:, :, :].rearrange("p g (j w) -> p (g j) w", w=32)[:, :, 0:1]
                last = g.affine_select(out=v, in_=v, compare_op=ALU.is_equal, fill=0.0, base=-row,
                                       pattern=[[0, AH], [0, 1]], channel_multiplier=1)
            last.then_inc(SEM["pool_setup"], 1)

            def rstd(n, mv, b, c):
                pool.wait_ge(SEM[f"{n}_var"], at(f"{n}_var", b))
                pool.sem_inc(SEM["passed_Pool"], 1)
                link(pool, c, b, g.tensor_scalar(mv[:, 2:3], mv[:, 1:2], LN_EPS, None, ALU.add))
                g.tensor_tensor(mv[:, 3:4], mv[:, 2:3], half_pow[:, 0:1], ALU.pow).then_inc(SEM[f"{n}_rstd"], 1)

            def ssd_steps(b):
                pool.wait_ge(SEM["a"], at("a", b))
                for k in range(4):
                    h = slice(8 * k, 8 * k + 8)
                    g.tensor_tensor(R[:, h, :], triu[:, :].unsqueeze(1).broadcast_to([P, 8, T]),
                                    dts[:, 7, h].unsqueeze(2).broadcast_to([P, 8, T]), ALU.mult).then_inc(SEM["R"], 1)

            def rms(b):
                pool.wait_ge(SEM["ss"], at("ss", b))
                pool.sem_inc(SEM["passed_Pool"], 1)
                link(pool, "pool0", b, g.tensor_scalar(ss0[:, 1:2], ss0[:, 0:1], 4.0 / DI, 16.0 * RMS_EPS, ALU.mult, ALU.add))
                g.tensor_tensor(ss0[:, 2:3], ss0[:, 1:2], half_pow[:, 0:1], ALU.pow).then_inc(SEM["rms"], 1)

            def l2norms(b):
                for k in range(3):
                    pool.wait_ge(SEM["latss"], at("latss", b, k + 1))
                    link(pool, "pool1", b, g.tensor_tensor(l2[:, k, :], l2[:, k, :], half_pow[:, :], ALU.pow), bare=True)
                    g.tensor_scalar(l2[:, k, :], l2[:, k, :], L2_CAP, None, ALU.min).then_inc(SEM["latr"], 1)

            def fin(b):
                pool.wait_ge(SEM["lno_xn"], at("lno_xn", b))
                link(pool, "pool1", b, g.tensor_tensor(fo[:, :], fo[:, :], lno[:, 0, :], ALU.mult))
                link(pool, "pool1", b, g.tensor_tensor(fo[:, :], fo[:, :], lno[:, 1, :], ALU.add))
                g.tensor_tensor(x5[:, :], fo[:, :], x4[:, :], ALU.add).then_inc(SEM["x5"], 1)

            r = rstd
            s0 = {"ln1": lambda b: r("ln1", mv0, b, "pool0"), "ssd": ssd_steps, "y": rms,
                  "ln2": lambda b: r("ln2", mv0, b, "pool0"), "ln3": lambda b: r("ln3", mv0, b, "pool0")}
            s1 = {"ln4": lambda b: r("ln4", mv1, b, "pool1"), "lnc": lambda b: r("lnc", mv1, b, "pool1"),
                  "ln5": lambda b: r("ln5", mv1, b, "pool1"), "ln6": lambda b: r("ln6", mv1, b, "pool1"),
                  "l2": l2norms,
                  "lno": lambda b: (r("lno", mv1, b, "pool1"), fin(b)), "ln7": lambda b: r("ln7", mv1, b, "pool1")}
            program(pool, *slots(s0, s1))

        @block.vector
        def _(dve):
            v = nc.vector
            dve.wait_ge(SEM["w_in"], loads[0])
            dve.wait_ge(SEM["consts"], 1)
            v.memset(x6[:], 0.0).then_inc(SEM["out_done"], 16)
            for c in range(IC):
                v.tensor_scalar(Wout[:, c, :], Wout[:, c, :], normw[:, c:c + 1], None, ALU.mult)
            dve.wait_ge(SEM["act_setup"], 1)
            v.tensor_scalar(Aneg[:, :], Aneg[:, :], -1.0, None, ALU.mult)
            v.tensor_scalar(qks[:, 0:1], qks[:, 0:1], qks[:, 1:2], None, ALU.mult)
            v.tensor_reduce(wscale[:, 0:1], Wt[:, :, :], AX.XY, ALU.add, apply_absolute_value=True).then_inc(SEM["dve_setup"], 1)
            dve.wait_ge(SEM["pe_setup"], 1)
            v.tensor_scalar(wscale[:, 1:2], A[0][:, 0:1], 1.0 / (D * D), Q_EPS, ALU.mult, ALU.add).then_inc(SEM["dve_setup"], 1)
            dve.wait_ge(SEM["dve_setup"], 2)
            v.reciprocal(wscale[:, 2:3], wscale[:, 1:2]).then_inc(SEM["dve_setup"], 1)
            dve.wait_ge(SEM["dve_setup"], 3)
            v.tensor_scalar(Wt[:, :, :], Wt[:, :, :], wscale[:, 2:3], None, ALU.mult).then_inc(SEM["dve_setup"], 1)
            dve.wait_ge(SEM["dve_setup"], 4)
            v.tensor_scalar(Wt[:, :, :], Wt[:, :, :], ROUND, ROUND, ALU.add, ALU.subtract).then_inc(SEM["dve_setup"], 1)
            dve.wait_ge(SEM["dve_setup"], 5)
            v.tensor_scalar(Wtq[:, :, :], Wt[:, :, :], 1.0, -1.0, ALU.min, ALU.max)
            v.tensor_scalar(wscale[:, 3:4], wscale[:, 1:2], 1.0 / 127.0, None, ALU.mult).then_inc(SEM["dve_setup"], 1)
            dve.wait_ge(SEM["dve_setup"], 6)
            dve.wait_ge(SEM["pool_setup"], 1)

            def norm(n, src, dst, st, mv, c, b):
                link(dve, c, b, v.bn_stats(st[:, :], src), bare=True)
                v.bn_aggr(mv[:, 0:2], st[:, :]).then_inc(SEM[f"{n}_var"], 1)
                dve.wait_ge(SEM[f"{n}_rstd"], at(f"{n}_rstd", b))
                v.tensor_scalar(dst[:, :], src, mv[:, 0:1], mv[:, 3:4], ALU.subtract, ALU.mult).then_inc(SEM[f"{n}_xn"], 1)

            def ln1(b):
                dve.wait_ge(SEM["x_in"], at("x_in", b, 16))
                norm("ln1", x[:, :], xn0, st0, mv0, "dve0", b)

            def dt(b):
                dve.wait_ge(SEM["dtBC"], at("dtBC", b))
                v.tensor_tensor(dts[:, 0, :], A[3][:, 2 * T:2 * T + NH], dtb[:, :], ALU.add).then_inc(SEM["dt_pre"], 1)
                dve.wait_ge(SEM["dt_exp"], at("dt_exp", b))
                L = lambda ins: link(dve, "dve0", b, ins)
                u, s, s2, q = dts[:, 1, :], dts[:, 2, :], dts[:, 3, :], dts[:, 4, :]
                L(v.tensor_scalar(dts[:, 5, :], u, 2.0, None, ALU.add))
                L(v.reciprocal(dts[:, 5, :], dts[:, 5, :]))
                L(v.tensor_tensor(s, u, dts[:, 5, :], ALU.mult))
                L(v.tensor_tensor(s2, s, s, ALU.mult))
                L(v.tensor_scalar(q, s2, 1.0 / 15, None, ALU.mult))
                for k in (13, 11, 9, 7, 5, 3):
                    L(v.scalar_tensor_tensor(q, q, 1.0 / k, s2, ALU.add, ALU.mult))
                L(v.scalar_tensor_tensor(q, q, 1.0, s, ALU.add, ALU.mult))
                L(v.tensor_scalar(dts[:, 0, :], dts[:, 0, :], 0.0, None, ALU.max))
                L(v.scalar_tensor_tensor(dts[:, 6, :], q, 2.0, dts[:, 0, :], ALU.mult, ALU.add))
                v.tensor_tensor(dts[:, 7, :], dts[:, 6, :], Aneg[:, :], ALU.mult).then_inc(SEM["a"], 1)

            def conv(b):
                dve.wait_ge(SEM["xpad"], at("xpad", b))
                L = lambda ins: link(dve, "dve0", b, ins)
                for k in range(NCONV):
                    for c in range(IC):
                        src, wk = xpad[:, c, k:k + T], convw[:, c, k:k + 1]
                        if k == 0:
                            last = v.tensor_scalar(xc[:, c, :], src, wk, convb[:, c:c + 1], ALU.mult, ALU.add)
                        else:
                            last = v.scalar_tensor_tensor(xc[:, c, :], src, wk, xc[:, c, :], ALU.mult, ALU.add)
                    if k < NCONV - 1:
                        L(last)
                    else:
                        last.then_inc(SEM["conv"], 1)
                dve.wait_ge(SEM["CB"], at("CB", b))
                v.tensor_tensor(cbm[:, :], A[0][:, 0:T], triu[:, :], ALU.mult).then_inc(SEM["cbm"], 1)
                dve.wait_ge(SEM["conv_th"], at("conv_th", b))
                v.scalar_tensor_tensor(xs2[:, :, :].rearrange("p c t -> p (c t)"), th0[:, :], 1.0,
                                       xc[:, :, :].rearrange("p c t -> p (c t)"), ALU.add, ALU.mult).then_inc(SEM["xs2"], 1)

            def ssd(b):
                dve.wait_ge(SEM["xsT"], at("xsT", b))
                heads = lambda t: t.rearrange("p (h w) -> p h w", w=HP)
                wide = lambda t: t.unsqueeze(2).broadcast_to([P, NH, HP])
                v.tensor_tensor(heads(xdt[:, :]), heads(A[1][:, :]), wide(dts[:, 6, :]), ALU.mult)
                v.tensor_tensor(heads(xD[:, :]), heads(A[1][:, :]), wide(Dpb[:, :]), ALU.mult).then_inc(SEM["xdt"], 1)
                dve.wait_ge(SEM["tz"], at("tz", b))
                v.scalar_tensor_tensor(gz[:, :], tz[:, :], 1.0, A[2][:, :], ALU.add, ALU.mult)
                for k in range(8):
                    dve.wait_ge(SEM["E"], at("E", b, k + 1))
                    if k >= 2:
                        dve.wait_ge(SEM["Yk"], at("Yk", b, k - 1))
                    v.tensor_tensor(Mh[k % 2], Ed[k % 2], cbm[:, :].unsqueeze(1).broadcast_to([P, 4, T]),
                                    ALU.mult).then_inc(SEM["M"], 1)

            def y(b):
                dve.wait_ge(SEM["Yk"], at("Yk", b, 8))
                v.tensor_tensor(y2[:, :], A[1][:, :], xD[:, :], ALU.add).then_inc(SEM["y2"], 1)
                dve.wait_ge(SEM["y2"], at("y2", b))
                v.tensor_tensor(gz[:, :], gz[:, :], y2[:, :], ALU.mult).then_inc(SEM["yg"], 1)
                dve.wait_ge(SEM["mamba"], at("mamba", b))
                dve.wait_ge(SEM["rms"], at("rms", b))
                v.scalar_tensor_tensor(x1[:, :], A[3][:, 0:D], ss0[:, 2:3], x[:, :], ALU.mult, ALU.add).then_inc(SEM["x1"], 1)

            def ln2(b):
                dve.wait_ge(SEM["mask0_in"], at("mask0_in", b, 16))
                v.tensor_scalar(mrow[0:1, :], mask0i[:, :], 4 * MASK0, -4 * MASK0, ALU.mult, ALU.add).then_inc(SEM["mrow"], 1)
                dve.wait_ge(SEM["x1"], at("x1", b))
                norm("ln2", x1[:, :], xn0, st0, mv0, "dve0", b)

            def scores(b, banks, S, mx, ss, sub):
                for j in range(4):
                    dve.wait_ge(SEM[ss], at(ss, b, j + 1))
                    c = "dve0" if ss == "S0" else "dve1"
                    pj = banks[j][:, :].rearrange("p (g k) -> p g k", g=NG)
                    link(dve, c, b, v.tensor_reduce(mx[:, 4 * j:4 * j + 4], pj, AX.X, ALU.max))
                    v.tensor_tensor(S[:, j, :, :], pj, mx[:, 4 * j:4 * j + 4].unsqueeze(2).broadcast_to([P, NG, T]),
                                    ALU.subtract).then_inc(SEM[sub], 1)

            def evac(b, banks, PT, ps, done, js):
                for j in js:
                    dve.wait_ge(SEM[ps], at(ps, b, j + 1))
                    v.tensor_copy(PT[:, j, :, :], banks[j][:, :].rearrange("p (g q) -> p g q", g=NG)).then_inc(SEM[done], 1)

            def kcopy(b, bank, KT, qk, done):
                dve.wait_ge(SEM[qk], at(qk, b, 2))
                dve.wait_ge(SEM[done], at(done, b))
                v.tensor_copy(KT[:, :, :], bank[:, :].rearrange("p (g k) -> p g k", g=NG)).then_inc(SEM[done], 1)

            def headout(b, bank, rc, o, c):
                pv = bank[:, 0:AH * (AW + 1)].rearrange("p (h w) -> p h w", w=AW + 1)
                link(dve, c, b, v.reciprocal(rc[:, :].unsqueeze(2), pv[:, :, AW:AW + 1]))
                return v.tensor_tensor(o[:, :].rearrange("p (h w) -> p h w", w=AW), pv[:, :, 0:AW],
                                       rc[:, :].unsqueeze(2).broadcast_to([P, AH, AW]), ALU.mult)

            def attn0(b):
                kcopy(b, A[3], KT0, "qk0", "qk0c")
                scores(b, A, S0, mx0, "S0", "S0sub")
                evac(b, A, PT0, "PT0ps", "PT0", range(4))
                dve.wait_ge(SEM["PV0"], at("PV0", b))
                link(dve, "dve0", b, headout(b, A[0], rc0, o0, "dve0"))
                v.tensor_tensor(x2[:, :], x1[:, :], o0[:, :], ALU.add).then_inc(SEM["x2"], 1)

            def ln3(b):
                dve.wait_ge(SEM["x2"], at("x2", b))
                norm("ln3", x2[:, :], xn0, st0, mv0, "dve0", b)

            def route(b):
                L = lambda ins, bare=False: link(dve, "dve0", b, ins, bare)
                dve.wait_ge(SEM["rout"], at("rout", b))
                lg = A[2][:, 0:NE]
                v.tensor_reduce(rt[:, 0, 0:1], lg, AX.X, ALU.max, negate=True).then_inc(SEM["rmax"], 1)
                dve.wait_ge(SEM["rexp"], at("rexp", b))
                L(v.reciprocal(rt[:, 0, 2:3], rt[:, 0, 1:2]))
                L(v.tensor_scalar(rt[:, 2, :], rt[:, 1, :], rt[:, 0, 2:3], None, ALU.mult), bare=True)
                L(v.max(rt[:, 3, 0:8], rt[:, 2, :]), bare=True)
                L(v.max_index(rti[:, 0, :], rt[:, 3, 0:8], rt[:, 2, :]))
                L(v.tensor_scalar(rt[:, 4, :], iota[:, :], rti[:, 0, 0:1], None, ALU.is_equal))
                L(v.scalar_tensor_tensor(rt[:, 5, :], rt[:, 4, :], -2.0, rt[:, 2, :], ALU.mult, ALU.add), bare=True)
                L(v.max(rt[:, 6, 0:8], rt[:, 5, :]), bare=True)
                L(v.max_index(rti[:, 1, :], rt[:, 6, 0:8], rt[:, 5, :]))
                L(v.tensor_scalar(rt[:, 7, :], iota[:, :], rti[:, 1, 0:1], None, ALU.is_equal))
                L(v.tensor_tensor(rt[:, 7, :], rt[:, 7, :], rt[:, 4, :], ALU.add))
                v.scalar_tensor_tensor(cw[:, 0:NE], rt[:, 7, :], 0.5, rt[:, 2, :], ALU.mult, ALU.mult).then_inc(SEM["cw"], 1)
                dve.wait_ge(SEM["cw"], at("cw", b))

            def experts(b):
                L = lambda ins: link(dve, "dve0", b, ins)
                for k in range(5):
                    n = 4 if k < 4 else 2
                    dve.wait_ge(SEM["gth"], at("gth", b, k + 1))
                    L(v.scalar_tensor_tensor(hg[:, 0:n * FF], thf[:, 0:n * FF], 1.0, A[0][:, 0:n * FF], ALU.add, ALU.mult))
                    dve.wait_ge(SEM["up"], at("up", b, k + 1))
                    if k >= 1:
                        dve.wait_ge(SEM["hTps"], at("hTps", b, k))
                    for i in range(n):
                        cols = slice(i * FF, (i + 1) * FF)
                        e = 4 * k + i
                        last = v.scalar_tensor_tensor(hh[:, cols], A[1][:, cols], cw[:, e:e + 1], hg[:, cols], ALU.mult, ALU.mult)
                    last.then_inc(SEM["hh"], 1)
                dve.wait_ge(SEM["down"], at("down", b))
                if not isinstance(b, int):
                    dve.wait_ge(SEM["x4"], at("x4", b, 0))
                v.tensor_tensor(handoff[:, :], A[3][:, 0:D], x2[:, :], ALU.add).then_inc(SEM["x3"], 1)

            def ln4(b):
                dve.wait_ge(SEM["x3"], at("x3", b))
                norm("ln4", handoff[:, :], xn1, st1, mv1, "dve1", b)

            def attn1(b):
                kcopy(b, B[3], KT1, "qk1", "qk1c")
                scores(b, B, S1, mx1, "S1", "S1sub")
                evac(b, B, PT1, "PT1ps", "PT1", range(4))
                dve.wait_ge(SEM["PV1"], at("PV1", b))
                headout(b, B[0], rc1, o1, "dve1").then_inc(SEM["o1"], 1)
                dve.wait_ge(SEM["proj1"], at("proj1", b))
                v.tensor_tensor(x4[:, :], B[2][:, 0:D], handoff[:, :], ALU.add).then_inc(SEM["x4"], 1)

            def lnc(b):
                dve.wait_ge(SEM["mask1_in"], at("mask1_in", b, 16))
                v.tensor_scalar(mrow1[:, :, 0:T], mask1i[:, :].bitcast(U8).unsqueeze(1).broadcast_to([1, 2, T]), -NEG, NEG,
                                ALU.mult, ALU.add).then_inc(SEM["mrow1"], 1)
                dve.wait_ge(SEM["ctx1_in"], at("ctx1_in", b, 16))
                norm("lnc", ctx1[:, :], xn1, st1, mv1, "dve1", b)

            def ln5(b):
                dve.wait_ge(SEM["x4"], at("x4", b))
                norm("ln5", x4[:, :], l5, st1, mv1, "dve1", b)

            def ln6(b):
                dve.wait_ge(SEM["ln5_xn"], at("ln5_xn", b))
                dve.wait_ge(SEM["lnc_Tps"], at("lnc_Tps", b))
                norm("ln6", l5[:, :], xn1, st1, mv1, "dve1", b)

            def latents(b):
                dst = (qn[:, :], kn[:, 0, :], kn[:, 1, :])
                for k, bank in enumerate((B[2], B[3], B[0])):
                    dve.wait_ge(SEM["latsq"], at("latsq", b, k + 1))
                    heads = lambda t: t.rearrange("p (h w) -> p h w", w=XW)
                    v.tensor_reduce(l2[:, k, :], heads(sq1[:, :]), AX.X, ALU.add).then_inc(SEM["latss"], 1)
                    dve.wait_ge(SEM["latr"], at("latr", b, k + 1))
                    v.tensor_tensor(heads(dst[k]), heads(bank[:, :]), l2[:, k, :].unsqueeze(2).broadcast_to([P, XH, XW]),
                                    ALU.mult).then_inc(SEM["latn"], 1)

            def lmax(b):
                for n, k in enumerate(BANKS_DONE):
                    dve.wait_ge(SEM["Sl"], at("Sl", b, n + 1))
                    last = v.tensor_reduce(mxl[:, 2 * k:2 * k + 2], B[k][:, :].rearrange("p (h k) -> p h k", h=2),
                                           AX.X, ALU.max)
                link(dve, "dve1", b, last)
                v.tensor_scalar(mxl[:, :], mxl[:, :], -8.0, None, ALU.mult).then_inc(SEM["mxl"], 1)
                for k in range(4):
                    dve.wait_ge(SEM["PTlps"], at("PTlps", b, k + 1))
                    v.tensor_copy(PTl[:, k, :], B[k][:, :]).then_inc(SEM["PTl"], 1)
                dve.wait_ge(SEM["PVl"], at("PVl", b))
                link(dve, "dve1", b, v.reciprocal(den[:, :], den[:, :]))
                v.tensor_tensor(ol[:, :].rearrange("p (h w) -> p h w", w=XW), B[0][:, :].rearrange("p (h w) -> p h w", w=XW),
                                den[:, :].unsqueeze(2).broadcast_to([P, XH, XW]), ALU.mult).then_inc(SEM["ol"], 1)

            def lno_(b):
                dve.wait_ge(SEM["wo"], at("wo", b))
                norm("lno", B[2][:, 0:D], fo, st1, mv1, "dve1", b)

            def ln7(b):
                L = lambda ins: link(dve, "dve1", b, ins)
                dve.wait_ge(SEM["x5"], at("x5", b))
                norm("ln7", x5[:, :], xf, st1, mv1, "dve1", b)
                dve.wait_ge(SEM["ln7_xn"], at("ln7_xn", b))
                L(v.tensor_reduce(am[:, 0:1], xf[:, :], AX.X, ALU.max, apply_absolute_value=True))
                L(v.tensor_scalar(am[:, 0:1], am[:, 0:1], Q_EPS, None, ALU.add))
                L(v.reciprocal(am[:, 1:2], am[:, 0:1]))
                L(v.tensor_scalar(xf[:, :], xf[:, :], am[:, 1:2], 127.0, ALU.mult, ALU.mult))
                L(v.tensor_scalar(xf[:, :], xf[:, :], 127.0, -128.0, ALU.min, ALU.max))
                v.tensor_scalar(am[:, 2:3], am[:, 0:1], wscale[:, 3:4], None, ALU.mult)
                v.tensor_scalar(aq[:, :], xf[:, :], ROUND, ROUND, ALU.add, ALU.subtract).then_inc(SEM["aq"], 1)
                dve.wait_ge(SEM["tern"], at("tern", b))
                dve.wait_ge(SEM["out_done"], at("out_done", b, 0))
                v.scalar_tensor_tensor(x6[:, :], B[2][:, D:2 * D], am[:, 2:3], x5[:, :], ALU.mult, ALU.add).then_inc(SEM["x6"], 1)

            s0 = {"ln1": ln1, "dt": dt, "conv": conv, "ssd": ssd, "y": y, "ln2": ln2, "attn": attn0, "ln3": ln3,
                  "route": route, "experts": experts}
            s1 = {"ln4": ln4, "attn": attn1, "lnc": lnc, "ln5": ln5, "ln6": ln6, "l2": latents, "lmax": lmax,
                  "lno": lno_, "ln7": ln7}
            program(dve, *slots(s0, s1))

        @block.scalar
        def _(act):
            s = nc.scalar
            act.wait_ge(SEM["w_in"], loads[0])
            s.activation(Aneg[:, :], Aneg[:, :], ACT.Exp).then_inc(SEM["act_setup"], 1)
            act.wait_ge(SEM["pool_setup"], 1)

            def copyT(n, bank, dst, b, wb=None):
                act.wait_ge(SEM[f"{n}_Tps"], at(f"{n}_Tps", b))
                pt = bank[:, 0:DC * T].rearrange("p (c t) -> p c t", c=DC)
                if wb is None:
                    s.activation(dst[:, :, :], pt, ACT.Copy).then_inc(SEM[f"{n}_T"], 1)
                else:
                    for c in range(DC):
                        last = s.activation(dst[:, c, :], pt[:, c, :], ACT.Identity, bias=wb[:, 1, c:c + 1], scale=wb[:, 0, c:c + 1])
                    last.then_inc(SEM[f"{n}_T"], 1)

            def dt(b):
                act.wait_ge(SEM["dt_pre"], at("dt_pre", b))
                s.activation(bcT[:, :, :], A[3][:, 0:2 * T].rearrange("p (c t) -> p c t", c=2), ACT.Copy).then_inc(SEM["bcT"], 1)
                s.activation(dts[:, 1, :], dts[:, 0, :], ACT.Abs).then_inc(SEM["dt_abs"], 1)
                act.wait_ge(SEM["dt_abs"], at("dt_abs", b))
                s.activation(dts[:, 1, :], dts[:, 1, :], ACT.Exp, scale=-1.0).then_inc(SEM["dt_exp"], 1)

            def conv(b):
                act.wait_ge(SEM["xs"], at("xs", b))
                s.activation(xpad[:, :, NCONV - 1:], A[1][:, :].rearrange("p (c t) -> p c t", c=IC), ACT.Copy).then_inc(SEM["xpad"], 1)
                act.wait_ge(SEM["z"], at("z", b))
                s.activation(tz[:, :], A[2][:, :], ACT.Tanh, scale=0.5).then_inc(SEM["tz"], 1)
                act.wait_ge(SEM["conv"], at("conv", b))
                s.activation(th0[:, :], xc[:, :, :].rearrange("p c t -> p (c t)"), ACT.Tanh, scale=0.5).then_inc(SEM["conv_th"], 1)

            def ssd(b):
                for k in range(8):
                    act.wait_ge(SEM["arg"], at("arg", b, k + 1))
                    if k >= 2:
                        act.wait_ge(SEM["M"], at("M", b, k - 1))
                    s.activation(Ed[k % 2], (A[0], A[3])[k % 2][:, :].rearrange("p (h t) -> p h t", t=T),
                                 ACT.Exp).then_inc(SEM["E"], 1)

            def y(b):
                act.wait_ge(SEM["y2"], at("y2", b))
                s.activation(sq0[:, :], y2[:, :], ACT.Square, accum_out=ss0[:, 0:1]).then_inc(SEM["ss"], 1)
                act.wait_ge(SEM["yTps"], at("yTps", b))
                s.activation(yT[:, :, :], A[0][:, :].rearrange("p (c t) -> p c t", c=IC), ACT.Copy).then_inc(SEM["yT"], 1)

            def qkv(b, banks, QT, V, qk, done):
                act.wait_ge(SEM[qk], at(qk, b))
                s.activation(QT[:, :, :], banks[2][:, :].rearrange("p (g q) -> p g q", g=NG), ACT.Copy).then_inc(SEM[done], 1)
                act.wait_ge(SEM[qk], at(qk, b, 3))
                act.wait_ge(SEM[done], at(done, b, 2))
                s.activation(V[:, :, 0:AW], banks[1][:, 0:D].rearrange("p (h w) -> p h w", w=AW), ACT.Copy).then_inc(SEM[done], 1)

            def probs(b, S, sub, done):
                for j in range(4):
                    act.wait_ge(SEM[sub], at(sub, b, j + 1))
                    s.activation(S[:, j, :, :], S[:, j, :, :], ACT.Exp, scale=AW ** -0.5).then_inc(SEM[done], 1)

            def attn0(b):
                act.wait_ge(SEM["ctxTps"], at("ctxTps", b))
                s.activation(ctxT[:, :, :], A[1][:, 0:DC * T].rearrange("p (c t) -> p c t", c=DC), ACT.Copy).then_inc(SEM["ctxT"], 1)
                qkv(b, A, QT0, V0, "qk0", "qk0c")
                probs(b, S0, "S0sub", "P0")

            def route(b):
                act.wait_ge(SEM["rmax"], at("rmax", b))
                s.activation(rt[:, 1, :], A[2][:, 0:NE], ACT.Exp, bias=rt[:, 0, 0:1], accum_out=rt[:, 0, 1:2]).then_inc(SEM["rexp"], 1)

            def experts(b):
                for k in range(5):
                    n = 4 if k < 4 else 2
                    act.wait_ge(SEM["gate"], at("gate", b, k + 1))
                    if k >= 1:
                        act.wait_ge(SEM["hh"], at("hh", b, k))
                    s.activation(thf[:, 0:n * FF], A[0][:, 0:n * FF], ACT.Tanh, scale=0.5).then_inc(SEM["gth"], 1)
                    act.wait_ge(SEM["hTps"], at("hTps", b, k + 1))
                    s.activation(hT[:, 0:n * FF], A[2][:, 0:n * FF], ACT.Copy).then_inc(SEM["hT"], 1)

            def attn1(b):
                qkv(b, B, QT1, V1, "qk1", "qk1c")
                probs(b, S1, "S1sub", "P1")
                act.wait_ge(SEM["oT1ps"], at("oT1ps", b))
                s.activation(oT1[:, :, :], B[1][:, 0:DC * T].rearrange("p (c t) -> p c t", c=DC), ACT.Copy).then_inc(SEM["oT1"], 1)

            def latents(b):
                for k, bank in enumerate((B[2], B[3], B[0])):
                    act.wait_ge(SEM["lat"], at("lat", b, k + 1))
                    if k:
                        act.wait_ge(SEM["latss"], at("latss", b, k))
                    s.activation(sq1[:, :], bank[:, :], ACT.Square).then_inc(SEM["latsq"], 1)
                for k, bank in enumerate((B[1], B[2])):
                    act.wait_ge(SEM["lat"], at("lat", b, 4 + k))
                    s.activation(Vl[:, k, :], bank[:, :], ACT.Copy).then_inc(SEM["Vl"], 1)

            def lmax(b):
                for k, (bank, dst) in enumerate(((B[3], qlT[:, :, :]), (B[0], klT[:, :, 0:T]), (B[1], klT[:, :, T:2 * T]))):
                    act.wait_ge(SEM["qlTps"], at("qlTps", b, k + 1))
                    src = bank[:, :].rearrange("p (m t) -> p m t", m=4)
                    if k == 0:
                        s.activation(dst, src, ACT.Copy, scale=qks[:, 0:1]).then_inc(SEM["qlT"], 1)
                    else:
                        s.activation(dst, src, ACT.Copy).then_inc(SEM["qlT"], 1)
                act.wait_ge(SEM["mxl"], at("mxl", b))
                for k in range(4):
                    for i in range(2):
                        n, h = 2 * k + i, head_at(k, i)
                        last = s.activation(Pl[:, k, i * 2 * T:(i + 1) * 2 * T], B[k][:, i * 2 * T:(i + 1) * 2 * T], ACT.Exp,
                                            bias=mxl[:, n:n + 1], scale=8.0, accum_out=den[:, h:h + 1])
                    last.then_inc(SEM["Pl"], 1)
                act.wait_ge(SEM["olTps"], at("olTps", b))
                s.activation(olT[:, :, :], B[1][:, :].rearrange("p (c t) -> p c t", c=IC), ACT.Copy).then_inc(SEM["olT"], 1)

            def ln7(b):
                act.wait_ge(SEM["aqTps"], at("aqTps", b))
                s.activation(aqT[:, :, :], B[3][:, 0:T].bitcast(BF16).rearrange("p (c t) -> p c t", c=DC), ACT.Copy).then_inc(SEM["aqT"], 1)

            s0 = {"ln1": lambda b: copyT("ln1", A[0], xT0, b), "dt": dt, "conv": conv, "ssd": ssd, "y": y,
                  "ln2": lambda b: copyT("ln2", A[0], xT0, b), "attn": attn0,
                  "ln3": lambda b: copyT("ln3", A[1], xT0, b), "route": route, "experts": experts}
            s1 = {"ln4": lambda b: copyT("ln4", B[0], xT1, b), "attn": attn1, "lnc": lambda b: copyT("lnc", B[0], cT, b, lnx),
                  "ln6": lambda b: copyT("ln6", B[1], lT, b, lnl), "l2": latents, "lmax": lmax, "ln7": ln7}
            program(act, *slots(s0, s1))

        @block.tensor
        def _(pe):
            mm = nc.tensor.matmul
            pe.wait_ge(SEM["dve_setup"], 1)
            pe.wait_ge(SEM["pool_setup"], 1)
            mm(A[0][:, 0:1], ones[:, :], wscale[:, 0:1], start=True, stop=True).then_inc(SEM["pe_setup"], 1)
            pe.wait_ge(SEM["dve_setup"], 6)

            def dot(out, lhs, rhs, n=DC):
                for c in range(n):
                    last = mm(out, lhs(c), rhs(c), start=c == 0, stop=c == n - 1)
                return last

            def transposes(out, src, n):
                for c in range(n):
                    last = nc.tensor.transpose(out[:, c * P:(c + 1) * P], src[:, c * P:(c + 1) * P], ident[:, :])
                return last

            def lnT(n, src, bank, b):
                pe.wait_ge(SEM[f"{n}_xn"], at(f"{n}_xn", b))
                transposes(bank, src, DC).then_inc(SEM[f"{n}_Tps"], 1)

            def inproj(b):
                pe.wait_ge(SEM["ln1_T"], at("ln1_T", b))
                tok = lambda c: xT0[:, c, :]
                dot(A[3][:, 2 * T:2 * T + NH], tok, lambda c: Win[:, c, 2 * DI + 2 * NS:])
                for k in range(2):
                    last = dot(A[3][:, k * T:(k + 1) * T], lambda c: Win[:, c, 2 * DI + k * NS:2 * DI + (k + 1) * NS], tok)
                last.then_inc(SEM["dtBC"], 1)
                for k in range(IC):
                    last = dot(A[1][:, k * T:(k + 1) * T], lambda c: Win[:, c, k * P:(k + 1) * P], tok)
                last.then_inc(SEM["xs"], 1)
                dot(A[2][:, :], tok, lambda c: Win[:, c, DI:2 * DI]).then_inc(SEM["z"], 1)

            def conv(b):
                pe.wait_ge(SEM["bcT"], at("bcT", b))
                mm(A[0][:, 0:T], bcT[:, 0, :], bcT[:, 1, :], start=True, stop=True).then_inc(SEM["CB"], 1)
                pe.wait_ge(SEM["xs2"], at("xs2", b))
                transposes(A[1], xs2[:, :, :].rearrange("p c t -> p (c t)"), IC).then_inc(SEM["xsT"], 1)

            def ssd(b):
                def arg(k):
                    pe.wait_ge(SEM["R"], at("R", b, k // 2 + 1))
                    if k >= 2:
                        pe.wait_ge(SEM["E"], at("E", b, k - 1))
                    mm((A[0], A[3])[k % 2][:, :], strict[:, :], R[:, 4 * k:4 * k + 4, :], start=True, stop=True).then_inc(SEM["arg"], 1)

                pe.wait_ge(SEM["cbm"], at("cbm", b))
                arg(0)
                arg(1)
                pe.wait_ge(SEM["xdt"], at("xdt", b))
                for k in range(8):
                    if k < 6:
                        arg(k + 2)
                    pe.wait_ge(SEM["M"], at("M", b, k + 1))
                    for i in range(4):
                        h = 4 * k + i
                        last = mm(A[1][:, h * HP:(h + 1) * HP], Mh[k % 2][:, i, :], xdt[:, h * HP:(h + 1) * HP], start=True, stop=True)
                    last.then_inc(SEM["Yk"], 1)

            def y(b):
                pe.wait_ge(SEM["yg"], at("yg", b))
                transposes(A[0], gz, IC).then_inc(SEM["yTps"], 1)
                pe.wait_ge(SEM["yT"], at("yT", b))
                dot(A[3][:, 0:D], lambda c: yT[:, c, :], lambda c: Wout[:, c, :], IC).then_inc(SEM["mamba"], 1)

            def attention(b, banks, QT, KT, V, S, PT, n, causal_):
                pe.wait_ge(SEM[f"qk{n}c"], at(f"qk{n}c", b, 3))
                if causal_:
                    for j in range(4):
                        mm(banks[j][:, :], identb[:, :], causal[:, :, :], start=True, stop=False)
                for g in range(NG):
                    for j in range(4):
                        r = slice(32 * j, 32 * j + 32)
                        last = mm(banks[j][:, g * T:(g + 1) * T], QT[r, g, :], KT[r, g, :], start=not causal_,
                                  stop=not causal_ or g == NG - 1)
                        if g == NG - 1:
                            last.then_inc(SEM[f"S{n}"], 1)
                for j in range(4):
                    pe.wait_ge(SEM[f"P{n}"], at(f"P{n}", b, j + 1))
                    for g in range(NG):
                        last = nc.tensor.transpose(banks[j][:, g * T:(g + 1) * T], S[:, j, g, :], ident[:, :])
                    last.then_inc(SEM[f"PT{n}ps"], 1)
                for j in range(4):
                    pe.wait_ge(SEM[f"PT{n}"], at(f"PT{n}", b, j + 1))
                    for g in range(NG):
                        h = 4 * g + j
                        last = mm(banks[0][:, h * (AW + 1):(h + 1) * (AW + 1)], PT[:, j, g, :], V[:, h, :], start=True, stop=True)
                last.then_inc(SEM[f"PV{n}"], 1)

            def attn0(b):
                pe.wait_ge(SEM["ctx0_in"], at("ctx0_in", b, 16))
                transposes(A[1], ctx0, DC).then_inc(SEM["ctxTps"], 1)
                pe.wait_ge(SEM["ln2_T"], at("ln2_T", b))
                pe.wait_ge(SEM["mrow"], at("mrow", b))

                def heads(bank, W, bias, src):
                    for g in range(NG):
                        o = bank[:, g * T:(g + 1) * T]
                        for c in range(DC):
                            mm(o, W[:, c, g, :], src[:, c, :], start=c == 0, stop=False)
                        last = mm(o, bias[:, g, :], mrow[:, :], start=False, stop=True)
                    return last

                heads(A[2], Wq0, QB0, xT0).then_inc(SEM["qk0"], 1)
                pe.wait_ge(SEM["ctxT"], at("ctxT", b))
                heads(A[3], Wk0, KB0, ctxT).then_inc(SEM["qk0"], 1)
                for c in range(DC):
                    mm(A[1][:, 0:D], ctxT[:, c, :], Wv0[:, c, :], start=c == 0, stop=False)
                mm(A[1][:, 0:D], mrow[:, :], VB0[:, :], start=False, stop=True).then_inc(SEM["qk0"], 1)
                attention(b, A, QT0, KT0, V0, S0, PT0, 0, False)

            def route(b):
                pe.wait_ge(SEM["ln3_T"], at("ln3_T", b))
                dot(A[2][:, 0:NE], lambda c: xT0[:, c, :], lambda c: Wr[:, c, :]).then_inc(SEM["rout"], 1)

            def experts(b):
                def gate_up(k):
                    cols = slice(4 * k * FF, min(4 * (k + 1), NBLK) * FF)
                    n = cols.stop - cols.start
                    if k >= 1:
                        pe.wait_ge(SEM["hh"], at("hh", b, k))
                    dot(A[0][:, 0:n], lambda c: xT0[:, c, :], lambda c: Wg[:, c, cols]).then_inc(SEM["gate"], 1)
                    dot(A[1][:, 0:n], lambda c: xT0[:, c, :], lambda c: Wu[:, c, cols]).then_inc(SEM["up"], 1)

                gate_up(0)
                pe.wait_ge(SEM["rexp"], at("rexp", b))
                for k in range(5):
                    n = 4 if k < 4 else 2
                    pe.wait_ge(SEM["hh"], at("hh", b, k + 1))
                    if k >= 1:
                        pe.wait_ge(SEM["hT"], at("hT", b, k))
                    transposes(A[2], hh, n).then_inc(SEM["hTps"], 1)
                    if k < 4:
                        gate_up(k + 1)
                    pe.wait_ge(SEM["hT"], at("hT", b, k + 1))
                    for i in range(n):
                        e = 4 * k + i
                        last = mm(A[3][:, 0:D], hT[:, i * FF:(i + 1) * FF], Wd[:, e, :], start=e == 0, stop=e == NBLK - 1)
                last.then_inc(SEM["down"], 1)

            def attn1(b):
                pe.wait_ge(SEM["ln4_T"], at("ln4_T", b))
                for bank, W in ((B[2], Wq1), (B[3], Wk1)):
                    for g in range(NG):
                        last = dot(bank[:, g * T:(g + 1) * T], lambda c: W[:, c, g, :], lambda c: xT1[:, c, :])
                    last.then_inc(SEM["qk1"], 1)
                dot(B[1][:, 0:D], lambda c: xT1[:, c, :], lambda c: Wv1[:, c, :]).then_inc(SEM["qk1"], 1)
                attention(b, B, QT1, KT1, V1, S1, PT1, 1, True)
                pe.wait_ge(SEM["o1"], at("o1", b))
                transposes(B[1], o1, DC).then_inc(SEM["oT1ps"], 1)
                pe.wait_ge(SEM["oT1"], at("oT1", b))
                dot(B[2][:, 0:D], lambda c: oT1[:, c, :], lambda c: Wp1[:, c, :]).then_inc(SEM["proj1"], 1)

            def latents(b):
                pe.wait_ge(SEM["ln6_T"], at("ln6_T", b))
                pe.wait_ge(SEM["lnc_T"], at("lnc_T", b))
                KV = XH * XW
                dot(B[2][:, :], lambda c: lT[:, c, :], lambda c: Wql[:, c, :]).then_inc(SEM["lat"], 1)
                dot(B[3][:, :], lambda c: cT[:, c, :], lambda c: Wkvl[:, c, 0:KV]).then_inc(SEM["lat"], 1)
                dot(B[0][:, :], lambda c: lT[:, c, :], lambda c: Wkvl[:, c, 0:KV]).then_inc(SEM["lat"], 1)
                dot(B[1][:, :], lambda c: cT[:, c, :], lambda c: Wkvl[:, c, KV:2 * KV]).then_inc(SEM["lat"], 1)
                pe.wait_ge(SEM["latn"], at("latn", b))
                dot(B[2][:, :], lambda c: lT[:, c, :], lambda c: Wkvl[:, c, KV:2 * KV]).then_inc(SEM["lat"], 1)

            def lmax(b):
                for k, (bank, src) in enumerate(((B[3], qn), (B[0], kn[:, 0, :]), (B[1], kn[:, 1, :]))):
                    pe.wait_ge(SEM["latn"], at("latn", b, (2, 3, 3)[k]))
                    if k == 2:
                        pe.wait_ge(SEM["Vl"], at("Vl", b))
                    transposes(bank, src, 4).then_inc(SEM["qlTps"], 1)
                pe.wait_ge(SEM["qlT"], at("qlT", b, 3))
                pe.wait_ge(SEM["Vl"], at("Vl", b, 2))
                pe.wait_ge(SEM["mrow1"], at("mrow1", b))
                for k in range(4):
                    mm(B[k][:, :], onesb[:, :], mrow1[:, :, :], start=True, stop=False)
                for m in range(4):
                    for r in range(2):
                        rows = slice(64 * r, 64 * r + 64)
                        k, i = 2 * r + m // 2, m % 2
                        last = mm(B[k][:, i * 2 * T:(i + 1) * 2 * T], qlT[rows, m, :], klT[rows, m, :], start=False, stop=i == 1)
                        if i == 1:
                            last.then_inc(SEM["Sl"], 1)
                for k in range(4):
                    pe.wait_ge(SEM["Pl"], at("Pl", b, k + 1))
                    transposes(B[k], Pl[:, k, :], 4).then_inc(SEM["PTlps"], 1)
                for k in range(4):
                    pe.wait_ge(SEM["PTl"], at("PTl", b, k + 1))
                    for i in range(2):
                        h = head_at(k, i)
                        for c in range(2):
                            last = mm(B[0][:, h * XW:(h + 1) * XW], PTl[:, k, (2 * i + c) * T:(2 * i + c + 1) * T],
                                      Vl[:, c, h * XW:(h + 1) * XW], start=c == 0, stop=c == 1)
                last.then_inc(SEM["PVl"], 1)
                pe.wait_ge(SEM["ol"], at("ol", b))
                transposes(B[1], ol, IC).then_inc(SEM["olTps"], 1)
                pe.wait_ge(SEM["olT"], at("olT", b))
                dot(B[2][:, 0:D], lambda c: olT[:, c, :], lambda c: Wol[:, c, :], IC).then_inc(SEM["wo"], 1)

            def tern(b):
                pe.wait_ge(SEM["aq"], at("aq", b))
                flipped = B[3][:, 0:T].bitcast(BF16)
                for c in range(DC):
                    last = nc.tensor.transpose(flipped[:, c * T:(c + 1) * T], aq[:, c * P:(c + 1) * P], identb[:, :])
                last.then_inc(SEM["aqTps"], 1)
                pe.wait_ge(SEM["aqT"], at("aqT", b))
                dot(B[2][:, D:2 * D], lambda c: aqT[:, c, :], lambda c: Wtq[:, c, :]).then_inc(SEM["tern"], 1)

            s0 = {"ln1": lambda b: lnT("ln1", xn0, A[0], b), "dt": inproj, "conv": conv, "ssd": ssd, "y": y,
                  "ln2": lambda b: lnT("ln2", xn0, A[0], b), "attn": attn0,
                  "ln3": lambda b: lnT("ln3", xn0, A[1], b), "route": route, "experts": experts}
            s1 = {"ln4": lambda b: lnT("ln4", xn1, B[0], b), "attn": attn1, "lnc": lambda b: lnT("lnc", xn1, B[0], b),
                  "ln6": lambda b: lnT("ln6", xn1, B[1], b), "l2": latents, "lmax": lmax, "ln7": tern}
            program(pe, *slots(s0, s1))


_INS = ['x', 'ctx_1024', 'mask_BxS2_ik0', 'mask_BxS2_bk0', 'L0_attn_in_proj_w', 'L0_attn_conv_w', 'L0_attn_conv_b',
        'L0_attn_A_log', 'L0_attn_Dp', 'L0_attn_dt_bias', 'L0_attn_norm_w', 'L0_attn_out_proj_w', 'L0_xattn_Wq',
        'L0_xattn_bq', 'L0_xattn_Wk', 'L0_xattn_bk', 'L0_xattn_Wv', 'L0_xattn_bv', 'L0_ffn_Wr', 'L0_ffn_Wg', 'L0_ffn_Wu',
        'L0_ffn_Wd', 'L0_ffn_Sg', 'L0_ffn_Su', 'L0_ffn_Sd', 'L1_attn_w_qkv', 'L1_attn_w_proj', 'L1_xattn_ln_x_w',
        'L1_xattn_ln_x_b', 'L1_xattn_ln_l_w', 'L1_xattn_ln_l_b', 'L1_xattn_Wq', 'L1_xattn_Wkv', 'L1_xattn_q_scale',
        'L1_xattn_k_scale', 'L1_xattn_Wo', 'L1_xattn_ln_o_w', 'L1_xattn_ln_o_b', 'L1_ffn_weight']
_TRANSPOSED = ('L0_attn_in_proj_w', 'L0_attn_out_proj_w', 'L0_xattn_Wq', 'L0_xattn_Wk', 'L0_xattn_Wv', 'L1_ffn_weight')


def kernel(**inputs):
    import numpy as _np
    import concourse.bacc as _bacc
    from concourse import mybir as _mybir
    from concourse.bass_utils import run_bass_kernel_spmd as _run

    nc = _bacc.Bacc("TRN2", target_bir_lowering=False, num_devices=1)
    arrays, args = {}, []
    for name in _INS:
        a = _np.asarray(inputs[name])
        if name in _TRANSPOSED:
            a = a.T
        a = _np.ascontiguousarray(a)
        if a.dtype == _np.bool_:
            a = a.view(_np.int32)
        arrays[f"in_{name}_dram"] = a
        args.append(nc.dram_tensor(f"in_{name}_dram", a.shape, _mybir.dt.from_np(a.dtype), kind="ExternalInput").ap())
    args.append(nc.dram_tensor("out_0_dram", (NB, T, D), F32, kind="ExternalOutput").ap())
    two_layers(nc, *args)
    r = _run(nc, [arrays], core_ids=[0])
    return r.results[0]["out_0_dram"]
```

```python
from contextlib import ExitStack

import numpy as np

import concourse.bass as bass
from concourse import mybir

F32 = mybir.dt.float32
BF16 = mybir.dt.bfloat16
I32 = mybir.dt.int32
U32 = mybir.dt.uint32
U8 = mybir.dt.uint8
ACT = mybir.ActivationFunctionType
ALU = mybir.AluOpType
AX = mybir.AxisListType

NB, T, D = 64, 128, 256
P = 128
DC = D // P
DI, NH, HP, NS, NCONV = 512, 32, 16, 128, 4
IC = DI // P
AH, AW = 16, 16
NG = AH // 4
NE, FF, FS = 16, 128, 256
NBLK = NE + FS // FF
XH, XW = 8, 64
LN_EPS, RMS_EPS, L2_CAP, Q_EPS = 1e-5, 1e-5, 1e12, 1e-8
MASK0 = 10000.0
NEG = -1e30
ROUND = 1.5 * 2.0 ** 23
CHAIN0, CHAIN1 = 41, 18
PCHAIN0, PCHAIN1 = 4, 11


def two_layers(nc, x_d, ctx_d, m0_d, m1_d, w_in, conv_w, conv_b, a_log, d_p, dt_bias, norm_w, w_out,
               wq0, bq0, wk0, bk0, wv0, bv0, w_r, w_g, w_u, w_d, s_g, s_u, s_d, w_qkv, w_proj,
               lnx_w, lnx_b, lnl_w, lnl_b, wq1, wkv1, q_sc, k_sc, wo1, lno_w, lno_b, w_tern, out_d):
    with ExitStack() as ctx:
        def sb(name, shape, dt=F32):
            return ctx.enter_context(nc.sbuf_tensor(name, shape, dt))

        PER = {}
        SEM = {}
        BASE = {"out_done": 16}

        def sig(name, per=1):
            SEM[name] = ctx.enter_context(nc.semaphore(name))
            PER[name] = per

        def at(name, b, k=1):
            return b * PER[name] + k + BASE.get(name, 0)

        Win = sb("Win", [P, DC, 2 * DI + 2 * NS + NH])
        Wout = sb("Wout", [P, IC, D])
        Wq0 = sb("Wq0", [P, DC, NG, P])
        Wk0 = sb("Wk0", [P, DC, NG, P])
        Wv0 = sb("Wv0", [P, DC, D])
        QB0 = sb("QB0", [2, NG, P])
        KB0 = sb("KB0", [2, NG, P])
        VB0 = sb("VB0", [2, D])
        Wr = sb("Wr", [P, DC, NE])
        Wg = sb("Wg", [P, DC, NBLK * FF])
        Wu = sb("Wu", [P, DC, NBLK * FF])
        Wd = sb("Wd", [P, NBLK, D])
        Wq1 = sb("Wq1", [P, DC, NG, P])
        Wk1 = sb("Wk1", [P, DC, NG, P])
        Wv1 = sb("Wv1", [P, DC, D])
        Wp1 = sb("Wp1", [P, DC, D])
        Wql = sb("Wql", [P, DC, XH * XW])
        Wkvl = sb("Wkvl", [P, DC, 2 * XH * XW])
        Wol = sb("Wol", [P, IC, D])
        Wtq = sb("Wtq", [P, DC, D], BF16)
        wscale = sb("wscale", [P, 4])
        convw = sb("convw", [P, IC, NCONV])
        convb = sb("convb", [P, IC])
        normw = sb("normw", [P, IC])
        Aneg = sb("Aneg", [P, NH])
        Dpb = sb("Dpb", [P, NH])
        dtb = sb("dtb", [P, NH])
        qks = sb("qks", [P, 2])
        lnx = sb("lnx", [P, 2, DC])
        lnl = sb("lnl", [P, 2, DC])
        lno = sb("lno", [P, 2, D])
        ident = sb("ident", [P, P])
        identb = sb("identb", [P, P], BF16)
        triu = sb("triu", [P, P])
        strict = sb("strict", [P, P])
        causal = sb("causal", [P, 4, P], BF16)
        ones = sb("ones", [P, P])
        onesb = sb("onesb", [1, P], BF16)
        iota = sb("iota", [P, NE])
        half_pow = sb("half_pow", [P, XH])
        x = sb("x", [P, D])
        ctx0 = sb("ctx0", [P, D])
        mask0i = sb("mask0i", [1, T], I32)
        mrow = sb("mrow", [2, T])
        big0 = sb("big0", [P, 6144])
        xn0 = sb("xn0", [P, D])
        xT0 = sb("xT0", [P, DC, T])
        st0 = sb("st0", [P, 6])
        mv0 = sb("mv0", [P, 4])
        xpad = sb("xpad", [P, IC, T + NCONV - 1])
        xc = sb("xc", [P, IC, T])
        th0 = sb("th0", [P, DI])
        xs2 = sb("xs2", [P, IC, T])
        bcT = sb("bcT", [P, 2, T])
        cbm = sb("cbm", [P, T])
        dts = sb("dts", [P, 8, NH])
        xdt = sb("xdt", [P, DI])
        ss0 = sb("ss0", [P, 4])
        tz = sb("tz", [P, DI])
        gz = sb("gz", [P, DI])
        x1 = sb("x1", [P, D])
        V0 = sb("V0", [P, AH, AW + 1])
        mx0 = sb("mx0", [P, AH])
        rc0 = sb("rc0", [P, AH])
        rt = sb("rt", [P, 10, NE])
        rti = sb("rti", [P, 2, 8], U32)
        cw = sb("cw", [P, NBLK])
        handoff = sb("handoff", [P, D])
        ctx1 = sb("ctx1", [P, D])
        mask1i = sb("mask1i", [1, T // 4], I32)
        mrow1 = sb("mrow1", [1, 2, 2 * T], BF16)
        big1 = sb("big1", [P, 4096])
        xn1 = sb("xn1", [P, D])
        xT1 = sb("xT1", [P, DC, T])
        st1 = sb("st1", [P, 6])
        mv1 = sb("mv1", [P, 4])
        V1 = sb("V1", [P, AH, AW + 1])
        mx1 = sb("mx1", [P, AH])
        rc1 = sb("rc1", [P, AH])
        x4 = sb("x4", [P, D])
        cT = sb("cT", [P, DC, T])
        l5 = sb("l5", [P, D])
        l2 = sb("l2", [P, 3, XH])
        qlT = sb("qlT", [P, 4, T])
        klT = sb("klT", [P, 4, 2 * T])
        Vl = sb("Vl", [P, 2, DI])
        mxl = sb("mxl", [P, XH])
        den = sb("den", [P, XH])
        x5 = sb("x5", [P, D])
        am = sb("am", [P, 4])
        aq = sb("aq", [P, D], BF16)
        aqT = sb("aqT", [P, DC, T], BF16)
        x6 = sb("x6", [P, D])

        A = [ctx.enter_context(nc.psum_tensor(f"A{i}", [P, 512], F32)) for i in range(4)]
        B = [ctx.enter_context(nc.psum_tensor(f"B{i}", [P, 512], F32)) for i in range(4)]

        def cut(t, at, c):
            return t[:, at:at + c * P].rearrange("p (c t) -> p c t", c=c)

        Wt = cut(big0, 0, 2 * DC).rearrange("p (c h) t -> p c (h t)", c=DC)
        y2 = xc[:, :, :].rearrange("p c t -> p (c t)")
        sq0 = xs2[:, :, :].rearrange("p c t -> p (c t)")
        xD, yT, ctxT, o0, x2 = th0, cut(xdt, 0, IC), cut(gz, 0, DC), xn0, x1
        QT0, KT0 = cut(big0, 4096, NG), cut(big0, 4608, NG)
        thf, hg, hh, hT = (big0[:, 512 * k:512 * k + 512] for k in range(4))
        QT1, KT1 = qlT, klT[:, :, :].rearrange("p c t -> p (c t)")[:, 0:512].rearrange("p (g t) -> p g t", g=NG)
        sq1, qn, ol = big1[:, 0:512], big1[:, 512:1024], big1[:, 0:512]
        kn = big1[:, 1024:2048].rearrange("p (c n) -> p c n", c=2)
        olT, o1, oT1, lT, fo, xf = cut(big1, 512, IC), xn1, xT1, xT1, l5, l5

        R = big0[:, 0:4096].rearrange("p (h t) -> p h t", t=T)
        Ed = [big0[:, 4096 + 512 * i:4608 + 512 * i].rearrange("p (h t) -> p h t", t=T) for i in range(2)]
        Mh = [big0[:, 5120 + 512 * i:5632 + 512 * i].rearrange("p (h t) -> p h t", t=T) for i in range(2)]
        S0 = big0[:, 0:2048].rearrange("p (j g k) -> p j g k", j=4, g=NG)
        PT0 = big0[:, 2048:4096].rearrange("p (j g q) -> p j g q", j=4, g=NG)
        S1 = big1[:, 0:2048].rearrange("p (j g k) -> p j g k", j=4, g=NG)
        PT1 = big1[:, 2048:4096].rearrange("p (j g q) -> p j g q", j=4, g=NG)

        for n, per in (("x_in", 16), ("ctx0_in", 16), ("mask0_in", 16), ("ctx1_in", 16), ("mask1_in", 16), ("out_done", 16)):
            sig(n, per)
        LNS = ("ln1", "ln2", "ln3", "ln4", "lnc", "ln5", "ln6", "lno", "ln7")
        for n in LNS:
            for what in ("var", "rstd", "xn") + ("Tps", "T") * (n not in ("ln5", "lno", "ln7")):
                sig(f"{n}_{what}")
        for n, per in (("dtBC", 1), ("xs", 1), ("z", 1), ("bcT", 1), ("xpad", 1), ("tz", 1), ("dt_abs", 1), ("dt_pre", 1),
                       ("dt_exp", 1), ("a", 1), ("R", 4), ("conv", 1), ("conv_th", 1), ("xs2", 1), ("CB", 1),
                       ("cbm", 1), ("xsT", 1), ("xdt", 1), ("arg", 8), ("E", 8), ("M", 8), ("Yk", 8), ("y2", 1), ("ss", 1),
                       ("rms", 1), ("yg", 1), ("yTps", 1), ("yT", 1), ("mamba", 1), ("x1", 1),
                       ("ctxTps", 1), ("ctxT", 1), ("mrow", 1), ("qk0", 3), ("q0c", 2), ("k0c", 1), ("S0", 4), ("S0sub", 4), ("P0", 4),
                       ("PT0ps", 4), ("PT0v", 2), ("PT0s", 2), ("PV0", 1), ("x2", 1),
                       ("rout", 1), ("rmax", 1), ("rexp", 1), ("cw", 1), ("gate", 5), ("up", 5), ("gth", 5), ("hh", 5),
                       ("hTps", 5), ("hT", 5), ("down", 1), ("x3", 1)):
            sig(n, per)
        for n, per in (("qk1", 3), ("q1c", 2), ("k1c", 1), ("S1", 4), ("S1sub", 4), ("P1", 4), ("PT1ps", 4), ("PT1v", 2), ("PT1s", 2), ("PV1", 1),
                       ("o1", 1), ("oT1ps", 1), ("oT1", 1), ("proj1", 1), ("x4", 1), ("mrow1", 1),
                       ("lat", 5), ("latsq", 3), ("latss", 3), ("latr", 3), ("latn", 3), ("Vl", 2), ("qlTps", 3), ("qlT", 3),
                       ("Sl", 4), ("mxl", 1), ("Pl", 4), ("PTlps", 4), ("PTlv", 2), ("PTls", 2), ("PVl", 1), ("ol", 1), ("olTps", 1),
                       ("olT", 1), ("wo", 1), ("x5", 1), ("aq", 1), ("aqTps", 1), ("aqT", 1), ("tern", 1), ("x6", 1)):
            sig(n, per)
        sig("dve0", CHAIN0)
        sig("dve1", CHAIN1)
        sig("pool0", PCHAIN0)
        sig("pool1", PCHAIN1)
        for n in ("passed_SP", "passed_DVE", "passed_Pool"):
            sig(n)
        for n in ("w_in", "pads", "consts", "dve_setup", "act_setup", "pe_setup", "pool_setup"):
            sig(n, 0)
        steps = {"dve0": 0, "dve1": 0, "pool0": 0, "pool1": 0}

        def link(eng, name, b, ins, bare=False):
            steps[name] += 1
            ins.then_inc(SEM[name], 1)
            eng.wait_ge(SEM[name], at(name, b, steps[name]))
            if bare:
                eng.sem_inc(SEM[f"passed_{eng.engine.name}"], 1)

        def weave(gen0, gen1):
            gens = (gen0, gen1)
            come_to = [next(g, None) if g else None for g in gens]
            for layer, name in ORDER:
                while come_to[layer] == name:
                    come_to[layer] = next(gens[layer], None)
            assert come_to == [None, None], come_to
            for n in ("dve0", "dve1", "pool0", "pool1"):
                assert steps[n] in (0, PER[n]), (n, steps[n])
                steps[n] = 0

        def program(eng, layer0, layer1):
            weave(layer0(0), None)
            with eng.Fori(0, NB - 1) as i:
                weave(layer0(i + 1), layer1(i))
            weave(None, layer1(NB - 1))

        STEPS0 = (("ln1", 1.5), ("ln1n", 1), ("ip1", 1.5), ("ip2", 2), ("ip3", 2), ("cv1", 3), ("cv2", 1.5), ("cv3", 2),
                  *((f"ssd{k}", 1.5) for k in range(9)), ("y1", 2.5), ("y2", 1.2), ("y3", 2), ("ln2", 1.5), ("ln2n", 1),
                  ("qk1", 2.5), ("qk2", 3), ("S", 3.5), *((f"m{j}", 1.5) for j in range(4)), *((f"t{j}", 1) for j in range(4)),
                  ("pv", 2), ("ln3", 1.5), ("ln3n", 1), ("r1", 1), ("r2", 3), *((f"e{k}", 5) for k in range(5)), ("x3", 1))
        STEPS1 = (("ln4", 1.5), ("ln4n", 1), ("qk1", 2), ("qk2", 3), ("S", 3.5), *((f"m{j}", 1.5) for j in range(4)),
                  *((f"t{j}", 1) for j in range(4)), ("pv", 2), ("oT", 1), ("proj", 1.5), ("lnc", 1.5), ("lncn", 1), ("ln5", 1.5),
                  ("ln6", 2), ("ln6n", 1), *((f"la{k}", 2) for k in range(5)), ("lT", 2), ("lS", 3.5), ("lP", 3),
                  *((f"lt{k}", 1) for k in range(4)), ("lpv", 2), ("lo", 1), ("wo", 1.5), ("lno", 1.5), ("x5", 2), ("ln7", 1.5),
                  ("aq", 2.5), ("aT", 1), ("tern", 1), ("x6", 1))

        def by_time():
            times = []
            for layer, table in enumerate((STEPS0, STEPS1)):
                total, at_ = sum(w for _, w in table), 0.0
                for name, w in table:
                    times.append((at_ / total, layer, name))
                    at_ += w
            return [(layer, name) for _, layer, name in sorted(times, key=lambda x: x[:2])]

        ORDER = by_time()

        Pl = big1[:, 0:2048].rearrange("p (k n) -> p k n", k=4)
        PTl = big1[:, 2048:4096].rearrange("p (k n) -> p k n", k=4)
        BANKS_DONE = (0, 2, 1, 3)

        def head_at(k, i):
            return 2 * (2 * (k % 2) + i) + k // 2

        loads = []
        block = ctx.enter_context(nc.Block())

        @block.sync
        def _(sp):
            n_w = 0

            def load(dst, src, slow=False):
                nonlocal n_w
                sp.dma_start(dst, src, allow_slow_non_contiguous=slow).then_inc(SEM["w_in"], 16)
                n_w += 16

            def chunks(dst, src):
                load(dst[:, :, :], src.rearrange("(c p) n -> p c n", p=P))

            chunks(Win, w_in)
            chunks(Wout, w_out)
            chunks(Wv0, wv0)
            chunks(Wr, w_r)
            for c in range(DC):
                rows = slice(c * P, (c + 1) * P)
                load(Wg[:, c, 0:NE * FF].rearrange("p (e f) -> p e f", f=FF), w_g[:, rows, :].rearrange("e p f -> p e f"))
                load(Wu[:, c, 0:NE * FF].rearrange("p (e f) -> p e f", f=FF), w_u[:, rows, :].rearrange("e p f -> p e f"))
                load(Wg[:, c, NE * FF:NBLK * FF], s_g[rows, :])
                load(Wu[:, c, NE * FF:NBLK * FF], s_u[rows, :])
            load(Wd[:, 0:NE, :], w_d.rearrange("e p d -> p e d"))
            load(Wd[:, NE:NBLK, :], s_d.rearrange("(c p) d -> p c d", p=P))
            load(Wv1[:, :, :], w_qkv[:, 2 * D:3 * D].rearrange("(c p) n -> p c n", p=P))
            chunks(Wp1, w_proj)
            chunks(Wql, wq1)
            chunks(Wkvl, wkv1)
            chunks(Wol, wo1)
            chunks(Wt, w_tern)
            load(convw[:, :, :], conv_w.rearrange("(c p) o k -> p c (o k)", p=P))
            for dst, src, c in ((convb, conv_b, IC), (normw, norm_w, IC)):
                load(dst[:, :], src.rearrange("(c p) -> p c", p=P), slow=True)
            for dst, src in ((Aneg, a_log), (Dpb, d_p), (dtb, dt_bias)):
                load(dst[:, :], src.partition_broadcast(P))
            for r in range(2):
                load(qks[64 * r:64 * r + 64, 0:1], q_sc.rearrange("(p a) -> p a", a=1))
                load(qks[64 * r:64 * r + 64, 1:2], k_sc.rearrange("(p a) -> p a", a=1))
            for dst, w, b_ in ((lnx, lnx_w, lnx_b), (lnl, lnl_w, lnl_b)):
                load(dst[:, 0, :], w.rearrange("(c p) -> p c", p=P), slow=True)
                load(dst[:, 1, :], b_.rearrange("(c p) -> p c", p=P), slow=True)
            load(lno[:, 0, :], lno_w.partition_broadcast(P))
            load(lno[:, 1, :], lno_b.partition_broadcast(P))
            sp.wait_ge(SEM["pads"], 1)
            for c in range(DC):
                rows = slice(c * P, (c + 1) * P)
                for dst, src in ((Wq0, wq0[rows, :]), (Wk0, wk0[rows, :]), (Wq1, w_qkv[rows, 0:D]), (Wk1, w_qkv[rows, D:2 * D])):
                    load(dst[:, c, :, :].rearrange("p g (j w) -> p (g j) w", w=32)[:, :, 1:1 + AW],
                         src.rearrange("p (h w) -> p h w", w=AW))
            for dst, src in ((QB0, bq0), (KB0, bk0)):
                load(dst[1:2, :, :].rearrange("p g (j w) -> p (g j) w", w=32)[:, :, 1:1 + AW],
                     src.rearrange("(a h w) -> a h w", a=1, w=AW))
            load(VB0[1:2, :], bv0.rearrange("(a n) -> a n", a=1))
            sp.wait_ge(SEM["w_in"], n_w)
            loads.append(n_w)

            def in0(b, first=False):
                if not first:
                    sp.wait_ge(SEM["x1"], at("x1", b, 0))
                sp.dma_start(x[:, :], x_d[bass.ds(b, 1)].rearrange("a p d -> (a p) d")).then_inc(SEM["x_in"], 16)
                if not first:
                    sp.wait_ge(SEM["ctxTps"], at("ctxTps", b, 0))
                sp.dma_start(ctx0[:, :], ctx_d[bass.ds(b, 1)].rearrange("a p d -> (a p) d")).then_inc(SEM["ctx0_in"], 16)
                if not first:
                    sp.wait_ge(SEM["mrow"], at("mrow", b, 0))
                sp.dma_start(mask0i[:, :], m0_d[bass.ds(b, 1), :]).then_inc(SEM["mask0_in"], 16)

            def in1(b, first=False):
                if not first:
                    sp.wait_ge(SEM["lnc_xn"], at("lnc_xn", b, 0))
                sp.dma_start(ctx1[:, :], ctx_d[bass.ds(b, 1)].rearrange("a p d -> (a p) d")).then_inc(SEM["ctx1_in"], 16)
                if not first:
                    sp.wait_ge(SEM["mrow1"], at("mrow1", b, 0))
                    sp.sem_inc(SEM["passed_SP"], 1)
                sp.dma_start(mask1i[:, :], m1_d[bass.ds(b, 1), :]).then_inc(SEM["mask1_in"], 16)

            def out1(b):
                sp.wait_ge(SEM["x6"], at("x6", b))
                sp.dma_start(out_d[bass.ds(b, 1)].rearrange("a p d -> (a p) d"), x6[:, :]).then_inc(SEM["out_done"], 16)

            in0(0, first=True)
            in1(0, first=True)
            in0(1)
            with sp.Fori(0, NB - 2) as i:
                in0(i + 2)
                in1(i + 1)
                out1(i)
            in1(NB - 1)
            out1(NB - 2)
            out1(NB - 1)
            sp.wait_ge(SEM["out_done"], at("out_done", NB, 0))

        @block.gpsimd
        def _(pool):
            g = nc.gpsimd
            for t in (Wq0, Wk0, Wq1, Wk1, QB0, KB0, VB0):
                g.memset(t[:], 0.0)
            g.memset(V0[:], 1.0)
            g.memset(V1[:], 1.0)
            g.memset(mrow[:], 1.0)
            g.memset(mrow1[:], 0.0)
            g.memset(xpad[:], 0.0)
            g.memset(half_pow[:], -0.5)
            g.memset(cw[:], 0.5)
            g.memset(onesb[:], 1.0)
            g.memset(causal[:], 0.0)
            g.memset(ident[:], 0.0)
            g.memset(identb[:], 0.0)
            g.memset(triu[:], 1.0)
            g.memset(strict[:], 1.0)
            g.memset(ones[:], 1.0).then_inc(SEM["pads"], 1)
            pool.wait_ge(SEM["pads"], 1)
            g.affine_select(out=ident[:, :], in_=ident[:, :], compare_op=ALU.not_equal, fill=1.0, base=0,
                            pattern=[[-1, P]], channel_multiplier=1)
            g.affine_select(out=identb[:, :], in_=identb[:, :], compare_op=ALU.not_equal, fill=1.0, base=0,
                            pattern=[[-1, P]], channel_multiplier=1)
            g.affine_select(out=triu[:, :], in_=triu[:, :], compare_op=ALU.is_ge, fill=0.0, base=0,
                            pattern=[[1, P]], channel_multiplier=-1)
            g.affine_select(out=strict[:, :], in_=strict[:, :], compare_op=ALU.is_gt, fill=0.0, base=0,
                            pattern=[[-1, P]], channel_multiplier=1)
            g.affine_select(out=causal[:, :, :], in_=causal[:, :, :], compare_op=ALU.is_ge, fill=NEG, base=0,
                            pattern=[[0, 4], [-1, P]], channel_multiplier=1)
            for t, row in ((QB0, 1), (KB0, 0)):
                v = t[:, :, :].rearrange("p g (j w) -> p (g j) w", w=32)[:, :, 0:1]
                g.memset(v, 1.0)
            g.iota(iota[:, :], pattern=[[1, NE]], base=0, channel_multiplier=0,
                   allow_small_or_imprecise_dtypes=True).then_inc(SEM["consts"], 1)
            pool.wait_ge(SEM["consts"], 1)
            pool.wait_ge(SEM["w_in"], loads[0])
            for t, row in ((QB0, 1), (KB0, 0)):
                v = t[:, :, :].rearrange("p g (j w) -> p (g j) w", w=32)[:, :, 0:1]
                last = g.affine_select(out=v, in_=v, compare_op=ALU.is_equal, fill=0.0, base=-row,
                                       pattern=[[0, AH], [0, 1]], channel_multiplier=1)
            last.then_inc(SEM["pool_setup"], 1)

            def rstd(n, mv, b, c):
                pool.wait_ge(SEM[f"{n}_var"], at(f"{n}_var", b))
                pool.sem_inc(SEM["passed_Pool"], 1)
                link(pool, c, b, g.tensor_scalar(mv[:, 2:3], mv[:, 1:2], LN_EPS, None, ALU.add))
                g.tensor_tensor(mv[:, 3:4], mv[:, 2:3], half_pow[:, 0:1], ALU.pow).then_inc(SEM[f"{n}_rstd"], 1)

            def layer0(b):
                yield "ln1"
                rstd("ln1", mv0, b, "pool0")
                yield "cv1"
                pool.wait_ge(SEM["a"], at("a", b))
                for k in range(4):
                    h = slice(8 * k, 8 * k + 8)
                    g.tensor_tensor(R[:, h, :], triu[:, :].unsqueeze(1).broadcast_to([P, 8, T]),
                                    dts[:, 7, h].unsqueeze(2).broadcast_to([P, 8, T]), ALU.mult).then_inc(SEM["R"], 1)
                yield "y1"
                pool.wait_ge(SEM["ss"], at("ss", b))
                pool.sem_inc(SEM["passed_Pool"], 1)
                link(pool, "pool0", b, g.tensor_scalar(ss0[:, 1:2], ss0[:, 0:1], 4.0 / DI, 16.0 * RMS_EPS, ALU.mult, ALU.add))
                g.tensor_tensor(ss0[:, 2:3], ss0[:, 1:2], half_pow[:, 0:1], ALU.pow).then_inc(SEM["rms"], 1)
                yield "ln2"
                rstd("ln2", mv0, b, "pool0")
                yield "ln3"
                rstd("ln3", mv0, b, "pool0")

            def layer1(b):
                yield "ln4"
                rstd("ln4", mv1, b, "pool1")
                yield "lnc"
                rstd("lnc", mv1, b, "pool1")
                yield "ln5"
                rstd("ln5", mv1, b, "pool1")
                yield "ln6"
                rstd("ln6", mv1, b, "pool1")
                for k in range(3):
                    yield f"la{k}"
                    pool.wait_ge(SEM["latss"], at("latss", b, k + 1))
                    link(pool, "pool1", b, g.tensor_tensor(l2[:, k, :], l2[:, k, :], half_pow[:, :], ALU.pow), bare=True)
                    g.tensor_scalar(l2[:, k, :], l2[:, k, :], L2_CAP, None, ALU.min).then_inc(SEM["latr"], 1)
                yield "lno"
                rstd("lno", mv1, b, "pool1")
                yield "x5"
                pool.wait_ge(SEM["lno_xn"], at("lno_xn", b))
                link(pool, "pool1", b, g.tensor_tensor(fo[:, :], fo[:, :], lno[:, 0, :], ALU.mult))
                link(pool, "pool1", b, g.tensor_tensor(fo[:, :], fo[:, :], lno[:, 1, :], ALU.add))
                g.tensor_tensor(x5[:, :], fo[:, :], x4[:, :], ALU.add).then_inc(SEM["x5"], 1)
                yield "ln7"
                rstd("ln7", mv1, b, "pool1")

            program(pool, layer0, layer1)

        @block.vector
        def _(dve):
            v = nc.vector
            dve.wait_ge(SEM["w_in"], loads[0])
            dve.wait_ge(SEM["consts"], 1)
            v.memset(x6[:], 0.0).then_inc(SEM["out_done"], 16)
            for c in range(IC):
                v.tensor_scalar(Wout[:, c, :], Wout[:, c, :], normw[:, c:c + 1], None, ALU.mult)
            dve.wait_ge(SEM["act_setup"], 1)
            v.tensor_scalar(Aneg[:, :], Aneg[:, :], -1.0, None, ALU.mult)
            v.tensor_scalar(qks[:, 0:1], qks[:, 0:1], qks[:, 1:2], None, ALU.mult)
            v.tensor_reduce(wscale[:, 0:1], Wt[:, :, :], AX.XY, ALU.add, apply_absolute_value=True).then_inc(SEM["dve_setup"], 1)
            dve.wait_ge(SEM["pe_setup"], 1)
            v.tensor_scalar(wscale[:, 1:2], A[0][:, 0:1], 1.0 / (D * D), Q_EPS, ALU.mult, ALU.add).then_inc(SEM["dve_setup"], 1)
            dve.wait_ge(SEM["dve_setup"], 2)
            v.reciprocal(wscale[:, 2:3], wscale[:, 1:2]).then_inc(SEM["dve_setup"], 1)
            dve.wait_ge(SEM["dve_setup"], 3)
            v.tensor_scalar(Wt[:, :, :], Wt[:, :, :], wscale[:, 2:3], None, ALU.mult).then_inc(SEM["dve_setup"], 1)
            dve.wait_ge(SEM["dve_setup"], 4)
            v.tensor_scalar(Wt[:, :, :], Wt[:, :, :], ROUND, ROUND, ALU.add, ALU.subtract).then_inc(SEM["dve_setup"], 1)
            dve.wait_ge(SEM["dve_setup"], 5)
            v.tensor_scalar(Wtq[:, :, :], Wt[:, :, :], 1.0, -1.0, ALU.min, ALU.max)
            v.tensor_scalar(wscale[:, 3:4], wscale[:, 1:2], 1.0 / 127.0, None, ALU.mult).then_inc(SEM["dve_setup"], 1)
            dve.wait_ge(SEM["dve_setup"], 6)
            dve.wait_ge(SEM["pool_setup"], 1)

            def norm(n, src, dst, st, mv, c, b, then):
                link(dve, c, b, v.bn_stats(st[:, :], src), bare=True)
                v.bn_aggr(mv[:, 0:2], st[:, :]).then_inc(SEM[f"{n}_var"], 1)
                yield then
                dve.wait_ge(SEM[f"{n}_rstd"], at(f"{n}_rstd", b))
                v.tensor_scalar(dst[:, :], src, mv[:, 0:1], mv[:, 3:4], ALU.subtract, ALU.mult).then_inc(SEM[f"{n}_xn"], 1)

            def scores(b, banks, S, mx, n):
                for j in range(4):
                    yield f"m{j}"
                    dve.wait_ge(SEM[f"S{n}"], at(f"S{n}", b, j + 1))
                    pj = banks[j][:, :].rearrange("p (g k) -> p g k", g=NG)
                    link(dve, f"dve{n}", b, v.tensor_reduce(mx[:, 4 * j:4 * j + 4], pj, AX.X, ALU.max))
                    v.tensor_tensor(S[:, j, :, :], pj, mx[:, 4 * j:4 * j + 4].unsqueeze(2).broadcast_to([P, NG, T]),
                                    ALU.subtract).then_inc(SEM[f"S{n}sub"], 1)

            def evac(b, banks, PT, n):
                for j in (0, 2):
                    yield f"t{j}"
                    dve.wait_ge(SEM[f"PT{n}ps"], at(f"PT{n}ps", b, j + 1))
                    v.tensor_copy(PT[:, j, :, :], banks[j][:, :].rearrange("p (g q) -> p g q", g=NG)).then_inc(SEM[f"PT{n}v"], 1)

            def kcopy(b, bank, KT, n):
                dve.wait_ge(SEM[f"qk{n}"], at(f"qk{n}", b, 2))
                v.tensor_copy(KT[:, :, :], bank[:, :].rearrange("p (g k) -> p g k", g=NG)).then_inc(SEM[f"k{n}c"], 1)

            def headout(b, bank, rc, o, c):
                pv = bank[:, 0:AH * (AW + 1)].rearrange("p (h w) -> p h w", w=AW + 1)
                link(dve, c, b, v.reciprocal(rc[:, :].unsqueeze(2), pv[:, :, AW:AW + 1]))
                return v.tensor_tensor(o[:, :].rearrange("p (h w) -> p h w", w=AW), pv[:, :, 0:AW],
                                       rc[:, :].unsqueeze(2).broadcast_to([P, AH, AW]), ALU.mult)

            def layer0(b):
                L = lambda ins, bare=False: link(dve, "dve0", b, ins, bare)
                yield "ln1"
                dve.wait_ge(SEM["x_in"], at("x_in", b, 16))
                yield from norm("ln1", x[:, :], xn0, st0, mv0, "dve0", b, "ln1n")
                yield "ip1"
                dve.wait_ge(SEM["dtBC"], at("dtBC", b))
                v.tensor_tensor(dts[:, 0, :], A[3][:, 2 * T:2 * T + NH], dtb[:, :], ALU.add).then_inc(SEM["dt_pre"], 1)
                yield "ip3"
                dve.wait_ge(SEM["dt_exp"], at("dt_exp", b))
                u, s, s2, q = dts[:, 1, :], dts[:, 2, :], dts[:, 3, :], dts[:, 4, :]
                L(v.tensor_scalar(dts[:, 5, :], u, 2.0, None, ALU.add))
                L(v.reciprocal(dts[:, 5, :], dts[:, 5, :]))
                L(v.tensor_tensor(s, u, dts[:, 5, :], ALU.mult))
                L(v.tensor_tensor(s2, s, s, ALU.mult))
                L(v.tensor_scalar(q, s2, 1.0 / 15, None, ALU.mult))
                for k in (13, 11, 9, 7, 5, 3):
                    L(v.scalar_tensor_tensor(q, q, 1.0 / k, s2, ALU.add, ALU.mult))
                L(v.scalar_tensor_tensor(q, q, 1.0, s, ALU.add, ALU.mult))
                L(v.tensor_scalar(dts[:, 0, :], dts[:, 0, :], 0.0, None, ALU.max))
                L(v.scalar_tensor_tensor(dts[:, 6, :], q, 2.0, dts[:, 0, :], ALU.mult, ALU.add))
                v.tensor_tensor(dts[:, 7, :], dts[:, 6, :], Aneg[:, :], ALU.mult).then_inc(SEM["a"], 1)
                yield "cv1"
                dve.wait_ge(SEM["xpad"], at("xpad", b))
                for k in range(NCONV):
                    for c in range(IC):
                        src, wk = xpad[:, c, k:k + T], convw[:, c, k:k + 1]
                        if k == 0:
                            last = v.tensor_scalar(xc[:, c, :], src, wk, convb[:, c:c + 1], ALU.mult, ALU.add)
                        else:
                            last = v.scalar_tensor_tensor(xc[:, c, :], src, wk, xc[:, c, :], ALU.mult, ALU.add)
                    if k < NCONV - 1:
                        L(last)
                    else:
                        last.then_inc(SEM["conv"], 1)
                yield "cv2"
                dve.wait_ge(SEM["CB"], at("CB", b))
                v.tensor_tensor(cbm[:, :], A[0][:, 0:T], triu[:, :], ALU.mult).then_inc(SEM["cbm"], 1)
                dve.wait_ge(SEM["conv_th"], at("conv_th", b))
                v.scalar_tensor_tensor(xs2[:, :, :].rearrange("p c t -> p (c t)"), th0[:, :], 1.0,
                                       xc[:, :, :].rearrange("p c t -> p (c t)"), ALU.add, ALU.mult).then_inc(SEM["xs2"], 1)
                yield "cv3"
                dve.wait_ge(SEM["xsT"], at("xsT", b))
                heads = lambda t: t.rearrange("p (h w) -> p h w", w=HP)
                wide = lambda t: t.unsqueeze(2).broadcast_to([P, NH, HP])
                v.tensor_tensor(heads(xdt[:, :]), heads(A[1][:, :]), wide(dts[:, 6, :]), ALU.mult)
                v.tensor_tensor(heads(xD[:, :]), heads(A[1][:, :]), wide(Dpb[:, :]), ALU.mult).then_inc(SEM["xdt"], 1)
                for k in range(8):
                    yield f"ssd{k + 1}"
                    dve.wait_ge(SEM["E"], at("E", b, k + 1))
                    if k >= 2:
                        dve.wait_ge(SEM["Yk"], at("Yk", b, k - 1))
                    v.tensor_tensor(Mh[k % 2], Ed[k % 2], cbm[:, :].unsqueeze(1).broadcast_to([P, 4, T]),
                                    ALU.mult).then_inc(SEM["M"], 1)
                    if k == 0:
                        dve.wait_ge(SEM["tz"], at("tz", b))
                        v.scalar_tensor_tensor(gz[:, :], tz[:, :], 1.0, A[2][:, :], ALU.add, ALU.mult)
                yield "y1"
                dve.wait_ge(SEM["Yk"], at("Yk", b, 8))
                v.tensor_tensor(y2[:, :], A[1][:, :], xD[:, :], ALU.add).then_inc(SEM["y2"], 1)
                dve.wait_ge(SEM["y2"], at("y2", b))
                v.tensor_tensor(gz[:, :], gz[:, :], y2[:, :], ALU.mult).then_inc(SEM["yg"], 1)
                dve.wait_ge(SEM["mask0_in"], at("mask0_in", b, 16))
                v.tensor_scalar(mrow[0:1, :], mask0i[:, :], 4 * MASK0, -4 * MASK0, ALU.mult, ALU.add).then_inc(SEM["mrow"], 1)
                yield "y3"
                dve.wait_ge(SEM["mamba"], at("mamba", b))
                dve.wait_ge(SEM["rms"], at("rms", b))
                v.scalar_tensor_tensor(x1[:, :], A[3][:, 0:D], ss0[:, 2:3], x[:, :], ALU.mult, ALU.add).then_inc(SEM["x1"], 1)
                yield "ln2"
                dve.wait_ge(SEM["x1"], at("x1", b))
                yield from norm("ln2", x1[:, :], xn0, st0, mv0, "dve0", b, "ln2n")
                yield "qk2"
                kcopy(b, A[3], KT0, 0)
                yield from scores(b, A, S0, mx0, 0)
                yield from evac(b, A, PT0, 0)
                yield "pv"
                dve.wait_ge(SEM["PV0"], at("PV0", b))
                L(headout(b, A[0], rc0, o0, "dve0"))
                v.tensor_tensor(x2[:, :], x1[:, :], o0[:, :], ALU.add).then_inc(SEM["x2"], 1)
                yield "ln3"
                dve.wait_ge(SEM["x2"], at("x2", b))
                yield from norm("ln3", x2[:, :], xn0, st0, mv0, "dve0", b, "ln3n")
                yield "r1"
                dve.wait_ge(SEM["rout"], at("rout", b))
                v.tensor_reduce(rt[:, 0, 0:1], A[2][:, 0:NE], AX.X, ALU.max, negate=True).then_inc(SEM["rmax"], 1)
                yield "r2"
                dve.wait_ge(SEM["rexp"], at("rexp", b))
                L(v.reciprocal(rt[:, 0, 2:3], rt[:, 0, 1:2]))
                L(v.tensor_scalar(rt[:, 2, :], rt[:, 1, :], rt[:, 0, 2:3], None, ALU.mult), bare=True)
                L(v.max(rt[:, 3, 0:8], rt[:, 2, :]), bare=True)
                L(v.max_index(rti[:, 0, :], rt[:, 3, 0:8], rt[:, 2, :]))
                L(v.tensor_scalar(rt[:, 4, :], iota[:, :], rti[:, 0, 0:1], None, ALU.is_equal))
                L(v.scalar_tensor_tensor(rt[:, 5, :], rt[:, 4, :], -2.0, rt[:, 2, :], ALU.mult, ALU.add), bare=True)
                L(v.max(rt[:, 6, 0:8], rt[:, 5, :]), bare=True)
                L(v.max_index(rti[:, 1, :], rt[:, 6, 0:8], rt[:, 5, :]))
                L(v.tensor_scalar(rt[:, 7, :], iota[:, :], rti[:, 1, 0:1], None, ALU.is_equal))
                L(v.tensor_tensor(rt[:, 7, :], rt[:, 7, :], rt[:, 4, :], ALU.add))
                v.scalar_tensor_tensor(cw[:, 0:NE], rt[:, 7, :], 0.5, rt[:, 2, :], ALU.mult, ALU.mult).then_inc(SEM["cw"], 1)
                dve.wait_ge(SEM["cw"], at("cw", b))
                for k in range(5):
                    yield f"e{k}"
                    n = 4 if k < 4 else 2
                    dve.wait_ge(SEM["gth"], at("gth", b, k + 1))
                    L(v.scalar_tensor_tensor(hg[:, 0:n * FF], thf[:, 0:n * FF], 1.0, A[0][:, 0:n * FF], ALU.add, ALU.mult))
                    dve.wait_ge(SEM["up"], at("up", b, k + 1))
                    if k >= 1:
                        dve.wait_ge(SEM["hTps"], at("hTps", b, k))
                    for i in range(n):
                        cols = slice(i * FF, (i + 1) * FF)
                        e = 4 * k + i
                        last = v.scalar_tensor_tensor(hh[:, cols], A[1][:, cols], cw[:, e:e + 1], hg[:, cols], ALU.mult, ALU.mult)
                    last.then_inc(SEM["hh"], 1)
                yield "x3"
                dve.wait_ge(SEM["down"], at("down", b))
                if not isinstance(b, int):
                    dve.wait_ge(SEM["x4"], at("x4", b, 0))
                v.tensor_tensor(handoff[:, :], A[3][:, 0:D], x2[:, :], ALU.add).then_inc(SEM["x3"], 1)

            def layer1(b):
                L = lambda ins: link(dve, "dve1", b, ins)
                yield "ln4"
                dve.wait_ge(SEM["x3"], at("x3", b))
                yield from norm("ln4", handoff[:, :], xn1, st1, mv1, "dve1", b, "ln4n")
                yield "qk2"
                kcopy(b, B[3], KT1, 1)
                yield from scores(b, B, S1, mx1, 1)
                yield from evac(b, B, PT1, 1)
                yield "pv"
                dve.wait_ge(SEM["PV1"], at("PV1", b))
                headout(b, B[0], rc1, o1, "dve1").then_inc(SEM["o1"], 1)
                dve.wait_ge(SEM["mask1_in"], at("mask1_in", b, 16))
                v.tensor_scalar(mrow1[:, :, 0:T], mask1i[:, :].bitcast(U8).unsqueeze(1).broadcast_to([1, 2, T]), -NEG, NEG,
                                ALU.mult, ALU.add).then_inc(SEM["mrow1"], 1)
                yield "proj"
                dve.wait_ge(SEM["proj1"], at("proj1", b))
                v.tensor_tensor(x4[:, :], B[2][:, 0:D], handoff[:, :], ALU.add).then_inc(SEM["x4"], 1)
                yield "lnc"
                dve.wait_ge(SEM["ctx1_in"], at("ctx1_in", b, 16))
                yield from norm("lnc", ctx1[:, :], xn1, st1, mv1, "dve1", b, "lncn")
                yield "ln5"
                dve.wait_ge(SEM["x4"], at("x4", b))
                yield from norm("ln5", x4[:, :], l5, st1, mv1, "dve1", b, "ln6")
                dve.wait_ge(SEM["ln5_xn"], at("ln5_xn", b))
                dve.wait_ge(SEM["lnc_Tps"], at("lnc_Tps", b))
                yield from norm("ln6", l5[:, :], xn1, st1, mv1, "dve1", b, "ln6n")
                dst = (qn[:, :], kn[:, 0, :], kn[:, 1, :])
                heads = lambda t: t.rearrange("p (h w) -> p h w", w=XW)
                for k, bank in enumerate((B[2], B[3], B[0])):
                    yield f"la{k}"
                    dve.wait_ge(SEM["latsq"], at("latsq", b, k + 1))
                    v.tensor_reduce(l2[:, k, :], heads(sq1[:, :]), AX.X, ALU.add).then_inc(SEM["latss"], 1)
                    yield f"la{k + 1}"
                    dve.wait_ge(SEM["latr"], at("latr", b, k + 1))
                    v.tensor_tensor(heads(dst[k]), heads(bank[:, :]), l2[:, k, :].unsqueeze(2).broadcast_to([P, XH, XW]),
                                    ALU.mult).then_inc(SEM["latn"], 1)
                yield "lS"
                for n, k in enumerate(BANKS_DONE):
                    dve.wait_ge(SEM["Sl"], at("Sl", b, n + 1))
                    last = v.tensor_reduce(mxl[:, 2 * k:2 * k + 2], B[k][:, :].rearrange("p (h k) -> p h k", h=2),
                                           AX.X, ALU.max)
                L(last)
                v.tensor_scalar(mxl[:, :], mxl[:, :], -8.0, None, ALU.mult).then_inc(SEM["mxl"], 1)
                for k in (0, 2):
                    yield f"lt{k}"
                    dve.wait_ge(SEM["PTlps"], at("PTlps", b, k + 1))
                    v.tensor_copy(PTl[:, k, :], B[k][:, :]).then_inc(SEM["PTlv"], 1)
                yield "lpv"
                dve.wait_ge(SEM["PVl"], at("PVl", b))
                L(v.reciprocal(den[:, :], den[:, :]))
                v.tensor_tensor(heads(ol[:, :]), heads(B[0][:, :]),
                                den[:, :].unsqueeze(2).broadcast_to([P, XH, XW]), ALU.mult).then_inc(SEM["ol"], 1)
                yield "lno"
                dve.wait_ge(SEM["wo"], at("wo", b))
                yield from norm("lno", B[2][:, 0:D], fo, st1, mv1, "dve1", b, "x5")
                yield "ln7"
                dve.wait_ge(SEM["x5"], at("x5", b))
                yield from norm("ln7", x5[:, :], xf, st1, mv1, "dve1", b, "aq")
                dve.wait_ge(SEM["ln7_xn"], at("ln7_xn", b))
                L(v.tensor_reduce(am[:, 0:1], xf[:, :], AX.X, ALU.max, apply_absolute_value=True))
                L(v.tensor_scalar(am[:, 0:1], am[:, 0:1], Q_EPS, None, ALU.add))
                L(v.reciprocal(am[:, 1:2], am[:, 0:1]))
                L(v.tensor_scalar(xf[:, :], xf[:, :], am[:, 1:2], 127.0, ALU.mult, ALU.mult))
                L(v.tensor_scalar(xf[:, :], xf[:, :], 127.0, -128.0, ALU.min, ALU.max))
                v.tensor_scalar(am[:, 2:3], am[:, 0:1], wscale[:, 3:4], None, ALU.mult)
                v.tensor_scalar(aq[:, :], xf[:, :], ROUND, ROUND, ALU.add, ALU.subtract).then_inc(SEM["aq"], 1)
                yield "x6"
                dve.wait_ge(SEM["tern"], at("tern", b))
                dve.wait_ge(SEM["out_done"], at("out_done", b, 0))
                v.scalar_tensor_tensor(x6[:, :], B[2][:, D:2 * D], am[:, 2:3], x5[:, :], ALU.mult, ALU.add).then_inc(SEM["x6"], 1)

            program(dve, layer0, layer1)

        @block.scalar
        def _(act):
            s = nc.scalar
            act.wait_ge(SEM["w_in"], loads[0])
            s.activation(Aneg[:, :], Aneg[:, :], ACT.Exp).then_inc(SEM["act_setup"], 1)
            act.wait_ge(SEM["pool_setup"], 1)

            def copyT(n, bank, dst, b, wb=None):
                act.wait_ge(SEM[f"{n}_Tps"], at(f"{n}_Tps", b))
                pt = bank[:, 0:DC * T].rearrange("p (c t) -> p c t", c=DC)
                if wb is None:
                    s.activation(dst[:, :, :], pt, ACT.Copy).then_inc(SEM[f"{n}_T"], 1)
                else:
                    for c in range(DC):
                        last = s.activation(dst[:, c, :], pt[:, c, :], ACT.Identity, bias=wb[:, 1, c:c + 1], scale=wb[:, 0, c:c + 1])
                    last.then_inc(SEM[f"{n}_T"], 1)

            def attention(b, banks, QT, V, S, PT, n):
                yield "qk1"
                act.wait_ge(SEM[f"qk{n}"], at(f"qk{n}", b, 1))
                s.activation(QT[:, :, :], banks[2][:, :].rearrange("p (g q) -> p g q", g=NG), ACT.Copy).then_inc(SEM[f"q{n}c"], 1)
                yield "qk2"
                act.wait_ge(SEM[f"qk{n}"], at(f"qk{n}", b, 3))
                s.activation(V[:, :, 0:AW], banks[1][:, 0:D].rearrange("p (h w) -> p h w", w=AW), ACT.Copy).then_inc(SEM[f"q{n}c"], 1)
                for j in range(4):
                    yield f"m{j}"
                    act.wait_ge(SEM[f"S{n}sub"], at(f"S{n}sub", b, j + 1))
                    s.activation(S[:, j, :, :], S[:, j, :, :], ACT.Exp, scale=AW ** -0.5).then_inc(SEM[f"P{n}"], 1)
                for j in (1, 3):
                    yield f"t{j}"
                    act.wait_ge(SEM[f"PT{n}ps"], at(f"PT{n}ps", b, j + 1))
                    s.activation(PT[:, j, :, :], banks[j][:, :].rearrange("p (g q) -> p g q", g=NG), ACT.Copy).then_inc(SEM[f"PT{n}s"], 1)

            def layer0(b):
                yield "ln1n"
                copyT("ln1", A[0], xT0, b)
                yield "ip1"
                act.wait_ge(SEM["dt_pre"], at("dt_pre", b))
                s.activation(dts[:, 1, :], dts[:, 0, :], ACT.Abs).then_inc(SEM["dt_abs"], 1)
                s.activation(bcT[:, :, :], A[3][:, 0:2 * T].rearrange("p (c t) -> p c t", c=2), ACT.Copy).then_inc(SEM["bcT"], 1)
                act.wait_ge(SEM["dt_abs"], at("dt_abs", b))
                s.activation(dts[:, 1, :], dts[:, 1, :], ACT.Exp, scale=-1.0).then_inc(SEM["dt_exp"], 1)
                yield "ip2"
                act.wait_ge(SEM["xs"], at("xs", b))
                s.activation(xpad[:, :, NCONV - 1:], A[1][:, :].rearrange("p (c t) -> p c t", c=IC), ACT.Copy).then_inc(SEM["xpad"], 1)
                yield "ip3"
                act.wait_ge(SEM["z"], at("z", b))
                s.activation(tz[:, :], A[2][:, :], ACT.Tanh, scale=0.5).then_inc(SEM["tz"], 1)
                yield "cv2"
                act.wait_ge(SEM["conv"], at("conv", b))
                s.activation(th0[:, :], xc[:, :, :].rearrange("p c t -> p (c t)"), ACT.Tanh, scale=0.5).then_inc(SEM["conv_th"], 1)
                for k in range(8):
                    yield f"ssd{k}"
                    act.wait_ge(SEM["arg"], at("arg", b, k + 1))
                    if k >= 2:
                        act.wait_ge(SEM["M"], at("M", b, k - 1))
                    s.activation(Ed[k % 2], (A[0], A[3])[k % 2][:, :].rearrange("p (h t) -> p h t", t=T),
                                 ACT.Exp).then_inc(SEM["E"], 1)
                yield "y1"
                act.wait_ge(SEM["y2"], at("y2", b))
                s.activation(sq0[:, :], y2[:, :], ACT.Square, accum_out=ss0[:, 0:1]).then_inc(SEM["ss"], 1)
                yield "y2"
                act.wait_ge(SEM["yTps"], at("yTps", b))
                s.activation(yT[:, :, :], A[0][:, :].rearrange("p (c t) -> p c t", c=IC), ACT.Copy).then_inc(SEM["yT"], 1)
                yield "ln2"
                act.wait_ge(SEM["ctxTps"], at("ctxTps", b))
                s.activation(ctxT[:, :, :], A[1][:, 0:DC * T].rearrange("p (c t) -> p c t", c=DC), ACT.Copy).then_inc(SEM["ctxT"], 1)
                yield "ln2n"
                copyT("ln2", A[0], xT0, b)
                yield from attention(b, A, QT0, V0, S0, PT0, 0)
                yield "ln3n"
                copyT("ln3", A[1], xT0, b)
                yield "r1"
                act.wait_ge(SEM["rmax"], at("rmax", b))
                s.activation(rt[:, 1, :], A[2][:, 0:NE], ACT.Exp, bias=rt[:, 0, 0:1], accum_out=rt[:, 0, 1:2]).then_inc(SEM["rexp"], 1)
                for k in range(5):
                    n = 4 if k < 4 else 2
                    yield f"e{k}"
                    act.wait_ge(SEM["gate"], at("gate", b, k + 1))
                    if k >= 1:
                        act.wait_ge(SEM["hh"], at("hh", b, k))
                    s.activation(thf[:, 0:n * FF], A[0][:, 0:n * FF], ACT.Tanh, scale=0.5).then_inc(SEM["gth"], 1)
                    yield f"e{k + 1}" if k < 4 else "x3"
                    act.wait_ge(SEM["hTps"], at("hTps", b, k + 1))
                    s.activation(hT[:, 0:n * FF], A[2][:, 0:n * FF], ACT.Copy).then_inc(SEM["hT"], 1)

            def layer1(b):
                yield "ln4n"
                copyT("ln4", B[0], xT1, b)
                yield from attention(b, B, QT1, V1, S1, PT1, 1)
                yield "oT"
                act.wait_ge(SEM["oT1ps"], at("oT1ps", b))
                s.activation(oT1[:, :, :], B[1][:, 0:DC * T].rearrange("p (c t) -> p c t", c=DC), ACT.Copy).then_inc(SEM["oT1"], 1)
                yield "lncn"
                copyT("lnc", B[0], cT, b, lnx)
                yield "ln6n"
                copyT("ln6", B[1], lT, b, lnl)
                for k, bank in enumerate((B[2], B[3], B[0])):
                    yield f"la{k}"
                    act.wait_ge(SEM["lat"], at("lat", b, k + 1))
                    if k:
                        act.wait_ge(SEM["latss"], at("latss", b, k))
                    s.activation(sq1[:, :], bank[:, :], ACT.Square).then_inc(SEM["latsq"], 1)
                for k, bank in enumerate((B[1], B[2])):
                    yield f"la{k + 3}"
                    act.wait_ge(SEM["lat"], at("lat", b, 4 + k))
                    s.activation(Vl[:, k, :], bank[:, :], ACT.Copy).then_inc(SEM["Vl"], 1)
                yield "lT"
                for k, (bank, dst) in enumerate(((B[3], qlT[:, :, :]), (B[0], klT[:, :, 0:T]), (B[1], klT[:, :, T:2 * T]))):
                    act.wait_ge(SEM["qlTps"], at("qlTps", b, k + 1))
                    src = bank[:, :].rearrange("p (m t) -> p m t", m=4)
                    if k == 0:
                        s.activation(dst, src, ACT.Copy, scale=qks[:, 0:1]).then_inc(SEM["qlT"], 1)
                    else:
                        s.activation(dst, src, ACT.Copy).then_inc(SEM["qlT"], 1)
                yield "lP"
                act.wait_ge(SEM["mxl"], at("mxl", b))
                for k in range(4):
                    for i in range(2):
                        n, h = 2 * k + i, head_at(k, i)
                        last = s.activation(Pl[:, k, i * 2 * T:(i + 1) * 2 * T], B[k][:, i * 2 * T:(i + 1) * 2 * T], ACT.Exp,
                                            bias=mxl[:, n:n + 1], scale=8.0, accum_out=den[:, h:h + 1])
                    last.then_inc(SEM["Pl"], 1)
                for k in (1, 3):
                    yield f"lt{k}"
                    act.wait_ge(SEM["PTlps"], at("PTlps", b, k + 1))
                    s.activation(PTl[:, k, :], B[k][:, :], ACT.Copy).then_inc(SEM["PTls"], 1)
                yield "lo"
                act.wait_ge(SEM["olTps"], at("olTps", b))
                s.activation(olT[:, :, :], B[1][:, :].rearrange("p (c t) -> p c t", c=IC), ACT.Copy).then_inc(SEM["olT"], 1)
                yield "aT"
                act.wait_ge(SEM["aqTps"], at("aqTps", b))
                s.activation(aqT[:, :, :], B[3][:, 0:T].bitcast(BF16).rearrange("p (c t) -> p c t", c=DC), ACT.Copy).then_inc(SEM["aqT"], 1)

            program(act, layer0, layer1)

        @block.tensor
        def _(pe):
            mm = nc.tensor.matmul
            pe.wait_ge(SEM["dve_setup"], 1)
            pe.wait_ge(SEM["pool_setup"], 1)
            mm(A[0][:, 0:1], ones[:, :], wscale[:, 0:1], start=True, stop=True).then_inc(SEM["pe_setup"], 1)
            pe.wait_ge(SEM["dve_setup"], 6)

            def dot(out, lhs, rhs, n=DC):
                for c in range(n):
                    last = mm(out, lhs(c), rhs(c), start=c == 0, stop=c == n - 1)
                return last

            def transposes(out, src, n):
                for c in range(n):
                    last = nc.tensor.transpose(out[:, c * P:(c + 1) * P], src[:, c * P:(c + 1) * P], ident[:, :])
                return last

            def lnT(n, src, bank, b):
                pe.wait_ge(SEM[f"{n}_xn"], at(f"{n}_xn", b))
                transposes(bank, src, DC).then_inc(SEM[f"{n}_Tps"], 1)

            def attention(b, banks, QT, KT, V, S, PT, n, causal_):
                yield "S"
                pe.wait_ge(SEM[f"q{n}c"], at(f"q{n}c", b, 2))
                pe.wait_ge(SEM[f"k{n}c"], at(f"k{n}c", b))
                if causal_:
                    for j in range(4):
                        mm(banks[j][:, :], identb[:, :], causal[:, :, :], start=True, stop=False)
                for g in range(NG):
                    for j in range(4):
                        r = slice(32 * j, 32 * j + 32)
                        last = mm(banks[j][:, g * T:(g + 1) * T], QT[r, g, :], KT[r, g, :], start=not causal_,
                                  stop=not causal_ or g == NG - 1)
                        if g == NG - 1:
                            last.then_inc(SEM[f"S{n}"], 1)
                for j in range(4):
                    yield f"t{j}"
                    pe.wait_ge(SEM[f"P{n}"], at(f"P{n}", b, j + 1))
                    for g in range(NG):
                        last = nc.tensor.transpose(banks[j][:, g * T:(g + 1) * T], S[:, j, g, :], ident[:, :])
                    last.then_inc(SEM[f"PT{n}ps"], 1)
                yield "pv"
                for j in (0, 1, 2, 3):
                    done = f"PT{n}{'vs'[j % 2]}"
                    pe.wait_ge(SEM[done], at(done, b, j // 2 + 1))
                    for g in range(NG):
                        h = 4 * g + j
                        last = mm(banks[0][:, h * (AW + 1):(h + 1) * (AW + 1)], PT[:, j, g, :], V[:, h, :], start=True, stop=True)
                last.then_inc(SEM[f"PV{n}"], 1)

            def arg(b, k):
                pe.wait_ge(SEM["R"], at("R", b, k // 2 + 1))
                if k >= 2:
                    pe.wait_ge(SEM["E"], at("E", b, k - 1))
                mm((A[0], A[3])[k % 2][:, :], strict[:, :], R[:, 4 * k:4 * k + 4, :], start=True, stop=True).then_inc(SEM["arg"], 1)

            def heads0(bank, W, bias, src):
                for g in range(NG):
                    o = bank[:, g * T:(g + 1) * T]
                    for c in range(DC):
                        mm(o, W[:, c, g, :], src[:, c, :], start=c == 0, stop=False)
                    last = mm(o, bias[:, g, :], mrow[:, :], start=False, stop=True)
                return last

            def gate_up(b, k):
                cols = slice(4 * k * FF, min(4 * (k + 1), NBLK) * FF)
                n = cols.stop - cols.start
                if k >= 1:
                    pe.wait_ge(SEM["hh"], at("hh", b, k))
                dot(A[0][:, 0:n], lambda c: xT0[:, c, :], lambda c: Wg[:, c, cols]).then_inc(SEM["gate"], 1)
                dot(A[1][:, 0:n], lambda c: xT0[:, c, :], lambda c: Wu[:, c, cols]).then_inc(SEM["up"], 1)

            def layer0(b):
                tok = lambda c: xT0[:, c, :]
                yield "ln1n"
                lnT("ln1", xn0, A[0], b)
                yield "ip1"
                pe.wait_ge(SEM["ln1_T"], at("ln1_T", b))
                dot(A[3][:, 2 * T:2 * T + NH], tok, lambda c: Win[:, c, 2 * DI + 2 * NS:])
                for k in range(2):
                    last = dot(A[3][:, k * T:(k + 1) * T], lambda c: Win[:, c, 2 * DI + k * NS:2 * DI + (k + 1) * NS], tok)
                last.then_inc(SEM["dtBC"], 1)
                yield "ip2"
                for k in range(IC):
                    last = dot(A[1][:, k * T:(k + 1) * T], lambda c: Win[:, c, k * P:(k + 1) * P], tok)
                last.then_inc(SEM["xs"], 1)
                yield "ip3"
                dot(A[2][:, :], tok, lambda c: Win[:, c, DI:2 * DI]).then_inc(SEM["z"], 1)
                yield "cv1"
                pe.wait_ge(SEM["bcT"], at("bcT", b))
                mm(A[0][:, 0:T], bcT[:, 0, :], bcT[:, 1, :], start=True, stop=True).then_inc(SEM["CB"], 1)
                yield "cv3"
                pe.wait_ge(SEM["xs2"], at("xs2", b))
                transposes(A[1], xs2[:, :, :].rearrange("p c t -> p (c t)"), IC).then_inc(SEM["xsT"], 1)
                yield "ssd0"
                pe.wait_ge(SEM["cbm"], at("cbm", b))
                arg(b, 0)
                arg(b, 1)
                pe.wait_ge(SEM["xdt"], at("xdt", b))
                for k in range(8):
                    yield f"ssd{k + 1}"
                    if k < 6:
                        arg(b, k + 2)
                    pe.wait_ge(SEM["M"], at("M", b, k + 1))
                    for i in range(4):
                        h = 4 * k + i
                        last = mm(A[1][:, h * HP:(h + 1) * HP], Mh[k % 2][:, i, :], xdt[:, h * HP:(h + 1) * HP], start=True, stop=True)
                    last.then_inc(SEM["Yk"], 1)
                yield "y2"
                pe.wait_ge(SEM["yg"], at("yg", b))
                transposes(A[0], gz, IC).then_inc(SEM["yTps"], 1)
                yield "y3"
                pe.wait_ge(SEM["yT"], at("yT", b))
                dot(A[3][:, 0:D], lambda c: yT[:, c, :], lambda c: Wout[:, c, :], IC).then_inc(SEM["mamba"], 1)
                yield "ln2"
                pe.wait_ge(SEM["ctx0_in"], at("ctx0_in", b, 16))
                transposes(A[1], ctx0, DC).then_inc(SEM["ctxTps"], 1)
                yield "ln2n"
                lnT("ln2", xn0, A[0], b)
                yield "qk1"
                pe.wait_ge(SEM["ln2_T"], at("ln2_T", b))
                pe.wait_ge(SEM["mrow"], at("mrow", b))
                heads0(A[2], Wq0, QB0, xT0).then_inc(SEM["qk0"], 1)
                yield "qk2"
                pe.wait_ge(SEM["ctxT"], at("ctxT", b))
                heads0(A[3], Wk0, KB0, ctxT).then_inc(SEM["qk0"], 1)
                for c in range(DC):
                    mm(A[1][:, 0:D], ctxT[:, c, :], Wv0[:, c, :], start=c == 0, stop=False)
                mm(A[1][:, 0:D], mrow[:, :], VB0[:, :], start=False, stop=True).then_inc(SEM["qk0"], 1)
                yield from attention(b, A, QT0, KT0, V0, S0, PT0, 0, False)
                yield "ln3n"
                lnT("ln3", xn0, A[1], b)
                yield "r1"
                pe.wait_ge(SEM["ln3_T"], at("ln3_T", b))
                dot(A[2][:, 0:NE], tok, lambda c: Wr[:, c, :]).then_inc(SEM["rout"], 1)
                yield "r2"
                gate_up(b, 0)
                pe.wait_ge(SEM["rexp"], at("rexp", b))
                for k in range(5):
                    n = 4 if k < 4 else 2
                    yield f"e{k + 1}" if k < 4 else "x3"
                    pe.wait_ge(SEM["hh"], at("hh", b, k + 1))
                    if k >= 1:
                        pe.wait_ge(SEM["hT"], at("hT", b, k))
                    transposes(A[2], hh, n).then_inc(SEM["hTps"], 1)
                    if k < 4:
                        gate_up(b, k + 1)
                    pe.wait_ge(SEM["hT"], at("hT", b, k + 1))
                    for i in range(n):
                        e = 4 * k + i
                        last = mm(A[3][:, 0:D], hT[:, i * FF:(i + 1) * FF], Wd[:, e, :], start=e == 0, stop=e == NBLK - 1)
                last.then_inc(SEM["down"], 1)

            def layer1(b):
                yield "ln4n"
                lnT("ln4", xn1, B[0], b)
                pe.wait_ge(SEM["ln4_T"], at("ln4_T", b))
                for step, bank, W in (("qk1", B[2], Wq1), ("qk2", B[3], Wk1)):
                    yield step
                    for g in range(NG):
                        last = dot(bank[:, g * T:(g + 1) * T], lambda c: W[:, c, g, :], lambda c: xT1[:, c, :])
                    last.then_inc(SEM["qk1"], 1)
                dot(B[1][:, 0:D], lambda c: xT1[:, c, :], lambda c: Wv1[:, c, :]).then_inc(SEM["qk1"], 1)
                yield from attention(b, B, QT1, KT1, V1, S1, PT1, 1, True)
                yield "oT"
                pe.wait_ge(SEM["o1"], at("o1", b))
                transposes(B[1], o1, DC).then_inc(SEM["oT1ps"], 1)
                yield "proj"
                pe.wait_ge(SEM["oT1"], at("oT1", b))
                dot(B[2][:, 0:D], lambda c: oT1[:, c, :], lambda c: Wp1[:, c, :]).then_inc(SEM["proj1"], 1)
                yield "lncn"
                lnT("lnc", xn1, B[0], b)
                yield "ln6n"
                lnT("ln6", xn1, B[1], b)
                KV = XH * XW
                lat = lambda c: lT[:, c, :]
                con = lambda c: cT[:, c, :]
                yield "la0"
                pe.wait_ge(SEM["ln6_T"], at("ln6_T", b))
                dot(B[2][:, :], lat, lambda c: Wql[:, c, :]).then_inc(SEM["lat"], 1)
                yield "la1"
                pe.wait_ge(SEM["lnc_T"], at("lnc_T", b))
                dot(B[3][:, :], con, lambda c: Wkvl[:, c, 0:KV]).then_inc(SEM["lat"], 1)
                yield "la2"
                dot(B[0][:, :], lat, lambda c: Wkvl[:, c, 0:KV]).then_inc(SEM["lat"], 1)
                yield "la3"
                dot(B[1][:, :], con, lambda c: Wkvl[:, c, KV:2 * KV]).then_inc(SEM["lat"], 1)
                yield "la4"
                pe.wait_ge(SEM["latn"], at("latn", b))
                dot(B[2][:, :], lat, lambda c: Wkvl[:, c, KV:2 * KV]).then_inc(SEM["lat"], 1)
                yield "lT"
                for k, (bank, src) in enumerate(((B[3], qn), (B[0], kn[:, 0, :]), (B[1], kn[:, 1, :]))):
                    pe.wait_ge(SEM["latn"], at("latn", b, (2, 3, 3)[k]))
                    if k == 2:
                        pe.wait_ge(SEM["Vl"], at("Vl", b))
                    transposes(bank, src, 4).then_inc(SEM["qlTps"], 1)
                yield "lS"
                pe.wait_ge(SEM["qlT"], at("qlT", b, 3))
                pe.wait_ge(SEM["Vl"], at("Vl", b, 2))
                pe.wait_ge(SEM["mrow1"], at("mrow1", b))
                for k in range(4):
                    mm(B[k][:, :], onesb[:, :], mrow1[:, :, :], start=True, stop=False)
                for m in range(4):
                    for r in range(2):
                        rows = slice(64 * r, 64 * r + 64)
                        k, i = 2 * r + m // 2, m % 2
                        last = mm(B[k][:, i * 2 * T:(i + 1) * 2 * T], qlT[rows, m, :], klT[rows, m, :], start=False, stop=i == 1)
                        if i == 1:
                            last.then_inc(SEM["Sl"], 1)
                for k in range(4):
                    yield f"lt{k}"
                    pe.wait_ge(SEM["Pl"], at("Pl", b, k + 1))
                    transposes(B[k], Pl[:, k, :], 4).then_inc(SEM["PTlps"], 1)
                yield "lpv"
                for k in range(4):
                    done = f"PTl{'vs'[k % 2]}"
                    pe.wait_ge(SEM[done], at(done, b, k // 2 + 1))
                    for i in range(2):
                        h = head_at(k, i)
                        for c in range(2):
                            last = mm(B[0][:, h * XW:(h + 1) * XW], PTl[:, k, (2 * i + c) * T:(2 * i + c + 1) * T],
                                      Vl[:, c, h * XW:(h + 1) * XW], start=c == 0, stop=c == 1)
                last.then_inc(SEM["PVl"], 1)
                yield "lo"
                pe.wait_ge(SEM["ol"], at("ol", b))
                transposes(B[1], ol, IC).then_inc(SEM["olTps"], 1)
                yield "wo"
                pe.wait_ge(SEM["olT"], at("olT", b))
                dot(B[2][:, 0:D], lambda c: olT[:, c, :], lambda c: Wol[:, c, :], IC).then_inc(SEM["wo"], 1)
                yield "aT"
                pe.wait_ge(SEM["aq"], at("aq", b))
                flipped = B[3][:, 0:T].bitcast(BF16)
                for c in range(DC):
                    last = nc.tensor.transpose(flipped[:, c * T:(c + 1) * T], aq[:, c * P:(c + 1) * P], identb[:, :])
                last.then_inc(SEM["aqTps"], 1)
                yield "tern"
                pe.wait_ge(SEM["aqT"], at("aqT", b))
                dot(B[2][:, D:2 * D], lambda c: aqT[:, c, :], lambda c: Wtq[:, c, :]).then_inc(SEM["tern"], 1)

            program(pe, layer0, layer1)


_INS = ['x', 'ctx_1024', 'mask_BxS2_ik0', 'mask_BxS2_bk0', 'L0_attn_in_proj_w', 'L0_attn_conv_w', 'L0_attn_conv_b',
        'L0_attn_A_log', 'L0_attn_Dp', 'L0_attn_dt_bias', 'L0_attn_norm_w', 'L0_attn_out_proj_w', 'L0_xattn_Wq',
        'L0_xattn_bq', 'L0_xattn_Wk', 'L0_xattn_bk', 'L0_xattn_Wv', 'L0_xattn_bv', 'L0_ffn_Wr', 'L0_ffn_Wg', 'L0_ffn_Wu',
        'L0_ffn_Wd', 'L0_ffn_Sg', 'L0_ffn_Su', 'L0_ffn_Sd', 'L1_attn_w_qkv', 'L1_attn_w_proj', 'L1_xattn_ln_x_w',
        'L1_xattn_ln_x_b', 'L1_xattn_ln_l_w', 'L1_xattn_ln_l_b', 'L1_xattn_Wq', 'L1_xattn_Wkv', 'L1_xattn_q_scale',
        'L1_xattn_k_scale', 'L1_xattn_Wo', 'L1_xattn_ln_o_w', 'L1_xattn_ln_o_b', 'L1_ffn_weight']
_TRANSPOSED = ('L0_attn_in_proj_w', 'L0_attn_out_proj_w', 'L0_xattn_Wq', 'L0_xattn_Wk', 'L0_xattn_Wv', 'L1_ffn_weight')


def kernel(**inputs):
    import numpy as _np
    import concourse.bacc as _bacc
    from concourse import mybir as _mybir
    from concourse.bass_utils import run_bass_kernel_spmd as _run

    nc = _bacc.Bacc("TRN2", target_bir_lowering=False, num_devices=1)
    arrays, args = {}, []
    for name in _INS:
        a = _np.asarray(inputs[name])
        if name in _TRANSPOSED:
            a = a.T
        a = _np.ascontiguousarray(a)
        if a.dtype == _np.bool_:
            a = a.view(_np.int32)
        arrays[f"in_{name}_dram"] = a
        args.append(nc.dram_tensor(f"in_{name}_dram", a.shape, _mybir.dt.from_np(a.dtype), kind="ExternalInput").ap())
    args.append(nc.dram_tensor("out_0_dram", (NB, T, D), F32, kind="ExternalOutput").ap())
    two_layers(nc, *args)
    r = _run(nc, [arrays], core_ids=[0])
    return r.results[0]["out_0_dram"]
```

```python
from contextlib import ExitStack

import numpy as np

import concourse.bass as bass
from concourse import mybir

F32 = mybir.dt.float32
BF16 = mybir.dt.bfloat16
F16 = mybir.dt.float16
I32 = mybir.dt.int32
U32 = mybir.dt.uint32
U8 = mybir.dt.uint8
ACT = mybir.ActivationFunctionType
ALU = mybir.AluOpType
AX = mybir.AxisListType

NB, T, D = 64, 128, 256
P = 128
DC = D // P
DI, NH, HP, NS, NCONV = 512, 32, 16, 128, 4
IC = DI // P
AH, AW = 16, 16
NG = AH // 4
NE, FF, FS = 16, 128, 256
NBLK = NE + FS // FF
XH, XW = 8, 64
LN_EPS, RMS_EPS, L2_EPS, Q_EPS = 1e-5, 1e-5, 1e-12, 1e-8
MASK0 = 10000.0
NEG = -1e30
ROUND = 1.5 * 2.0 ** 23
CHAIN0, CHAIN1 = 38, 19
PCHAIN0, PCHAIN1 = 3, 9


def two_layers(nc, x_d, ctx_d, m0_d, m1_d, w_in, conv_w, conv_b, a_log, d_p, dt_bias, norm_w, w_out,
               wq0, bq0, wk0, bk0, wv0, bv0, w_r, w_g, w_u, w_d, s_g, s_u, s_d, w_qkv, w_proj,
               lnx_w, lnx_b, lnl_w, lnl_b, wq1, wkv1, q_sc, k_sc, wo1, lno_w, lno_b, w_tern, out_d):
    with ExitStack() as ctx:
        def sb(name, shape, dt=F32):
            return ctx.enter_context(nc.sbuf_tensor(name, shape, dt))

        PER = {}
        SEM = {}
        BASE = {"out_done": 16}

        def sig(name, per=1):
            SEM[name] = ctx.enter_context(nc.semaphore(name))
            PER[name] = per

        def share(names):
            sig(names[0], len(names))
            for k, n in enumerate(names):
                SEM[n], PER[n], BASE[n] = SEM[names[0]], len(names), k

        def at(name, b, k=1):
            return b * PER[name] + k + BASE.get(name, 0)

        Win = sb("Win", [P, DC, 2 * DI + 2 * NS + NH])
        Wout = sb("Wout", [P, IC, D])
        Wq0 = sb("Wq0", [P, DC, D])
        Wk0 = sb("Wk0", [P, DC, D])
        Wv0 = sb("Wv0", [P, DC, D])
        bqk0 = sb("bqk0", [P, 2, DC])
        par = sb("par", [P, 2])
        bq0s = sb("bq0s", [P, DC, 2])
        bv0b = sb("bv0b", [P, D])
        mask_w = sb("mask_w", [P, P], F16)
        Wr = sb("Wr", [P, DC, NE])
        Wg = sb("Wg", [P, DC, NBLK * FF])
        Wu = sb("Wu", [P, DC, NBLK * FF])
        Wd = sb("Wd", [P, NBLK, D])
        Wq1 = sb("Wq1", [P, DC, D])
        Wk1 = sb("Wk1", [P, DC, D])
        Wv1 = sb("Wv1", [P, DC, D])
        Wp1 = sb("Wp1", [P, DC, D])
        Wql = sb("Wql", [P, DC, XH * XW])
        Wkvl = sb("Wkvl", [P, DC, 2 * XH * XW])
        Wol = sb("Wol", [P, IC, D])
        Wtq = sb("Wtq", [P, DC, D], BF16)
        wscale = sb("wscale", [P, 4])
        convw = sb("convw", [P, IC, NCONV])
        convb = sb("convb", [P, IC])
        normw = sb("normw", [P, IC])
        Aneg = sb("Aneg", [P, NH])
        Dpb = sb("Dpb", [P, NH])
        dtb = sb("dtb", [P, NH])
        qks = sb("qks", [P, 2])
        lnx = sb("lnx", [P, 2, DC])
        lnl = sb("lnl", [P, 2, DC])
        lno = sb("lno", [P, 2, D])
        ident = sb("ident", [P, P])
        identb = sb("identb", [P, P], BF16)
        triu = sb("triu", [P, P])
        strict = sb("strict", [P, P])
        causal = sb("causal", [P, 4, P], BF16)
        ones = sb("ones", [P, P])
        onesb = sb("onesb", [1, P], BF16)
        iota = sb("iota", [P, NE])
        half_pow = sb("half_pow", [P, XH])
        eps = sb("eps", [P, 2])
        x = sb("x", [P, D])
        ctx0 = sb("ctx0", [P, D])
        mask0i = sb("mask0i", [1, T], I32)
        mrow = sb("mrow", [P, NG, T], F16)
        big0 = sb("big0", [P, 6144])
        xn0 = sb("xn0", [P, D])
        xT0 = sb("xT0", [P, DC, T])
        st0 = sb("st0", [P, 6])
        mv0 = sb("mv0", [P, 4])
        xpad = sb("xpad", [P, IC, T + NCONV - 1])
        xc = sb("xc", [P, IC, T])
        th0 = sb("th0", [P, DI])
        xs2 = sb("xs2", [P, IC, T])
        bcT = sb("bcT", [P, 2, T])
        cbm = sb("cbm", [P, T])
        dts = sb("dts", [P, 8, NH])
        xdt = sb("xdt", [P, DI])
        ss0 = sb("ss0", [P, 4])
        tz = sb("tz", [P, DI])
        gz = sb("gz", [P, DI])
        x1 = sb("x1", [P, D])
        V0 = sb("V0", [P, AH, AW + 1])
        mx0 = sb("mx0", [P, AH])
        rc0 = sb("rc0", [P, AH])
        rt = sb("rt", [P, 10, NE])
        rti = sb("rti", [P, 2, 8], U32)
        cw = sb("cw", [P, NBLK])
        handoff = sb("handoff", [P, D])
        ctx1 = sb("ctx1", [P, D])
        mask1i = sb("mask1i", [1, T // 4], I32)
        mrow1 = sb("mrow1", [1, 2, 2 * T], BF16)
        big1 = sb("big1", [P, 4096])
        xn1 = sb("xn1", [P, D])
        xT1 = sb("xT1", [P, DC, T])
        st1 = sb("st1", [P, 6])
        mv1 = sb("mv1", [P, 4])
        V1 = sb("V1", [P, AH, AW + 1])
        mx1 = sb("mx1", [P, AH])
        rc1 = sb("rc1", [P, AH])
        x4 = sb("x4", [P, D])
        cT = sb("cT", [P, DC, T])
        l5 = sb("l5", [P, D])
        l2 = sb("l2", [P, 3, XH])
        qlT = sb("qlT", [P, 4, T])
        klT = sb("klT", [P, 4, 2 * T])
        Vl = sb("Vl", [P, 2, DI])
        mxl = sb("mxl", [P, XH])
        den = sb("den", [P, XH])
        x5 = sb("x5", [P, D])
        am = sb("am", [P, 4])
        aq = sb("aq", [P, D], BF16)
        aqT = sb("aqT", [P, DC, T], BF16)
        x6 = sb("x6", [P, D])

        A = [ctx.enter_context(nc.psum_tensor(f"A{i}", [P, 512], F32)) for i in range(4)]
        B = [ctx.enter_context(nc.psum_tensor(f"B{i}", [P, 512], F32)) for i in range(4)]

        def cut(t, at, c):
            return t[:, at:at + c * P].rearrange("p (c t) -> p c t", c=c)

        Wt = cut(big0, 0, 2 * DC).rearrange("p (c h) t -> p c (h t)", c=DC)
        y2 = xc[:, :, :].rearrange("p c t -> p (c t)")
        sq0 = xs2[:, :, :].rearrange("p c t -> p (c t)")
        xD, yT, ctxT, o0, x2 = th0, cut(xdt, 0, IC), cut(gz, 0, DC), xn0, x1
        QT0, KT0 = cut(big0, 4096, NG), cut(big0, 4608, DC)
        thf, hg, hh, hT = (big0[:, 512 * k:512 * k + 512] for k in range(4))
        QT1, KT1 = qlT, klT[:, 0, :].rearrange("p (c t) -> p c t", c=DC)
        sq1, qn = big1[:, 2048:2560], big1[:, 512:1024]
        kn = big1[:, 1024:2048].rearrange("p (c n) -> p c n", c=2)
        olT, o1, oT1, lT, fo, xf = cut(big1, 512, IC), xn1, xT1, xT1, l5, l5

        R = big0[:, 0:4096].rearrange("p (h t) -> p h t", t=T)
        Ed = [big0[:, 4096 + 512 * i:4608 + 512 * i].rearrange("p (h t) -> p h t", t=T) for i in range(2)]
        Mh = [big0[:, 5120 + 512 * i:5632 + 512 * i].rearrange("p (h t) -> p h t", t=T) for i in range(2)]
        Yt = big0[:, 0:1024]
        S0 = big0[:, 0:2048].rearrange("p (j g k) -> p j g k", j=4, g=NG)
        PT0 = big0[:, 2048:4096].rearrange("p (j g q) -> p j g q", j=4, g=NG)
        S1 = big1[:, 0:2048].rearrange("p (j g k) -> p j g k", j=4, g=NG)
        PT1 = big1[:, 2048:4096].rearrange("p (j g q) -> p j g q", j=4, g=NG)

        for n, per in (("x_in", 16), ("ctx0_in", 16), ("mask0_in", 16), ("ctx1_in", 16), ("mask1_in", 16), ("out_done", 16)):
            sig(n, per)
        for LNS in (("ln1", "ln2", "ln3"), ("ln4", "lnc", "ln5", "ln6", "lno", "ln7")):
            for what in ("var", "rstd", "xn"):
                share([f"{n}_{what}" for n in LNS])
            for what in ("Tps", "T"):
                share([f"{n}_{what}" for n in LNS if n not in ("ln5", "lno", "ln7")])
        for n, per in (("ip", 3), ("bcT", 1), ("xpad", 1), ("tz", 1), ("dt_abs", 1), ("dt_pre", 1),
                       ("dt_exp", 1), ("a", 1), ("R", 4), ("conv", 1), ("conv_th", 1), ("xs2", 1), ("CB", 1),
                       ("cbm", 1), ("xsT", 1), ("xdt", 1), ("arg", 8), ("E", 8), ("M", 8), ("Yk", 8), ("Yt", 2), ("Yb", 2), ("y2", 1), ("ss", 1),
                       ("rms", 1), ("yg", 1), ("yTps", 1), ("yT", 1), ("mamba", 1), ("x1", 1),
                       ("ctxTps", 1), ("ctxT", 1), ("mrow", 1), ("qk0", 3), ("q0c", 1), ("k0c", 1), ("v0c", 1), ("S0", 4), ("S0max", 4), ("P0", 4),
                       ("PT0ps", 4), ("PT0v", 2), ("PT0s", 2), ("PV0", 2), ("OT0", 1), ("x2", 1),
                       ("rout", 1), ("rmax", 1), ("rexp", 1), ("cw", 1), ("gu", 10), ("gth", 5), ("hh", 5),
                       ("hTps", 5), ("hT", 5), ("down", 1), ("x3", 1)):
            sig(n, per)
        for n, per in (("qk1", 3), ("q1c", 1), ("k1c", 1), ("v1c", 1), ("S1", 4), ("S1max", 4), ("P1", 4), ("PT1ps", 4), ("PT1v", 2), ("PT1s", 2), ("PV1", 2), ("OT1", 1),
                       ("o1", 1), ("oT1ps", 1), ("oT1", 1), ("proj1", 1), ("x4", 1), ("mrow1", 1),
                       ("lat", 5), ("latsq", 3), ("latss", 3), ("latr", 3), ("latn", 3), ("Vl", 2), ("qlTps", 3), ("qlT", 3),
                       ("Sl", 4), ("mxl", 1), ("Pl", 4), ("PTlps", 4), ("PTlv", 2), ("PTls", 2), ("Pln", 4), ("PVl", 1),
                       ("olT", 1), ("wo", 1), ("x4b", 1), ("x5", 1), ("aq", 1), ("aqTps", 1), ("aqT", 1), ("tern", 1), ("x6", 1)):
            sig(n, per)
        sig("ln1_st")
        sig("ln1_eps")
        sig("dve0", CHAIN0)
        sig("dve1", CHAIN1)
        sig("pool0", PCHAIN0)
        sig("pool1", PCHAIN1)
        for n in ("passed_SP", "passed_DVE", "passed_Pool"):
            sig(n)
        for n in ("w_in", "pads", "consts", "dve_setup", "act_setup", "pe_setup"):
            sig(n, 0)
        steps = {"dve0": 0, "dve1": 0, "pool0": 0, "pool1": 0}

        def link(eng, name, b, ins, bare=False):
            if name in steps:
                steps[name] += 1
            ins.then_inc(SEM[name], 1)
            eng.wait_ge(SEM[name], at(name, b, steps.get(name, 1)))
            if bare:
                eng.sem_inc(SEM[f"passed_{eng.engine.name}"], 1)

        def weave(gen0, gen1, order=None):
            gens = (gen0, gen1)
            come_to = [next(g, None) if g else None for g in gens]
            for layer, name in order or ORDER:
                while come_to[layer] == name:
                    come_to[layer] = next(gens[layer], None)
            assert come_to == [None, None], come_to
            for n in ("dve0", "dve1", "pool0", "pool1"):
                assert steps[n] in (0, PER[n]), (n, steps[n])
                steps[n] = 0

        def program(eng, first, layer0, layer1):
            weave(first(0), None, [(0, "ln1"), (0, "ln1a"), (0, "ln1n")])
            weave(layer0(0, 1), None)
            with eng.Fori(0, NB - 2) as i:
                weave(layer0(i + 1, i + 2), layer1(i))
            weave(layer0(NB - 1, None), layer1(NB - 2))
            weave(None, layer1(NB - 1))

        WOVEN = """
             | ln4 | ip1 ip1b | ln4n lnc | ip2 | qk1 lncn | ip3 | qk2 qk3 S | ip3h | S1 S2 | cv1 cv2 | S3 m0 | cv3 ssd0 ssd1
            ssd2 ssd3 | m1 | ssd4 ssd5 ssd6 | m2 | ssd7 | m3 t0 t1 t2 t3 | ssd8 | pv pv1 pv2 pv3 | y0 | la1 la1h | y1 y2 |
            ot lq0 | y3 y3h | la3 | ln2 | la3h ln0u oT | ln2n | proj | qk1 | ln5 | qk2 qk3 | ln6 | S S1 S2 | ln6n | S3 m0 m1
            m2 | la0 | m3 t0 | la0h lq1 la2 | t1 t2 | la2h | t3 pv pv1 pv2 | ln1u lq2 | pv3 | la4 | ot ln3 | la4h ln2u lT0
            lT1 | ln3n | lT2 | r1 g0 g0h u0 u0h | lS lS1 lS2 lS3 | e1 | lP0 lP1 | g1 g1h | lP2 lP3 | u1 | lt0 | u1h | lt1 |
            d0 d0h | lt2 lt3 lpv0 lpv1 lpv2 lpv3 lo | e2 g2 g2h u2 u2h d1 | wo woh lno | d1h e3 | x5 | g3 g3h | ln7 | u3 u3h
            d2 d2h ln1 e4 g4 g4h u4 | aq | u4h ln1a d3 d3h | aT | ln1n e5 | tern x6 | d4 x3
        """
        ORDER = [(k % 2, step) for k, run in enumerate(WOVEN.split("|")) for step in run.split()]

        Pl = big1[:, 0:2048].rearrange("p (k n) -> p k n", k=4)
        PTl = big1[:, 2048:4096].rearrange("p (k n) -> p k n", k=4)
        BANKS_DONE = (0, 2, 1, 3)

        def head_at(k, i):
            return 2 * (2 * (k % 2) + i) + k // 2

        loads = []
        block = ctx.enter_context(nc.Block())

        @block.sync
        def _(sp):
            n_w = 0

            def load(dst, src, slow=False):
                nonlocal n_w
                sp.dma_start(dst, src, allow_slow_non_contiguous=slow).then_inc(SEM["w_in"], 16)
                n_w += 16

            def chunks(dst, src):
                load(dst[:, :, :], src.rearrange("(c p) n -> p c n", p=P))

            chunks(Win, w_in)
            chunks(Wout, w_out)
            chunks(Wv0, wv0)
            chunks(Wr, w_r)
            for c in range(DC):
                rows = slice(c * P, (c + 1) * P)
                load(Wg[:, c, 0:NE * FF].rearrange("p (e f) -> p e f", f=FF), w_g[:, rows, :].rearrange("e p f -> p e f"))
                load(Wu[:, c, 0:NE * FF].rearrange("p (e f) -> p e f", f=FF), w_u[:, rows, :].rearrange("e p f -> p e f"))
                load(Wg[:, c, NE * FF:NBLK * FF], s_g[rows, :])
                load(Wu[:, c, NE * FF:NBLK * FF], s_u[rows, :])
            load(Wd[:, 0:NE, :], w_d.rearrange("e p d -> p e d"))
            load(Wd[:, NE:NBLK, :], s_d.rearrange("(c p) d -> p c d", p=P))
            load(Wv1[:, :, :], w_qkv[:, 2 * D:3 * D].rearrange("(c p) n -> p c n", p=P))
            chunks(Wp1, w_proj)
            chunks(Wql, wq1)
            chunks(Wkvl, wkv1)
            chunks(Wol, wo1)
            chunks(Wt, w_tern)
            load(convw[:, :, :], conv_w.rearrange("(c p) o k -> p c (o k)", p=P))
            for dst, src, c in ((convb, conv_b, IC), (normw, norm_w, IC)):
                load(dst[:, :], src.rearrange("(c p) -> p c", p=P), slow=True)
            for dst, src in ((Aneg, a_log), (Dpb, d_p), (dtb, dt_bias)):
                load(dst[:, :], src.partition_broadcast(P))
            for r in range(2):
                load(qks[64 * r:64 * r + 64, 0:1], q_sc.rearrange("(p a) -> p a", a=1))
                load(qks[64 * r:64 * r + 64, 1:2], k_sc.rearrange("(p a) -> p a", a=1))
            for dst, w, b_ in ((lnx, lnx_w, lnx_b), (lnl, lnl_w, lnl_b)):
                load(dst[:, 0, :], w.rearrange("(c p) -> p c", p=P), slow=True)
                load(dst[:, 1, :], b_.rearrange("(c p) -> p c", p=P), slow=True)
            load(lno[:, 0, :], lno_w.partition_broadcast(P))
            load(lno[:, 1, :], lno_b.partition_broadcast(P))
            for dst, src in ((Wq0, wq0), (Wk0, wk0)):
                chunks(dst, src)
            for k, dst in enumerate((Wq1, Wk1)):
                load(dst[:, :, :], w_qkv[:, k * D:(k + 1) * D].rearrange("(c p) n -> p c n", p=P))
            for k, src in enumerate((bq0, bk0)):
                load(bqk0[:, k, :], src.rearrange("(c p) -> p c", p=P), slow=True)
            load(bv0b[:, :], bv0.partition_broadcast(P))
            sp.wait_ge(SEM["w_in"], n_w)
            loads.append(n_w)

            def in0(b, first=False):
                if not first:
                    sp.wait_ge(SEM["x1"], at("x1", b, 0))
                sp.dma_start(x[:, :], x_d[bass.ds(b, 1)].rearrange("a p d -> (a p) d")).then_inc(SEM["x_in"], 16)
                if not first:
                    sp.wait_ge(SEM["ctxTps"], at("ctxTps", b, 0))
                sp.dma_start(ctx0[:, :], ctx_d[bass.ds(b, 1)].rearrange("a p d -> (a p) d")).then_inc(SEM["ctx0_in"], 16)
                if not first:
                    sp.wait_ge(SEM["mrow"], at("mrow", b, 0))
                sp.dma_start(mask0i[:, :], m0_d[bass.ds(b, 1), :]).then_inc(SEM["mask0_in"], 16)

            def in1(b, first=False):
                if not first:
                    sp.wait_ge(SEM["lnc_xn"], at("lnc_xn", b - 1))
                sp.dma_start(ctx1[:, :], ctx_d[bass.ds(b, 1)].rearrange("a p d -> (a p) d")).then_inc(SEM["ctx1_in"], 16)
                if not first:
                    sp.wait_ge(SEM["mrow1"], at("mrow1", b, 0))
                    sp.sem_inc(SEM["passed_SP"], 1)
                sp.dma_start(mask1i[:, :], m1_d[bass.ds(b, 1), :]).then_inc(SEM["mask1_in"], 16)

            def out1(b):
                sp.wait_ge(SEM["x6"], at("x6", b))
                sp.dma_start(out_d[bass.ds(b, 1)].rearrange("a p d -> (a p) d"), x6[:, :]).then_inc(SEM["out_done"], 16)

            in0(0, first=True)
            in1(0, first=True)
            in0(1)
            with sp.Fori(0, NB - 2) as i:
                in0(i + 2)
                in1(i + 1)
                out1(i)
            in1(NB - 1)
            out1(NB - 2)
            out1(NB - 1)
            sp.wait_ge(SEM["out_done"], at("out_done", NB, 0))

        @block.gpsimd
        def _(pool):
            g = nc.gpsimd
            g.memset(mask_w[:], 0.0)
            g.memset(mrow[:], 0.0)
            g.memset(V0[:], 1.0)
            g.memset(V1[:], 1.0)
            g.memset(mrow1[:], 0.0)
            g.memset(xpad[:], 0.0)
            g.memset(half_pow[:], -0.5)
            g.memset(eps[:, 0:1], LN_EPS)
            g.memset(eps[:, 1:2], 16.0 * RMS_EPS)
            g.memset(cw[:], 0.5)
            g.memset(onesb[:], 1.0)
            g.memset(causal[:], 0.0)
            g.memset(ident[:], 0.0)
            g.memset(identb[:], 0.0)
            g.memset(triu[:], 1.0)
            g.memset(strict[:], 1.0)
            g.memset(ones[:], 1.0).then_inc(SEM["pads"], 1)
            pool.wait_ge(SEM["pads"], 1)
            g.affine_select(out=ident[:, :], in_=ident[:, :], compare_op=ALU.not_equal, fill=1.0, base=0,
                            pattern=[[-1, P]], channel_multiplier=1)
            g.affine_select(out=identb[:, :], in_=identb[:, :], compare_op=ALU.not_equal, fill=1.0, base=0,
                            pattern=[[-1, P]], channel_multiplier=1)
            g.affine_select(out=triu[:, :], in_=triu[:, :], compare_op=ALU.is_ge, fill=0.0, base=0,
                            pattern=[[1, P]], channel_multiplier=-1)
            g.affine_select(out=strict[:, :], in_=strict[:, :], compare_op=ALU.is_gt, fill=0.0, base=0,
                            pattern=[[-1, P]], channel_multiplier=1)
            g.affine_select(out=causal[:, :, :], in_=causal[:, :, :], compare_op=ALU.is_ge, fill=NEG, base=0,
                            pattern=[[0, 4], [-1, P]], channel_multiplier=1)
            g.iota(iota[:, :], pattern=[[1, NE]], base=0, channel_multiplier=0,
                   allow_small_or_imprecise_dtypes=True).then_inc(SEM["consts"], 1)
            def rstd(n, mv, b, c):
                pool.wait_ge(SEM[f"{n}_var"], at(f"{n}_var", b))
                link(pool, c, b, g.tensor_tensor(mv[:, 2:3], mv[:, 1:2], eps[:, 0:1], ALU.add))
                g.tensor_tensor(mv[:, 3:4], mv[:, 2:3], half_pow[:, 0:1], ALU.pow).then_inc(SEM[f"{n}_rstd"], 1)

            def first(b):
                yield "ln1"
                rstd("ln1", mv0, b, "ln1_eps")

            def layer0(b, following):
                yield "cv1"
                pool.wait_ge(SEM["a"], at("a", b))
                for k in range(4):
                    h = slice(8 * k, 8 * k + 8)
                    g.tensor_tensor(R[:, h, :], triu[:, :].unsqueeze(1).broadcast_to([P, 8, T]),
                                    dts[:, 7, h].unsqueeze(2).broadcast_to([P, 8, T]), ALU.mult).then_inc(SEM["R"], 1)
                yield "y1"
                pool.wait_ge(SEM["ss"], at("ss", b))
                link(pool, "pool0", b, g.tensor_tensor(ss0[:, 1:2], ss0[:, 0:1], eps[:, 1:2], ALU.add))
                g.tensor_tensor(ss0[:, 2:3], ss0[:, 1:2], half_pow[:, 0:1], ALU.pow).then_inc(SEM["rms"], 1)
                yield "ln2"
                rstd("ln2", mv0, b, "pool0")
                yield "ln3"
                rstd("ln3", mv0, b, "pool0")
                if following is not None:
                    yield from first(following)

            def layer1(b):
                yield "ln4"
                rstd("ln4", mv1, b, "pool1")
                yield "lnc"
                rstd("lnc", mv1, b, "pool1")

                def unit(k):
                    yield f"lq{k}"
                    pool.wait_ge(SEM["latss"], at("latss", b, k + 1))
                    link(pool, "pool1", b, g.tensor_tensor(l2[:, k, :], l2[:, k, :], half_pow[:, :], ALU.pow), bare=True)
                    g.tensor_scalar(l2[:, k, :], l2[:, k, :], 1.0 / L2_EPS, None, ALU.min).then_inc(SEM["latr"], 1)

                yield from unit(0)
                yield "ln5"
                rstd("ln5", mv1, b, "pool1")
                yield "ln6"
                rstd("ln6", mv1, b, "pool1")
                pool.wait_ge(SEM["ln5_xn"], at("ln5_xn", b))
                g.tensor_tensor(x4[:, :], x4[:, :], lno[:, 1, :], ALU.add).then_inc(SEM["x4b"], 1)
                yield from unit(1)
                yield from unit(2)
                yield "lno"
                rstd("lno", mv1, b, "pool1")
                yield "ln7"
                rstd("ln7", mv1, b, "pool1")

            program(pool, first, layer0, layer1)

        @block.vector
        def _(dve):
            v = nc.vector
            dve.wait_ge(SEM["w_in"], loads[0])
            dve.wait_ge(SEM["consts"], 1)
            v.memset(x6[:], 0.0).then_inc(SEM["out_done"], 16)
            for c in range(IC):
                v.tensor_scalar(Wout[:, c, :], Wout[:, c, :], normw[:, c:c + 1], None, ALU.mult)
            dve.wait_ge(SEM["act_setup"], 1)
            v.tensor_scalar(Aneg[:, :], Aneg[:, :], -1.0, None, ALU.mult)
            for k in range(2):
                v.tensor_reduce(par[:, k:k + 1], ident[:, :].rearrange("p (a s w) -> p a s w", s=2, w=AW)[:, :, k, :], AX.XY, ALU.add)
            v.tensor_scalar(qks[:, 0:1], qks[:, 0:1], qks[:, 1:2], None, ALU.mult)
            v.tensor_reduce(wscale[:, 0:1], Wt[:, :, :], AX.XY, ALU.add, apply_absolute_value=True).then_inc(SEM["dve_setup"], 1)
            dve.wait_ge(SEM["pe_setup"], 1)
            dve.wait_ge(SEM["dve_setup"], 1)
            v.tensor_scalar(par[:, :], par[:, :], AW ** -0.5, None, ALU.mult)
            v.memset(mask_w[0:1, :], MASK0)
            v.tensor_scalar(wscale[:, 1:2], A[0][:, 0:1], 1.0 / (D * D), Q_EPS, ALU.mult, ALU.add).then_inc(SEM["dve_setup"], 1)
            dve.wait_ge(SEM["dve_setup"], 2)
            for k in range(2):
                v.tensor_scalar(bq0s[:, :, k], bqk0[:, 0, :], par[:, k:k + 1], None, ALU.mult)
            v.reciprocal(wscale[:, 2:3], wscale[:, 1:2]).then_inc(SEM["dve_setup"], 1)
            dve.wait_ge(SEM["dve_setup"], 3)
            v.tensor_scalar(Wt[:, :, :], Wt[:, :, :], wscale[:, 2:3], None, ALU.mult).then_inc(SEM["dve_setup"], 1)
            dve.wait_ge(SEM["dve_setup"], 4)
            v.tensor_scalar(Wt[:, :, :], Wt[:, :, :], ROUND, ROUND, ALU.add, ALU.subtract).then_inc(SEM["dve_setup"], 1)
            dve.wait_ge(SEM["dve_setup"], 5)
            v.tensor_scalar(Wtq[:, :, :], Wt[:, :, :], 1.0, -1.0, ALU.min, ALU.max)
            v.tensor_scalar(wscale[:, 3:4], wscale[:, 1:2], 1.0 / 127.0, None, ALU.mult).then_inc(SEM["dve_setup"], 1)
            dve.wait_ge(SEM["dve_setup"], 6)

            def norm(n, src, dst, st, mv, c, b, then):
                link(dve, c, b, v.bn_stats(st[:, :], src), bare=True)
                v.bn_aggr(mv[:, 0:2], st[:, :]).then_inc(SEM[f"{n}_var"], 1)
                yield then
                dve.wait_ge(SEM[f"{n}_rstd"], at(f"{n}_rstd", b))
                v.tensor_scalar(dst[:, :], src, mv[:, 0:1], mv[:, 3:4], ALU.subtract, ALU.mult).then_inc(SEM[f"{n}_xn"], 1)

            def scores(b, banks, S, mx, n):
                for j in range(4):
                    yield f"m{j}"
                    dve.wait_ge(SEM[f"S{n}"], at(f"S{n}", b, j + 1))
                    pj = banks[j][:, :].rearrange("p (g k) -> p g k", g=NG)
                    largest = v.tensor_reduce(mx[:, 4 * j:4 * j + 4], pj, AX.X, ALU.max, negate=True)
                    if j < 2:
                        link(dve, f"dve{n}", b, largest)
                        v.tensor_tensor(S[:, j, :, :], pj, mx[:, 4 * j:4 * j + 4].unsqueeze(2).broadcast_to([P, NG, T]),
                                        ALU.add).then_inc(SEM[f"S{n}max"], 1)
                    else:
                        largest.then_inc(SEM[f"S{n}max"], 1)

            def evac(b, banks, PT, n):
                for j in (0, 2):
                    yield f"t{j}"
                    dve.wait_ge(SEM[f"PT{n}ps"], at(f"PT{n}ps", b, j + 1))
                    v.tensor_copy(PT[:, j, :, :], banks[j][:, :].rearrange("p (g q) -> p g q", g=NG)).then_inc(SEM[f"PT{n}v"], 1)

            def headout(b, bank, rc, o, c):
                pv = bank[:, :].rearrange("p (h w) -> p h w", w=32)
                link(dve, c, b, v.reciprocal(rc[:, :].unsqueeze(2), pv[:, :, AW:AW + 1]))
                return v.tensor_tensor(o[:, :].rearrange("p (h w) -> p h w", w=AW), pv[:, :, 0:AW],
                                       rc[:, :].unsqueeze(2).broadcast_to([P, AH, AW]), ALU.mult)

            def first(b):
                yield "ln1"
                dve.wait_ge(SEM["x_in"], at("x_in", b, 16))
                yield from norm("ln1", x[:, :], xn0, st0, mv0, "ln1_st", b, "ln1a")

            def layer0(b, following):
                L = lambda ins, bare=False: link(dve, "dve0", b, ins, bare)
                yield "ip2"
                dve.wait_ge(SEM["ip"], at("ip", b, 2))
                v.tensor_tensor(dts[:, 0, :], A[3][:, 2 * T:2 * T + NH], dtb[:, :], ALU.add).then_inc(SEM["dt_pre"], 1)
                yield "ip3"
                dve.wait_ge(SEM["dt_exp"], at("dt_exp", b))
                u, s, s2, q = dts[:, 1, :], dts[:, 2, :], dts[:, 3, :], dts[:, 4, :]
                L(v.tensor_scalar(dts[:, 5, :], u, 2.0, None, ALU.add))
                L(v.reciprocal(dts[:, 5, :], dts[:, 5, :]))
                L(v.tensor_tensor(s, u, dts[:, 5, :], ALU.mult))
                L(v.tensor_tensor(s2, s, s, ALU.mult))
                L(v.tensor_scalar(q, s2, 1.0 / 15, None, ALU.mult))
                for k in (13, 11, 9, 7, 5, 3):
                    L(v.scalar_tensor_tensor(q, q, 1.0 / k, s2, ALU.add, ALU.mult))
                L(v.scalar_tensor_tensor(q, q, 1.0, s, ALU.add, ALU.mult))
                L(v.tensor_scalar(dts[:, 0, :], dts[:, 0, :], 0.0, None, ALU.max))
                L(v.scalar_tensor_tensor(dts[:, 6, :], q, 2.0, dts[:, 0, :], ALU.mult, ALU.add))
                v.tensor_tensor(dts[:, 7, :], dts[:, 6, :], Aneg[:, :], ALU.mult).then_inc(SEM["a"], 1)
                yield "cv1"
                dve.wait_ge(SEM["xpad"], at("xpad", b))
                for k in range(NCONV):
                    for c in range(IC):
                        src, wk = xpad[:, c, k:k + T], convw[:, c, k:k + 1]
                        if k == 0:
                            last = v.tensor_scalar(xc[:, c, :], src, wk, convb[:, c:c + 1], ALU.mult, ALU.add)
                        else:
                            last = v.scalar_tensor_tensor(xc[:, c, :], src, wk, xc[:, c, :], ALU.mult, ALU.add)
                    if k < NCONV - 1:
                        L(last)
                    else:
                        last.then_inc(SEM["conv"], 1)
                yield "cv2"
                dve.wait_ge(SEM["CB"], at("CB", b))
                v.tensor_tensor(cbm[:, :], A[0][:, 0:T], triu[:, :], ALU.mult).then_inc(SEM["cbm"], 1)
                dve.wait_ge(SEM["conv_th"], at("conv_th", b))
                v.scalar_tensor_tensor(xs2[:, :, :].rearrange("p c t -> p (c t)"), th0[:, :], 1.0,
                                       xc[:, :, :].rearrange("p c t -> p (c t)"), ALU.add, ALU.mult).then_inc(SEM["xs2"], 1)
                yield "cv3"
                dve.wait_ge(SEM["xsT"], at("xsT", b))
                heads = lambda t: t.rearrange("p (h w) -> p h w", w=HP)
                wide = lambda t: t.unsqueeze(2).broadcast_to([P, NH, HP])
                v.tensor_tensor(heads(xdt[:, :]), heads(A[1][:, :]), wide(dts[:, 6, :]), ALU.mult)
                v.tensor_tensor(heads(xD[:, :]), heads(A[1][:, :]), wide(Dpb[:, :]), ALU.mult).then_inc(SEM["xdt"], 1)
                for k in range(8):
                    yield f"ssd{k + 1}"
                    dve.wait_ge(SEM["E"], at("E", b, k + 1))
                    if k >= 2:
                        dve.wait_ge(SEM["Yk"], at("Yk", b, k - 1))
                    v.tensor_tensor(Mh[k % 2], Ed[k % 2], cbm[:, :].unsqueeze(1).broadcast_to([P, 4, T]),
                                    ALU.mult).then_inc(SEM["M"], 1)
                    if k == 0:
                        dve.wait_ge(SEM["tz"], at("tz", b))
                        v.scalar_tensor_tensor(gz[:, :], tz[:, :], 1.0, A[2][:, :], ALU.add, ALU.mult)
                yield "y1"
                for half in range(2):
                    dve.wait_ge(SEM["Yb"], at("Yb", b, half + 1))
                    o = slice(half * DI // 2, (half + 1) * DI // 2)
                    last = v.tensor_tensor(heads(y2[:, o]), A[1 + half][:, :].rearrange("p (h w) -> p h w", w=32)[:, :, 0:HP],
                                           heads(xD[:, o]), ALU.add)
                last.then_inc(SEM["y2"], 1)
                dve.wait_ge(SEM["y2"], at("y2", b))
                v.tensor_tensor(gz[:, :], gz[:, :], y2[:, :], ALU.mult).then_inc(SEM["yg"], 1)
                dve.wait_ge(SEM["mask0_in"], at("mask0_in", b, 16))
                v.tensor_scalar(mrow[0:1, :, :], mask0i[:, :].unsqueeze(1).broadcast_to([1, NG, T]), 1.0, -1.0,
                                ALU.mult, ALU.add).then_inc(SEM["mrow"], 1)
                yield "y3h"
                dve.wait_ge(SEM["mamba"], at("mamba", b))
                dve.wait_ge(SEM["rms"], at("rms", b))
                v.scalar_tensor_tensor(x1[:, :], A[3][:, 0:D], ss0[:, 2:3], x[:, :], ALU.mult, ALU.add).then_inc(SEM["x1"], 1)
                yield "ln2"
                dve.wait_ge(SEM["x1"], at("x1", b))
                yield from norm("ln2", x1[:, :], xn0, st0, mv0, "dve0", b, "ln2n")
                yield "qk2"
                dve.wait_ge(SEM["qk0"], at("qk0", b, 2))
                v.tensor_tensor(KT0[:, :, :], A[3][:, 0:D].rearrange("p (c k) -> p c k", c=DC),
                                bqk0[:, 1, :].unsqueeze(2).broadcast_to([P, DC, T]), ALU.add).then_inc(SEM["k0c"], 1)
                yield "qk3"
                dve.wait_ge(SEM["qk0"], at("qk0", b, 3))
                v.tensor_tensor(V0[:, :, 0:AW], A[1][:, 0:D].rearrange("p (h w) -> p h w", w=AW),
                                bv0b[:, :].rearrange("p (h w) -> p h w", w=AW), ALU.add).then_inc(SEM["v0c"], 1)
                yield from scores(b, A, S0, mx0, 0)
                yield from evac(b, A, PT0, 0)
                yield "ot"
                dve.wait_ge(SEM["PV0"], at("PV0", b, 2))
                L(headout(b, A[1], rc0, o0, "dve0"))
                v.tensor_tensor(x2[:, :], x1[:, :], o0[:, :], ALU.add).then_inc(SEM["x2"], 1)
                yield "ln3"
                dve.wait_ge(SEM["x2"], at("x2", b))
                yield from norm("ln3", x2[:, :], xn0, st0, mv0, "dve0", b, "ln3n")
                yield "r1"
                dve.wait_ge(SEM["rout"], at("rout", b))
                v.tensor_reduce(rt[:, 0, 0:1], A[2][:, 0:NE], AX.X, ALU.max, negate=True).then_inc(SEM["rmax"], 1)
                yield "g0"
                dve.wait_ge(SEM["rexp"], at("rexp", b))
                L(v.reciprocal(rt[:, 0, 2:3], rt[:, 0, 1:2]))
                L(v.tensor_scalar(rt[:, 2, :], rt[:, 1, :], rt[:, 0, 2:3], None, ALU.mult), bare=True)
                L(v.max(rt[:, 3, 0:8], rt[:, 2, :]), bare=True)
                L(v.max_index(rti[:, 0, :], rt[:, 3, 0:8], rt[:, 2, :]))
                L(v.tensor_scalar(rt[:, 4, :], iota[:, :], rti[:, 0, 0:1], None, ALU.is_equal))
                L(v.scalar_tensor_tensor(rt[:, 5, :], rt[:, 4, :], -2.0, rt[:, 2, :], ALU.mult, ALU.add), bare=True)
                L(v.max(rt[:, 6, 0:8], rt[:, 5, :]), bare=True)
                L(v.max_index(rti[:, 1, :], rt[:, 6, 0:8], rt[:, 5, :]))
                L(v.tensor_scalar(rt[:, 7, :], iota[:, :], rti[:, 1, 0:1], None, ALU.is_equal))
                L(v.tensor_tensor(rt[:, 7, :], rt[:, 7, :], rt[:, 4, :], ALU.add))
                v.scalar_tensor_tensor(cw[:, 0:NE], rt[:, 7, :], 0.5, rt[:, 2, :], ALU.mult, ALU.mult).then_inc(SEM["cw"], 1)
                dve.wait_ge(SEM["cw"], at("cw", b))
                ahead = first(following) if following is not None else iter(())
                next(ahead, None)
                for k in range(5):
                    if k == 4 and following is not None:
                        yield "ln1"
                        next(ahead)
                    yield f"u{k}h"
                    n = 4 if k < 4 else 2
                    dve.wait_ge(SEM["gth"], at("gth", b, k + 1))
                    L(v.scalar_tensor_tensor(hg[:, 0:n * FF], thf[:, 0:n * FF], 1.0, A[0][:, 0:n * FF], ALU.add, ALU.mult))
                    dve.wait_ge(SEM["gu"], at("gu", b, 2 * k + 2))
                    if k >= 1:
                        dve.wait_ge(SEM["hTps"], at("hTps", b, k))
                    for i in range(n):
                        cols = slice(i * FF, (i + 1) * FF)
                        e = 4 * k + i
                        last = v.scalar_tensor_tensor(hh[:, cols], A[1][:, cols], cw[:, e:e + 1], hg[:, cols], ALU.mult, ALU.mult)
                    last.then_inc(SEM["hh"], 1)
                if following is not None:
                    yield "ln1a"
                    yield from ahead
                yield "x3"
                dve.wait_ge(SEM["down"], at("down", b))
                if not isinstance(b, int) or b > 0:
                    dve.wait_ge(SEM["x4"], at("x4", b, 0))
                v.tensor_tensor(handoff[:, :], A[3][:, 0:D], x2[:, :], ALU.add).then_inc(SEM["x3"], 1)

            def layer1(b):
                L = lambda ins: link(dve, "dve1", b, ins)
                yield "ln4"
                dve.wait_ge(SEM["x3"], at("x3", b))
                yield from norm("ln4", handoff[:, :], xn1, st1, mv1, "dve1", b, "ln4n")
                yield "lnc"
                dve.wait_ge(SEM["ctx1_in"], at("ctx1_in", b, 16))
                dve.wait_ge(SEM["ln4_Tps"], at("ln4_Tps", b))
                yield from norm("lnc", ctx1[:, :], xn1, st1, mv1, "dve1", b, "lncn")
                yield "qk2"
                dve.wait_ge(SEM["qk1"], at("qk1", b, 2))
                v.tensor_copy(KT1[:, :, :], B[3][:, 0:D].rearrange("p (c k) -> p c k", c=DC)).then_inc(SEM["k1c"], 1)
                yield from scores(b, B, S1, mx1, 1)
                yield from evac(b, B, PT1, 1)
                yield "ot"
                dve.wait_ge(SEM["PV1"], at("PV1", b, 2))
                headout(b, B[1], rc1, o1, "dve1").then_inc(SEM["o1"], 1)
                dve.wait_ge(SEM["mask1_in"], at("mask1_in", b, 16))
                v.tensor_scalar(mrow1[:, :, 0:T], mask1i[:, :].bitcast(U8).unsqueeze(1).broadcast_to([1, 2, T]), -NEG, NEG,
                                ALU.mult, ALU.add).then_inc(SEM["mrow1"], 1)
                dst = (kn[:, 0, :], qn[:, :], kn[:, 1, :])
                heads = lambda t: t.rearrange("p (h w) -> p h w", w=XW)

                def unit(k):
                    yield f"lq{k}"
                    dve.wait_ge(SEM["latsq"], at("latsq", b, k + 1))
                    v.tensor_reduce(l2[:, k, :], heads(sq1[:, :]), AX.X, ALU.add).then_inc(SEM["latss"], 1)
                    yield f"ln{k}u"
                    dve.wait_ge(SEM["latr"], at("latr", b, k + 1))
                    v.tensor_tensor(heads(dst[k]), heads((B[3], B[0], B[1])[k][:, :]), l2[:, k, :].unsqueeze(2).broadcast_to([P, XH, XW]),
                                    ALU.mult).then_inc(SEM["latn"], 1)

                yield from unit(0)
                yield "proj"
                dve.wait_ge(SEM["proj1"], at("proj1", b))
                v.tensor_tensor(x4[:, :], B[0][:, 0:D], handoff[:, :], ALU.add).then_inc(SEM["x4"], 1)
                yield "ln5"
                dve.wait_ge(SEM["x4"], at("x4", b))
                yield from norm("ln5", x4[:, :], l5, st1, mv1, "dve1", b, "ln6")
                dve.wait_ge(SEM["ln5_xn"], at("ln5_xn", b))
                dve.wait_ge(SEM["lnc_Tps"], at("lnc_Tps", b))
                yield from norm("ln6", l5[:, :], xn1, st1, mv1, "dve1", b, "ln6n")
                for k in (1, 2):
                    yield from unit(k)
                for n, k in enumerate(BANKS_DONE):
                    yield f"lS{1 + 2 * (n // 2)}"
                    dve.wait_ge(SEM["Sl"], at("Sl", b, n + 1))
                    last = v.tensor_reduce(mxl[:, 2 * k:2 * k + 2], B[k][:, :].rearrange("p (h k) -> p h k", h=2),
                                           AX.X, ALU.max)
                L(last)
                v.tensor_scalar(mxl[:, :], mxl[:, :], -8.0, None, ALU.mult).then_inc(SEM["mxl"], 1)
                for k in range(4):
                    yield f"lP{k}"
                    dve.wait_ge(SEM["Pl"], at("Pl", b, k + 1))
                    L(v.reciprocal(den[:, 2 * k:2 * k + 2], den[:, 2 * k:2 * k + 2]))
                    half = Pl[:, k, :].rearrange("p (h n) -> p h n", h=2)
                    v.tensor_tensor(half, half, den[:, 2 * k:2 * k + 2].unsqueeze(2).broadcast_to([P, 2, 2 * T]),
                                    ALU.mult).then_inc(SEM["Pln"], 1)
                for k in (0, 2):
                    yield f"lt{k}"
                    dve.wait_ge(SEM["PTlps"], at("PTlps", b, k + 1))
                    v.tensor_copy(PTl[:, k, :], B[k][:, :]).then_inc(SEM["PTlv"], 1)
                yield "lno"
                dve.wait_ge(SEM["wo"], at("wo", b))
                link(dve, "dve1", b, v.bn_stats(st1[:, :], B[2][:, 0:D]), bare=True)
                v.bn_aggr(mv1[:, 0:2], st1[:, :]).then_inc(SEM["lno_var"], 1)
                dve.wait_ge(SEM["lno_var"], at("lno_var", b))
                v.scalar_tensor_tensor(fo[:, :], B[2][:, 0:D], mv1[:, 0:1], lno[:, 0, :], ALU.subtract, ALU.mult).then_inc(SEM["lno_xn"], 1)
                yield "x5"
                dve.wait_ge(SEM["lno_xn"], at("lno_xn", b))
                dve.wait_ge(SEM["lno_rstd"], at("lno_rstd", b))
                dve.wait_ge(SEM["x4b"], at("x4b", b))
                v.scalar_tensor_tensor(x5[:, :], fo[:, :], mv1[:, 3:4], x4[:, :], ALU.mult, ALU.add).then_inc(SEM["x5"], 1)
                yield "ln7"
                dve.wait_ge(SEM["x5"], at("x5", b))
                yield from norm("ln7", x5[:, :], xf, st1, mv1, "dve1", b, "aq")
                dve.wait_ge(SEM["ln7_xn"], at("ln7_xn", b))
                L(v.tensor_reduce(am[:, 0:1], xf[:, :], AX.X, ALU.max, apply_absolute_value=True))
                L(v.tensor_scalar(am[:, 0:1], am[:, 0:1], Q_EPS, None, ALU.add))
                L(v.reciprocal(am[:, 1:2], am[:, 0:1]))
                L(v.tensor_scalar(xf[:, :], xf[:, :], am[:, 1:2], 127.0, ALU.mult, ALU.mult))
                L(v.tensor_scalar(xf[:, :], xf[:, :], 127.0, -128.0, ALU.min, ALU.max))
                v.tensor_scalar(am[:, 2:3], am[:, 0:1], wscale[:, 3:4], None, ALU.mult)
                v.tensor_scalar(aq[:, :], xf[:, :], ROUND, ROUND, ALU.add, ALU.subtract).then_inc(SEM["aq"], 1)
                yield "x6"
                dve.wait_ge(SEM["tern"], at("tern", b))
                dve.wait_ge(SEM["out_done"], at("out_done", b, 0))
                v.scalar_tensor_tensor(x6[:, :], B[2][:, D:2 * D], am[:, 2:3], x5[:, :], ALU.mult, ALU.add).then_inc(SEM["x6"], 1)

            program(dve, first, layer0, layer1)

        @block.scalar
        def _(act):
            s = nc.scalar
            act.wait_ge(SEM["w_in"], loads[0])
            s.activation(Aneg[:, :], Aneg[:, :], ACT.Exp).then_inc(SEM["act_setup"], 1)
            act.wait_ge(SEM["dve_setup"], 6)

            def copyT(n, bank, dst, b, wb=None):
                act.wait_ge(SEM[f"{n}_Tps"], at(f"{n}_Tps", b))
                pt = bank[:, 0:DC * T].rearrange("p (c t) -> p c t", c=DC)
                if wb is None:
                    s.activation(dst[:, :, :], pt, ACT.Copy).then_inc(SEM[f"{n}_T"], 1)
                else:
                    for c in range(DC):
                        last = s.activation(dst[:, c, :], pt[:, c, :], ACT.Identity, bias=wb[:, 1, c:c + 1], scale=wb[:, 0, c:c + 1])
                    last.then_inc(SEM[f"{n}_T"], 1)

            def attention(b, banks, QT, V, S, PT, mx, n):
                yield "qk1"
                act.wait_ge(SEM[f"qk{n}"], at(f"qk{n}", b, 1))
                src = banks[2][:, 0:D].rearrange("p (c q) -> p c q", c=DC)
                dst = QT[:, :, :].rearrange("p (c k) q -> p c k q", k=2)
                if n == 0:
                    for k in range(2):
                        for c in range(DC):
                            last = s.activation(dst[:, c, k, :], src[:, c, :], ACT.Identity, bias=bq0s[:, c, k:k + 1],
                                                scale=par[:, k:k + 1])
                    last.then_inc(SEM["q0c"], 1)
                else:
                    for k in range(2):
                        last = s.activation(dst[:, :, k, :], src, ACT.Copy, scale=par[:, k:k + 1])
                    last.then_inc(SEM["q1c"], 1)
                    yield "lncn"
                    copyT("lnc", B[0], cT, b, lnx)
                    yield "qk3"
                    act.wait_ge(SEM["qk1"], at("qk1", b, 3))
                    s.activation(V[:, :, 0:AW], banks[1][:, 0:D].rearrange("p (h w) -> p h w", w=AW), ACT.Copy).then_inc(SEM["v1c"], 1)
                for j in range(4):
                    yield f"m{j}"
                    act.wait_ge(SEM[f"S{n}max"], at(f"S{n}max", b, j + 1))
                    if j < 2:
                        last = s.activation(S[:, j, :, :], S[:, j, :, :], ACT.Exp)
                    else:
                        for g in range(NG):
                            last = s.activation(S[:, j, g, :], banks[j][:, g * T:(g + 1) * T], ACT.Exp,
                                                bias=mx[:, 4 * j + g:4 * j + g + 1])
                    last.then_inc(SEM[f"P{n}"], 1)
                for j in (1, 3):
                    yield f"t{j}"
                    act.wait_ge(SEM[f"PT{n}ps"], at(f"PT{n}ps", b, j + 1))
                    s.activation(PT[:, j, :, :], banks[j][:, :].rearrange("p (g q) -> p g q", g=NG), ACT.Copy).then_inc(SEM[f"PT{n}s"], 1)
                yield "pv3"
                act.wait_ge(SEM[f"PV{n}"], at(f"PV{n}", b))
                s.activation(S[:, 0, :, :], banks[0][:, :].rearrange("p (g q) -> p g q", g=NG), ACT.Copy).then_inc(SEM[f"OT{n}"], 1)

            def first(b):
                yield "ln1n"
                copyT("ln1", A[0], xT0, b)

            def layer0(b, following):
                yield "ip1"
                act.wait_ge(SEM["ip"], at("ip", b))
                s.activation(xpad[:, :, NCONV - 1:], A[1][:, :].rearrange("p (c t) -> p c t", c=IC), ACT.Copy).then_inc(SEM["xpad"], 1)
                yield "ip2"
                act.wait_ge(SEM["dt_pre"], at("dt_pre", b))
                s.activation(dts[:, 1, :], dts[:, 0, :], ACT.Abs).then_inc(SEM["dt_abs"], 1)
                s.activation(bcT[:, :, :], A[3][:, 0:2 * T].rearrange("p (c t) -> p c t", c=2), ACT.Copy).then_inc(SEM["bcT"], 1)
                act.wait_ge(SEM["dt_abs"], at("dt_abs", b))
                s.activation(dts[:, 1, :], dts[:, 1, :], ACT.Exp, scale=-1.0).then_inc(SEM["dt_exp"], 1)
                yield "ip3h"
                act.wait_ge(SEM["ip"], at("ip", b, 3))
                s.activation(tz[:, :], A[2][:, :], ACT.Tanh, scale=0.5).then_inc(SEM["tz"], 1)
                yield "cv2"
                act.wait_ge(SEM["conv"], at("conv", b))
                s.activation(th0[:, :], xc[:, :, :].rearrange("p c t -> p (c t)"), ACT.Tanh, scale=0.5).then_inc(SEM["conv_th"], 1)
                for k in range(8):
                    yield f"ssd{k}"
                    act.wait_ge(SEM["arg"], at("arg", b, k + 1))
                    if k >= 2:
                        act.wait_ge(SEM["M"], at("M", b, k - 1))
                    s.activation(Ed[k % 2], (A[0], A[3])[k % 2][:, :].rearrange("p (h t) -> p h t", t=T),
                                 ACT.Exp).then_inc(SEM["E"], 1)
                    if k == 5:
                        act.wait_ge(SEM["Yk"], at("Yk", b, 4))
                        s.activation(Yt[:, 0:512], A[1][:, :], ACT.Copy).then_inc(SEM["Yt"], 1)
                yield "ssd8"
                act.wait_ge(SEM["Yk"], at("Yk", b, 8))
                s.activation(Yt[:, 512:1024], A[2][:, :], ACT.Copy).then_inc(SEM["Yt"], 1)
                yield "y1"
                act.wait_ge(SEM["y2"], at("y2", b))
                s.activation(sq0[:, :], y2[:, :], ACT.Square, scale=2.0 * DI ** -0.5, accum_out=ss0[:, 0:1]).then_inc(SEM["ss"], 1)
                yield "y2"
                act.wait_ge(SEM["yTps"], at("yTps", b))
                s.activation(yT[:, :, :], A[0][:, :].rearrange("p (c t) -> p c t", c=IC), ACT.Copy).then_inc(SEM["yT"], 1)
                yield "ln2"
                act.wait_ge(SEM["ctxTps"], at("ctxTps", b))
                s.activation(ctxT[:, :, :], A[1][:, 0:DC * T].rearrange("p (c t) -> p c t", c=DC), ACT.Copy).then_inc(SEM["ctxT"], 1)
                yield "ln2n"
                copyT("ln2", A[0], xT0, b)
                yield from attention(b, A, QT0, V0, S0, PT0, mx0, 0)
                yield "ln3n"
                copyT("ln3", A[1], xT0, b)
                yield "r1"
                act.wait_ge(SEM["rmax"], at("rmax", b))
                s.activation(rt[:, 1, :], A[2][:, 0:NE], ACT.Exp, bias=rt[:, 0, 0:1], accum_out=rt[:, 0, 1:2]).then_inc(SEM["rexp"], 1)
                for k in range(5):
                    n = 4 if k < 4 else 2
                    yield f"g{k}h"
                    act.wait_ge(SEM["gu"], at("gu", b, 2 * k + 1))
                    if k >= 1:
                        act.wait_ge(SEM["hh"], at("hh", b, k))
                    s.activation(thf[:, 0:n * FF], A[0][:, 0:n * FF], ACT.Tanh, scale=0.5).then_inc(SEM["gth"], 1)
                    if k == 4 and following is not None:
                        yield from first(following)
                    yield f"e{k + 1}"
                    act.wait_ge(SEM["hTps"], at("hTps", b, k + 1))
                    s.activation(hT[:, 0:n * FF], A[2][:, 0:n * FF], ACT.Copy).then_inc(SEM["hT"], 1)

            def layer1(b):
                yield "ln4n"
                copyT("ln4", B[0], xT1, b)

                def square(k):
                    yield f"lq{k}"
                    act.wait_ge(SEM["lat"], at("lat", b, (1, 3, 4)[k]))
                    if k:
                        act.wait_ge(SEM["latss"], at("latss", b, k))
                    s.activation(sq1[:, :], (B[3], B[0], B[1])[k][:, :], ACT.Square).then_inc(SEM["latsq"], 1)

                yield from attention(b, B, QT1, V1, S1, PT1, mx1, 1)
                yield from square(0)
                yield "la3h"
                act.wait_ge(SEM["lat"], at("lat", b, 2))
                s.activation(Vl[:, 0, :], B[2][:, :], ACT.Copy).then_inc(SEM["Vl"], 1)
                yield "oT"
                act.wait_ge(SEM["oT1ps"], at("oT1ps", b))
                s.activation(oT1[:, :, :], B[1][:, 0:DC * T].rearrange("p (c t) -> p c t", c=DC), ACT.Copy).then_inc(SEM["oT1"], 1)
                yield "ln6n"
                copyT("ln6", B[1], lT, b, lnl)
                yield from square(1)
                yield from square(2)
                yield "la4h"
                act.wait_ge(SEM["lat"], at("lat", b, 5))
                s.activation(Vl[:, 1, :], B[2][:, :], ACT.Copy).then_inc(SEM["Vl"], 1)
                for k, (bank, dst) in enumerate(((B[3], klT[:, :, 0:T]), (B[0], qlT[:, :, :]), (B[1], klT[:, :, T:2 * T]))):
                    yield f"lT{k}"
                    act.wait_ge(SEM["qlTps"], at("qlTps", b, k + 1))
                    src = bank[:, :].rearrange("p (m t) -> p m t", m=4)
                    if k == 1:
                        s.activation(dst, src, ACT.Copy, scale=qks[:, 0:1]).then_inc(SEM["qlT"], 1)
                    else:
                        s.activation(dst, src, ACT.Copy).then_inc(SEM["qlT"], 1)
                yield "lP0"
                act.wait_ge(SEM["mxl"], at("mxl", b))
                for k in range(4):
                    if k:
                        yield f"lP{k}"
                    for i in range(2):
                        n = 2 * k + i
                        last = s.activation(Pl[:, k, i * 2 * T:(i + 1) * 2 * T], B[k][:, i * 2 * T:(i + 1) * 2 * T], ACT.Exp,
                                            bias=mxl[:, n:n + 1], scale=8.0, accum_out=den[:, n:n + 1])
                    last.then_inc(SEM["Pl"], 1)
                for k in (1, 3):
                    yield f"lt{k}"
                    act.wait_ge(SEM["PTlps"], at("PTlps", b, k + 1))
                    s.activation(PTl[:, k, :], B[k][:, :], ACT.Copy).then_inc(SEM["PTls"], 1)
                yield "lo"
                act.wait_ge(SEM["PVl"], at("PVl", b))
                s.activation(olT[:, :, :], B[0][:, :].rearrange("p (c t) -> p c t", c=IC), ACT.Copy).then_inc(SEM["olT"], 1)
                yield "aT"
                act.wait_ge(SEM["aqTps"], at("aqTps", b))
                s.activation(aqT[:, :, :], B[3][:, 0:T].bitcast(BF16).rearrange("p (c t) -> p c t", c=DC), ACT.Copy).then_inc(SEM["aqT"], 1)

            program(act, first, layer0, layer1)

        @block.tensor
        def _(pe):
            mm = nc.tensor.matmul
            pe.wait_ge(SEM["dve_setup"], 1)
            pe.wait_ge(SEM["consts"], 1)
            mm(A[0][:, 0:1], ones[:, :], wscale[:, 0:1], start=True, stop=True).then_inc(SEM["pe_setup"], 1)
            pe.wait_ge(SEM["dve_setup"], 6)

            def dot(out, lhs, rhs, n=DC):
                for c in range(n):
                    last = mm(out, lhs(c), rhs(c), start=c == 0, stop=c == n - 1)
                return last

            def dot_halves(step, out, lhs, rhs, n=DC):
                for c in range(n):
                    if c == n // 2:
                        yield f"{step}h"
                    last = mm(out, lhs(c), rhs(c), start=c == 0, stop=c == n - 1)
                return last

            def transposes(out, src, n):
                for c in range(n):
                    last = nc.tensor.transpose(out[:, c * P:(c + 1) * P], src[:, c * P:(c + 1) * P], ident[:, :])
                return last

            def lnT(n, src, bank, b):
                pe.wait_ge(SEM[f"{n}_xn"], at(f"{n}_xn", b))
                transposes(bank, src, DC).then_inc(SEM[f"{n}_Tps"], 1)

            def attention(b, banks, QT, KT, V, S, PT, n, causal_, meanwhile=()):
                yield "S"
                pe.wait_ge(SEM[f"q{n}c"], at(f"q{n}c", b))
                pe.wait_ge(SEM[f"k{n}c"], at(f"k{n}c", b))
                pe.wait_ge(SEM[f"v{n}c"], at(f"v{n}c", b))
                if causal_:
                    pe.wait_ge(SEM["lnc_T"], at("lnc_T", b))
                else:
                    pe.wait_ge(SEM["mrow"], at("mrow", b))
                for j in range(4):
                    if causal_:
                        mm(banks[j][:, :], identb[:, :], causal[:, :, :], start=True, stop=False)
                    else:
                        mm(banks[j][:, :], mask_w[:, :], mrow[:, :, :], start=True, stop=False)
                for g in range(NG):
                    if g:
                        yield f"S{g}"
                    for j in range(4):
                        r = slice(32 * j, 32 * j + 32)
                        last = mm(banks[j][:, g * T:(g + 1) * T], QT[r, g, :], KT[r, g // 2, :], start=False, stop=g == NG - 1)
                        if g == NG - 1:
                            last.then_inc(SEM[f"S{n}"], 1)
                for j in range(4):
                    yield f"t{j}"
                    pe.wait_ge(SEM[f"P{n}"], at(f"P{n}", b, j + 1))
                    for g in range(NG):
                        last = nc.tensor.transpose(banks[j][:, g * T:(g + 1) * T], S[:, j, g, :], ident[:, :])
                    last.then_inc(SEM[f"PT{n}ps"], 1)
                yield "pv"
                for j in range(4):
                    if j:
                        yield f"pv{j}"
                    done = f"PT{n}{'vs'[j % 2]}"
                    pe.wait_ge(SEM[done], at(done, b, j // 2 + 1))
                    for g in range(NG):
                        h = 8 * (g // 2) + 2 * j + g % 2
                        last = mm(banks[0][32 * (h % 4):32 * (h % 4) + AW + 1, h // 4 * T:(h // 4 + 1) * T], V[:, h, :], PT[:, j, g, :], start=True, stop=True)
                last.then_inc(SEM[f"PV{n}"], 1)
                yield from meanwhile
                yield "ot"
                pe.wait_ge(SEM[f"OT{n}"], at(f"OT{n}", b))
                transposes(banks[1], S[:, 0, :, :].rearrange("p g q -> p (g q)"), NG).then_inc(SEM[f"PV{n}"], 1)

            def arg(b, k):
                pe.wait_ge(SEM["R"], at("R", b, k // 2 + 1))
                if k >= 2:
                    pe.wait_ge(SEM["E"], at("E", b, k - 1))
                mm((A[0], A[3])[k % 2][:, :], strict[:, :], R[:, 4 * k:4 * k + 4, :], start=True, stop=True).then_inc(SEM["arg"], 1)

            def heads(bank, W, src):
                for k in range(DC):
                    last = dot(bank[:, k * T:(k + 1) * T], lambda c: W[:, c, k * P:(k + 1) * P], lambda c: src[:, c, :])
                return last

            def gate_up(b, k):
                cols = slice(4 * k * FF, min(4 * (k + 1), NBLK) * FF)
                n = cols.stop - cols.start
                if k >= 1:
                    pe.wait_ge(SEM["hh"], at("hh", b, k))
                last = yield from dot_halves(f"g{k}", A[0][:, 0:n], lambda c: xT0[:, c, :], lambda c: Wg[:, c, cols])
                last.then_inc(SEM["gu"], 1)
                yield f"u{k}"
                last = yield from dot_halves(f"u{k}", A[1][:, 0:n], lambda c: xT0[:, c, :], lambda c: Wu[:, c, cols])
                last.then_inc(SEM["gu"], 1)

            def first(b):
                yield "ln1n"
                lnT("ln1", xn0, A[0], b)

            def layer0(b, following):
                tok = lambda c: xT0[:, c, :]
                yield "ip1"
                pe.wait_ge(SEM["ln1_T"], at("ln1_T", b))
                for k in range(IC):
                    if k == 2:
                        yield "ip1b"
                    last = dot(A[1][:, k * T:(k + 1) * T], lambda c: Win[:, c, k * P:(k + 1) * P], tok)
                last.then_inc(SEM["ip"], 1)
                yield "ip2"
                if not isinstance(b, int) or b > 0:
                    pe.wait_ge(SEM["x3"], at("x3", b, 0))
                dot(A[3][:, 2 * T:2 * T + NH], tok, lambda c: Win[:, c, 2 * DI + 2 * NS:])
                for k in range(2):
                    last = dot(A[3][:, k * T:(k + 1) * T], lambda c: Win[:, c, 2 * DI + k * NS:2 * DI + (k + 1) * NS], tok)
                last.then_inc(SEM["ip"], 1)
                yield "ip3"
                last = yield from dot_halves("ip3", A[2][:, :], tok, lambda c: Win[:, c, DI:2 * DI])
                last.then_inc(SEM["ip"], 1)
                yield "cv1"
                pe.wait_ge(SEM["bcT"], at("bcT", b))
                mm(A[0][:, 0:T], bcT[:, 0, :], bcT[:, 1, :], start=True, stop=True).then_inc(SEM["CB"], 1)
                yield "cv3"
                pe.wait_ge(SEM["xs2"], at("xs2", b))
                transposes(A[1], xs2[:, :, :].rearrange("p c t -> p (c t)"), IC).then_inc(SEM["xsT"], 1)
                yield "ssd0"
                pe.wait_ge(SEM["cbm"], at("cbm", b))
                arg(b, 0)
                arg(b, 1)
                pe.wait_ge(SEM["xdt"], at("xdt", b))
                for k in range(8):
                    yield f"ssd{k + 1}"
                    if k < 6:
                        arg(b, k + 2)
                    pe.wait_ge(SEM["M"], at("M", b, k + 1))
                    for i in range(4):
                        h = 4 * k + i
                        last = mm(A[1 + k // 4][32 * i:32 * i + HP, (k % 4) * T:(k % 4 + 1) * T], xdt[:, h * HP:(h + 1) * HP], Mh[k % 2][:, i, :],
                                  start=True, stop=True)
                    last.then_inc(SEM["Yk"], 1)
                    if k in (5, 7):
                        if k == 7:
                            yield "y0"
                        half = k // 7
                        pe.wait_ge(SEM["Yt"], at("Yt", b, half + 1))
                        transposes(A[1 + half], Yt[:, half * 512:(half + 1) * 512], 4).then_inc(SEM["Yb"], 1)
                yield "y2"
                pe.wait_ge(SEM["yg"], at("yg", b))
                transposes(A[0], gz, IC).then_inc(SEM["yTps"], 1)
                yield "y3"
                pe.wait_ge(SEM["yT"], at("yT", b))
                last = yield from dot_halves("y3", A[3][:, 0:D], lambda c: yT[:, c, :], lambda c: Wout[:, c, :], IC)
                last.then_inc(SEM["mamba"], 1)
                yield "ln2"
                pe.wait_ge(SEM["ctx0_in"], at("ctx0_in", b, 16))
                transposes(A[1], ctx0, DC).then_inc(SEM["ctxTps"], 1)
                yield "ln2n"
                lnT("ln2", xn0, A[0], b)
                yield "qk1"
                pe.wait_ge(SEM["ln2_T"], at("ln2_T", b))
                heads(A[2], Wq0, xT0).then_inc(SEM["qk0"], 1)
                yield "qk2"
                pe.wait_ge(SEM["ctxT"], at("ctxT", b))
                heads(A[3], Wk0, ctxT).then_inc(SEM["qk0"], 1)
                yield "qk3"
                dot(A[1][:, 0:D], lambda c: ctxT[:, c, :], lambda c: Wv0[:, c, :]).then_inc(SEM["qk0"], 1)
                yield from attention(b, A, QT0, KT0, V0, S0, PT0, 0, False)
                yield "ln3n"
                lnT("ln3", xn0, A[1], b)
                yield "r1"
                pe.wait_ge(SEM["ln3_T"], at("ln3_T", b))
                dot(A[2][:, 0:NE], tok, lambda c: Wr[:, c, :]).then_inc(SEM["rout"], 1)
                yield "g0"
                yield from gate_up(b, 0)
                pe.wait_ge(SEM["rexp"], at("rexp", b))
                for k in range(5):
                    n = 4 if k < 4 else 2
                    if k == 4 and following is not None:
                        yield "ln1n"
                        pe.wait_ge(SEM["hh"], at("hh", b, 5))
                        yield from first(following)
                    yield f"e{k + 1}"
                    pe.wait_ge(SEM["hh"], at("hh", b, k + 1))
                    if k >= 1:
                        pe.wait_ge(SEM["hT"], at("hT", b, k))
                    transposes(A[2], hh, n).then_inc(SEM["hTps"], 1)
                    if k < 4:
                        yield f"g{k + 1}"
                        yield from gate_up(b, k + 1)
                    yield f"d{k}"
                    pe.wait_ge(SEM["hT"], at("hT", b, k + 1))
                    for i in range(n):
                        e = 4 * k + i
                        if i == 2:
                            yield f"d{k}h"
                        last = mm(A[3][:, 0:D], hT[:, i * FF:(i + 1) * FF], Wd[:, e, :], start=e == 0, stop=e == NBLK - 1)
                last.then_inc(SEM["down"], 1)

            def layer1(b):
                yield "ln4n"
                lnT("ln4", xn1, B[0], b)
                pe.wait_ge(SEM["ln4_T"], at("ln4_T", b))
                for step, bank, W in (("qk1", B[2], Wq1), ("qk2", B[3], Wk1)):
                    if bank is B[3]:
                        yield "lncn"
                        lnT("lnc", xn1, B[0], b)
                    yield step
                    heads(bank, W, xT1).then_inc(SEM["qk1"], 1)
                yield "qk3"
                dot(B[1][:, 0:D], lambda c: xT1[:, c, :], lambda c: Wv1[:, c, :]).then_inc(SEM["qk1"], 1)
                KV = XH * XW
                lat = lambda c: lT[:, c, :]
                con = lambda c: cT[:, c, :]

                def context_keys():
                    yield "la1"
                    pe.wait_ge(SEM["lnc_T"], at("lnc_T", b))
                    last = yield from dot_halves("la1", B[3][:, :], con, lambda c: Wkvl[:, c, 0:KV])
                    last.then_inc(SEM["lat"], 1)

                yield from attention(b, B, QT1, KT1, V1, S1, PT1, 1, True, context_keys())
                yield "la3"
                last = yield from dot_halves("la3", B[2][:, :], con, lambda c: Wkvl[:, c, KV:2 * KV])
                last.then_inc(SEM["lat"], 1)
                yield "oT"
                pe.wait_ge(SEM["o1"], at("o1", b))
                transposes(B[1], o1, DC).then_inc(SEM["oT1ps"], 1)
                yield "proj"
                pe.wait_ge(SEM["oT1"], at("oT1", b))
                dot(B[0][:, 0:D], lambda c: oT1[:, c, :], lambda c: Wp1[:, c, :]).then_inc(SEM["proj1"], 1)
                yield "ln6n"
                lnT("ln6", xn1, B[1], b)
                yield "la0"
                pe.wait_ge(SEM["ln6_T"], at("ln6_T", b))
                last = yield from dot_halves("la0", B[0][:, :], lat, lambda c: Wql[:, c, :])
                last.then_inc(SEM["lat"], 1)
                yield "la2"
                last = yield from dot_halves("la2", B[1][:, :], lat, lambda c: Wkvl[:, c, 0:KV])
                last.then_inc(SEM["lat"], 1)
                yield "la4"
                pe.wait_ge(SEM["Vl"], at("Vl", b))
                last = yield from dot_halves("la4", B[2][:, :], lat, lambda c: Wkvl[:, c, KV:2 * KV])
                last.then_inc(SEM["lat"], 1)
                for k, (bank, src) in enumerate(((B[3], kn[:, 0, :]), (B[0], qn), (B[1], kn[:, 1, :]))):
                    yield f"lT{k}"
                    pe.wait_ge(SEM["latn"], at("latn", b, k + 1))
                    transposes(bank, src, 4).then_inc(SEM["qlTps"], 1)
                yield "lS"
                pe.wait_ge(SEM["qlT"], at("qlT", b, 3))
                pe.wait_ge(SEM["Vl"], at("Vl", b, 2))
                pe.wait_ge(SEM["mrow1"], at("mrow1", b))
                for k in range(4):
                    mm(B[k][:, :], onesb[:, :], mrow1[:, :, :], start=True, stop=False)
                for m in range(4):
                    if m:
                        yield f"lS{m}"
                    for r in range(2):
                        rows = slice(64 * r, 64 * r + 64)
                        k, i = 2 * r + m // 2, m % 2
                        last = mm(B[k][:, i * 2 * T:(i + 1) * 2 * T], qlT[rows, m, :], klT[rows, m, :], start=False, stop=i == 1)
                        if i == 1:
                            last.then_inc(SEM["Sl"], 1)
                for k in range(4):
                    yield f"lt{k}"
                    pe.wait_ge(SEM["Pln"], at("Pln", b, k + 1))
                    transposes(B[k], Pl[:, k, :], 4).then_inc(SEM["PTlps"], 1)
                for k in range(4):
                    yield f"lpv{k}"
                    done = f"PTl{'vs'[k % 2]}"
                    pe.wait_ge(SEM[done], at(done, b, k // 2 + 1))
                    for i in range(2):
                        h = head_at(k, i)
                        for c in range(2):
                            last = mm(B[0][64 * (h % 2):64 * (h % 2) + 64, (h // 2) * T:(h // 2 + 1) * T], Vl[:, c, h * XW:(h + 1) * XW],
                                      PTl[:, k, (2 * i + c) * T:(2 * i + c + 1) * T], start=c == 0, stop=c == 1)
                last.then_inc(SEM["PVl"], 1)
                yield "wo"
                pe.wait_ge(SEM["olT"], at("olT", b))
                last = yield from dot_halves("wo", B[2][:, 0:D], lambda c: olT[:, c, :], lambda c: Wol[:, c, :], IC)
                last.then_inc(SEM["wo"], 1)
                yield "aT"
                pe.wait_ge(SEM["aq"], at("aq", b))
                flipped = B[3][:, 0:T].bitcast(BF16)
                for c in range(DC):
                    last = nc.tensor.transpose(flipped[:, c * T:(c + 1) * T], aq[:, c * P:(c + 1) * P], identb[:, :])
                last.then_inc(SEM["aqTps"], 1)
                yield "tern"
                pe.wait_ge(SEM["aqT"], at("aqT", b))
                dot(B[2][:, D:2 * D], lambda c: aqT[:, c, :], lambda c: Wtq[:, c, :]).then_inc(SEM["tern"], 1)

            program(pe, first, layer0, layer1)


_INS = ['x', 'ctx_1024', 'mask_BxS2_ik0', 'mask_BxS2_bk0', 'L0_attn_in_proj_w', 'L0_attn_conv_w', 'L0_attn_conv_b',
        'L0_attn_A_log', 'L0_attn_Dp', 'L0_attn_dt_bias', 'L0_attn_norm_w', 'L0_attn_out_proj_w', 'L0_xattn_Wq',
        'L0_xattn_bq', 'L0_xattn_Wk', 'L0_xattn_bk', 'L0_xattn_Wv', 'L0_xattn_bv', 'L0_ffn_Wr', 'L0_ffn_Wg', 'L0_ffn_Wu',
        'L0_ffn_Wd', 'L0_ffn_Sg', 'L0_ffn_Su', 'L0_ffn_Sd', 'L1_attn_w_qkv', 'L1_attn_w_proj', 'L1_xattn_ln_x_w',
        'L1_xattn_ln_x_b', 'L1_xattn_ln_l_w', 'L1_xattn_ln_l_b', 'L1_xattn_Wq', 'L1_xattn_Wkv', 'L1_xattn_q_scale',
        'L1_xattn_k_scale', 'L1_xattn_Wo', 'L1_xattn_ln_o_w', 'L1_xattn_ln_o_b', 'L1_ffn_weight']
_TRANSPOSED = ('L0_attn_in_proj_w', 'L0_attn_out_proj_w', 'L0_xattn_Wq', 'L0_xattn_Wk', 'L0_xattn_Wv', 'L1_ffn_weight')


def kernel(**inputs):
    import numpy as _np
    import concourse.bacc as _bacc
    from concourse import mybir as _mybir
    from concourse.bass_utils import run_bass_kernel_spmd as _run

    nc = _bacc.Bacc("TRN2", target_bir_lowering=False, num_devices=1)
    arrays, args = {}, []
    for name in _INS:
        a = _np.asarray(inputs[name])
        if name in _TRANSPOSED:
            a = a.T
        a = _np.ascontiguousarray(a)
        if a.dtype == _np.bool_:
            a = a.view(_np.int32)
        arrays[f"in_{name}_dram"] = a
        args.append(nc.dram_tensor(f"in_{name}_dram", a.shape, _mybir.dt.from_np(a.dtype), kind="ExternalInput").ap())
    args.append(nc.dram_tensor("out_0_dram", (NB, T, D), F32, kind="ExternalOutput").ap())
    two_layers(nc, *args)
    r = _run(nc, [arrays], core_ids=[0])
    return r.results[0]["out_0_dram"]
```
